# Optimizing a Trainium2 kernel written in Bass

```python
import numpy as np
import jax
import jax.numpy as jnp

def _softmax(x, axis=-1):
    return jax.nn.softmax(x, axis=axis)

def _gelu(x):
    return jax.nn.gelu(x, approximate=True)

def _silu(x):
    return jax.nn.silu(x)

def _sigmoid(x):
    return jax.nn.sigmoid(x)

def _layernorm(x, axis=-1, eps=1e-05):
    m = jnp.mean(x, axis=axis, keepdims=True)
    v = jnp.var(x, axis=axis, keepdims=True)
    return (x - m) / jnp.sqrt(v + eps)

def _scatter_add(tgt, idx, src, axis=0):
    return tgt.at[idx].add(src)

def _segment_sum(src, seg, n):
    return jax.ops.segment_sum(src, seg, n)
kernel_name = 'mk_pixart_seq_d4_seqx_r4_154050'

def setup_inputs(seed: int=0):
    np.random.seed(seed)
    _w = jnp.asarray

    def _rec_inputs():
        import jax
        import jax.numpy as jnp
        _rk = jax.random.key(seed)
        x = -0.0002928 + 1 * jax.random.normal(jax.random.fold_in(_rk, 1), (4, 1024, 256), jnp.float32)
        _lenS = 1024 - jax.random.randint(jax.random.fold_in(_rk, 7), (4,), 0, max(1, 1024 // 4) + 1, jnp.int32)
        _lenS2 = 77 - jax.random.randint(jax.random.fold_in(_rk, 8), (4,), 0, max(1, 77 // 4) + 1, jnp.int32)
        cond_1024 = 0.000887014 + 1.03683 * jax.random.normal(jax.random.fold_in(_rk, 11), (4, 256), jnp.float32)
        _ctx_1024P = jax.random.normal(jax.random.fold_in(_rk, 12), (4, 16, 256), jnp.float32)
        _ctx_1024c = jax.random.dirichlet(jax.random.fold_in(_rk, 512), 0.3 * jnp.ones((16,), jnp.float32), (4, 77))
        _ctx_1024t = jnp.einsum('bsk,bkd->bsd', _ctx_1024c, _ctx_1024P)
        _ctx_1024t = _ctx_1024t * jax.lax.rsqrt(jnp.mean(jnp.square(_ctx_1024t)) + 1e-12) * 0.953939
        ctx_1024 = -0.00606593 + 0.997213 * (_ctx_1024t + 0.3 * jax.random.normal(jax.random.fold_in(_rk, 612), (4, 77, 256), jnp.float32))
        _validS = jnp.arange(1024)[None, :] < _lenS[:, None]
        _validS2 = jnp.arange(77)[None, :] < _lenS2[:, None]
        _causal = jnp.tril(jnp.ones((1024, 1024), dtype=bool))
        mask_BxS2_bf1 = jnp.ones((4, 77), dtype=bool)
        mask_SxS_bk0 = jnp.logical_not(jnp.broadcast_to(_validS[0:1, :], (1024, 1024)))
        return (x, cond_1024, ctx_1024, mask_BxS2_bf1, mask_SxS_bk0)
    x, cond_1024, ctx_1024, mask_BxS2_bf1, mask_SxS_bk0 = _rec_inputs()

    def _L0_xcond_setup():
        import jax, jax.numpy as jnp
        import numpy as np
        B, N, D, H, LC = (2, 256, 256, 16, 77)
        HD = D // H
        BLOCK = 16
        ROPE_BASE = 10000.0
        EPS = 1e-05

        def _block_diff_mask(n, block_size):
            idx = np.arange(2 * n)
            q = idx[:, None]
            kv = idx[None, :]
            fq = q >= n
            fkv = kv >= n
            bq = np.where(fq, (q - n) // block_size, q // block_size)
            bkv = np.where(fkv, (kv - n) // block_size, kv // block_size)
            block_diagonal = (bq == bkv) & (fq == fkv)
            offset_block_causal = (bq > bkv) & fkv & ~fq
            block_causal = (bq >= bkv) & fq & fkv
            return jnp.asarray(block_diagonal | offset_block_causal | block_causal)

        def _rope_tables(n):
            inv_freq = 1.0 / ROPE_BASE ** (np.arange(0, HD, 2, dtype=np.float32) / HD)
            freqs = np.outer(np.arange(n, dtype=np.float32), inv_freq)
            emb = np.concatenate([freqs, freqs], axis=-1)
            cos = jnp.asarray(np.cos(emb), jnp.float32)[None, :, None, :]
            sin = jnp.asarray(np.sin(emb), jnp.float32)[None, :, None, :]
            return (cos, sin)

        def _ln(x, w):
            xf = x.astype(jnp.float32)
            mu = jnp.mean(xf, axis=-1, keepdims=True)
            var = jnp.mean(jnp.square(xf - mu), axis=-1, keepdims=True)
            y = (xf - mu) * jax.lax.rsqrt(var + EPS)
            return y * w[None, None, :]

        def _apply_rope(t, cos, sin):
            t1, t2 = jnp.split(t, 2, axis=-1)
            rot = jnp.concatenate([-t2, t1], axis=-1)
            return t * cos + rot * sin

        def _attn(q, k, v, mask):
            scale = 1.0 / np.sqrt(HD)
            s = jnp.einsum('bqhd,bkhd->bhqk', q, k) * scale
            s = jnp.where(mask, s, jnp.finfo(s.dtype).min)
            a = jax.nn.softmax(s, axis=-1)
            return jnp.einsum('bhqk,bkhd->bqhd', a, v)
        key = jax.random.key(seed)
        ks = jax.random.split(key, 16)
        w = lambda k, shp: jax.random.normal(k, shp, jnp.float32) * 0.02
        inp = {'x': jax.random.normal(ks[0], (B, 2 * N, D), jnp.float32), 'cond_global': jax.random.normal(ks[1], (B, D), jnp.float32), 'cond_tokens': jax.random.normal(ks[2], (B, LC, D), jnp.float32), 'adaLN_W': w(ks[3], (D, 9 * D)), 'adaLN_b': w(ks[4], (9 * D,)), 'norm1_w': jnp.ones((D,), jnp.float32), 'qkv_W': w(ks[5], (D, 3 * D)), 'attn_out_W': w(ks[6], (D, D)), 'normc_w': jnp.ones((D,), jnp.float32), 'cq_W': w(ks[7], (D, D)), 'ck_W': w(ks[8], (D, D)), 'cv_W': w(ks[9], (D, D)), 'co_W': w(ks[10], (D, D)), 'norm2_w': jnp.ones((D,), jnp.float32), 'mlp_W1': w(ks[11], (D, 4 * D)), 'mlp_b1': w(ks[12], (4 * D,)), 'mlp_W2': w(ks[13], (4 * D, D)), 'mlp_b2': w(ks[14], (D,)), 'cond_kv_mask': jnp.ones((B, LC), bool), 'attn_mask': _block_diff_mask(N, BLOCK)}
        return inp
    _L0_xcond_all = _L0_xcond_setup()
    _L0_xcond_in = {k: v for k, v in _L0_xcond_all.items() if k in ('adaLN_W', 'adaLN_b', 'norm1_w', 'qkv_W', 'attn_out_W', 'normc_w', 'cq_W', 'ck_W', 'cv_W', 'co_W', 'norm2_w', 'mlp_W1', 'mlp_b1', 'mlp_W2', 'mlp_b2')}
    del _L0_xcond_all

    def _L1_xcond_setup():
        import jax, jax.numpy as jnp
        import numpy as np
        H = 256
        RH = 2 * H
        E = 3
        B, T, P = (8, 512, 64)
        LN_EPS = 1e-05

        def _layer_norm(x, gamma, beta):
            mu = jnp.mean(x, axis=-1, keepdims=True)
            var = jnp.mean(jnp.square(x - mu), axis=-1, keepdims=True)
            return (x - mu) * jax.lax.rsqrt(var + LN_EPS) * gamma + beta
        key = jax.random.key(seed)
        ks = jax.random.split(key, 24)
        s = lambda fan_in: 1.0 / np.sqrt(fan_in)
        inp = {'mix_hidden_states': jax.random.normal(ks[0], (B, T, H), jnp.float32), 'global_anchor': jax.random.normal(ks[1], (B, H), jnp.float32), 'prototype_bank': jax.random.normal(ks[2], (B, P, H), jnp.float32), 'ln_gamma': jnp.ones((H,), jnp.float32), 'ln_beta': jnp.zeros((H,), jnp.float32), 'Wq': jax.random.normal(ks[3], (H, H), jnp.float32) * s(H), 'Wk': jax.random.normal(ks[4], (H, H), jnp.float32) * s(H), 'Wv': jax.random.normal(ks[5], (H, H), jnp.float32) * s(H), 'router_W': jax.random.normal(ks[6], (3 * H, E), jnp.float32) * s(3 * H), 'router_b': jnp.zeros((E,), jnp.float32), 'e_w1': jax.random.normal(ks[7], (E, 3 * H, RH), jnp.float32) * s(3 * H), 'e_b1': jnp.zeros((E, RH), jnp.float32), 'e_w2': jax.random.normal(ks[8], (E, RH, H), jnp.float32) * s(RH), 'e_b2': jnp.zeros((E, H), jnp.float32), 'gate_w1': jax.random.normal(ks[9], (3 * H, H), jnp.float32) * s(3 * H), 'gate_b1': jnp.zeros((H,), jnp.float32), 'gate_w2': jax.random.normal(ks[10], (H, H), jnp.float32) * s(H), 'gate_b2': jnp.zeros((H,), jnp.float32), 'out_w': jax.random.normal(ks[11], (H, H), jnp.float32) * s(H), 'out_b': jnp.zeros((H,), jnp.float32)}
        return inp
    _L1_xcond_all = _L1_xcond_setup()
    _L1_xcond_in = {k: v for k, v in _L1_xcond_all.items() if k in ('ln_gamma', 'ln_beta', 'Wq', 'Wk', 'Wv', 'router_W', 'router_b', 'e_w1', 'e_b1', 'e_w2', 'e_b2', 'gate_w1', 'gate_b1', 'gate_w2', 'gate_b2', 'out_w', 'out_b')}
    del _L1_xcond_all

    def _L2_xcond_setup():
        import jax, jax.numpy as jnp
        import numpy as np
        LN_EPS = 1e-06

        def _ln(x):
            mu = jnp.mean(x, axis=-1, keepdims=True)
            var = jnp.var(x, axis=-1, keepdims=True)
            return (x - mu) * jax.lax.rsqrt(var + LN_EPS)
        key = jax.random.key(seed)
        H, NH = (256, 16)
        B, N, S = (4, 256, 77)
        MLP = int(H * 4.0)
        ks = jax.random.split(key, 20)
        s = 1.0 / np.sqrt(H)
        return {'x': jax.random.normal(ks[0], (B, N, H), jnp.float32), 'c': jax.random.normal(ks[1], (B, H), jnp.float32), 'context': jax.random.normal(ks[2], (B, S, H), jnp.float32), 'W_mod': jax.random.normal(ks[3], (H, 6 * H), jnp.float32) * s, 'b_mod': jnp.zeros((6 * H,), jnp.float32), 'W_qkv': jax.random.normal(ks[4], (H, 3 * H), jnp.float32) * s, 'b_qkv': jnp.zeros((3 * H,), jnp.float32), 'W_proj': jax.random.normal(ks[5], (H, H), jnp.float32) * s, 'b_proj': jnp.zeros((H,), jnp.float32), 'W_qc': jax.random.normal(ks[6], (H, H), jnp.float32) * s, 'b_qc': jnp.zeros((H,), jnp.float32), 'W_kvc': jax.random.normal(ks[7], (H, 2 * H), jnp.float32) * s, 'b_kvc': jnp.zeros((2 * H,), jnp.float32), 'W_cproj': jax.random.normal(ks[8], (H, H), jnp.float32) * s, 'b_cproj': jnp.zeros((H,), jnp.float32), 'W_mlp1': jax.random.normal(ks[9], (H, MLP), jnp.float32) * s, 'b_mlp1': jnp.zeros((MLP,), jnp.float32), 'W_mlp2': jax.random.normal(ks[10], (MLP, H), jnp.float32) * (1.0 / np.sqrt(MLP)), 'b_mlp2': jnp.zeros((H,), jnp.float32)}
    _L2_xcond_all = _L2_xcond_setup()
    _L2_xcond_in = {k: v for k, v in _L2_xcond_all.items() if k in ('W_mod', 'b_mod', 'W_qkv', 'b_qkv', 'W_proj', 'b_proj', 'W_qc', 'b_qc', 'W_kvc', 'b_kvc', 'W_cproj', 'b_cproj', 'W_mlp1', 'b_mlp1', 'W_mlp2', 'b_mlp2')}
    del _L2_xcond_all

    def _L3_xcond_setup():
        import jax, jax.numpy as jnp
        import numpy as np
        EPS = 1e-05

        def _ada_ln(x, c, W_ss, b_ss):
            mu = jnp.mean(x, axis=-1, keepdims=True)
            var = jnp.mean((x - mu) ** 2, axis=-1, keepdims=True)
            h = (x - mu) / jnp.sqrt(var + EPS)
            ss = jax.nn.silu(c) @ W_ss + b_ss
            scale, bias = jnp.split(ss, 2, axis=-1)
            return (1.0 + scale)[:, None, :] * h + bias[:, None, :]
        key = jax.random.key(seed)
        ks = jax.random.split(key, 12)
        B, Lq, Lkv, H = (8, 512, 128, 256)
        s = 0.02
        return {'x_q': jax.random.normal(ks[0], (B, Lq, H), jnp.float32), 'x_kv': jax.random.normal(ks[1], (B, Lkv, H), jnp.float32), 't_vec': jax.random.normal(ks[2], (B, H), jnp.float32), 'Wq': jax.random.normal(ks[3], (H, H), jnp.float32) * s, 'bq': jnp.zeros((H,), jnp.float32), 'Wkv': jax.random.normal(ks[4], (H, 2 * H), jnp.float32) * s, 'bkv': jnp.zeros((2 * H,), jnp.float32), 'Wp': jax.random.normal(ks[5], (H, H), jnp.float32) * s, 'bp': jnp.zeros((H,), jnp.float32), 'Wss_q': jax.random.normal(ks[6], (H, 2 * H), jnp.float32) * s, 'bss_q': jnp.zeros((2 * H,), jnp.float32), 'Wss_kv': jax.random.normal(ks[7], (H, 2 * H), jnp.float32) * s, 'bss_kv': jnp.zeros((2 * H,), jnp.float32)}
    _L3_xcond_all = _L3_xcond_setup()
    _L3_xcond_in = {k: v for k, v in _L3_xcond_all.items() if k in ('Wq', 'bq', 'Wkv', 'bkv', 'Wp', 'bp', 'Wss_q', 'bss_q', 'Wss_kv', 'bss_kv')}
    del _L3_xcond_all
    return {'x': x, 'cond_1024': cond_1024, 'ctx_1024': ctx_1024, 'mask_BxS2_bf1': mask_BxS2_bf1, 'mask_SxS_bk0': mask_SxS_bk0, 'L0_xcond_adaLN_W': _L0_xcond_in['adaLN_W'], 'L0_xcond_adaLN_b': _L0_xcond_in['adaLN_b'], 'L0_xcond_norm1_w': _L0_xcond_in['norm1_w'], 'L0_xcond_qkv_W': _L0_xcond_in['qkv_W'], 'L0_xcond_attn_out_W': _L0_xcond_in['attn_out_W'], 'L0_xcond_normc_w': _L0_xcond_in['normc_w'], 'L0_xcond_cq_W': _L0_xcond_in['cq_W'], 'L0_xcond_ck_W': _L0_xcond_in['ck_W'], 'L0_xcond_cv_W': _L0_xcond_in['cv_W'], 'L0_xcond_co_W': _L0_xcond_in['co_W'], 'L0_xcond_norm2_w': _L0_xcond_in['norm2_w'], 'L0_xcond_mlp_W1': _L0_xcond_in['mlp_W1'], 'L0_xcond_mlp_b1': _L0_xcond_in['mlp_b1'], 'L0_xcond_mlp_W2': _L0_xcond_in['mlp_W2'], 'L0_xcond_mlp_b2': _L0_xcond_in['mlp_b2'], 'L1_xcond_ln_gamma': _L1_xcond_in['ln_gamma'], 'L1_xcond_ln_beta': _L1_xcond_in['ln_beta'], 'L1_xcond_Wq': _L1_xcond_in['Wq'], 'L1_xcond_Wk': _L1_xcond_in['Wk'], 'L1_xcond_Wv': _L1_xcond_in['Wv'], 'L1_xcond_router_W': _L1_xcond_in['router_W'], 'L1_xcond_router_b': _L1_xcond_in['router_b'], 'L1_xcond_e_w1': _L1_xcond_in['e_w1'], 'L1_xcond_e_b1': _L1_xcond_in['e_b1'], 'L1_xcond_e_w2': _L1_xcond_in['e_w2'], 'L1_xcond_e_b2': _L1_xcond_in['e_b2'], 'L1_xcond_gate_w1': _L1_xcond_in['gate_w1'], 'L1_xcond_gate_b1': _L1_xcond_in['gate_b1'], 'L1_xcond_gate_w2': _L1_xcond_in['gate_w2'], 'L1_xcond_gate_b2': _L1_xcond_in['gate_b2'], 'L1_xcond_out_w': _L1_xcond_in['out_w'], 'L1_xcond_out_b': _L1_xcond_in['out_b'], 'L2_xcond_W_mod': _L2_xcond_in['W_mod'], 'L2_xcond_b_mod': _L2_xcond_in['b_mod'], 'L2_xcond_W_qkv': _L2_xcond_in['W_qkv'], 'L2_xcond_b_qkv': _L2_xcond_in['b_qkv'], 'L2_xcond_W_proj': _L2_xcond_in['W_proj'], 'L2_xcond_b_proj': _L2_xcond_in['b_proj'], 'L2_xcond_W_qc': _L2_xcond_in['W_qc'], 'L2_xcond_b_qc': _L2_xcond_in['b_qc'], 'L2_xcond_W_kvc': _L2_xcond_in['W_kvc'], 'L2_xcond_b_kvc': _L2_xcond_in['b_kvc'], 'L2_xcond_W_cproj': _L2_xcond_in['W_cproj'], 'L2_xcond_b_cproj': _L2_xcond_in['b_cproj'], 'L2_xcond_W_mlp1': _L2_xcond_in['W_mlp1'], 'L2_xcond_b_mlp1': _L2_xcond_in['b_mlp1'], 'L2_xcond_W_mlp2': _L2_xcond_in['W_mlp2'], 'L2_xcond_b_mlp2': _L2_xcond_in['b_mlp2'], 'L3_xcond_Wq': _L3_xcond_in['Wq'], 'L3_xcond_bq': _L3_xcond_in['bq'], 'L3_xcond_Wkv': _L3_xcond_in['Wkv'], 'L3_xcond_bkv': _L3_xcond_in['bkv'], 'L3_xcond_Wp': _L3_xcond_in['Wp'], 'L3_xcond_bp': _L3_xcond_in['bp'], 'L3_xcond_Wss_q': _L3_xcond_in['Wss_q'], 'L3_xcond_bss_q': _L3_xcond_in['bss_q'], 'L3_xcond_Wss_kv': _L3_xcond_in['Wss_kv'], 'L3_xcond_bss_kv': _L3_xcond_in['bss_kv']}

def reference(x, cond_1024, ctx_1024, mask_BxS2_bf1, mask_SxS_bk0, L0_xcond_adaLN_W, L0_xcond_adaLN_b, L0_xcond_norm1_w, L0_xcond_qkv_W, L0_xcond_attn_out_W, L0_xcond_normc_w, L0_xcond_cq_W, L0_xcond_ck_W, L0_xcond_cv_W, L0_xcond_co_W, L0_xcond_norm2_w, L0_xcond_mlp_W1, L0_xcond_mlp_b1, L0_xcond_mlp_W2, L0_xcond_mlp_b2, L1_xcond_ln_gamma, L1_xcond_ln_beta, L1_xcond_Wq, L1_xcond_Wk, L1_xcond_Wv, L1_xcond_router_W, L1_xcond_router_b, L1_xcond_e_w1, L1_xcond_e_b1, L1_xcond_e_w2, L1_xcond_e_b2, L1_xcond_gate_w1, L1_xcond_gate_b1, L1_xcond_gate_w2, L1_xcond_gate_b2, L1_xcond_out_w, L1_xcond_out_b, L2_xcond_W_mod, L2_xcond_b_mod, L2_xcond_W_qkv, L2_xcond_b_qkv, L2_xcond_W_proj, L2_xcond_b_proj, L2_xcond_W_qc, L2_xcond_b_qc, L2_xcond_W_kvc, L2_xcond_b_kvc, L2_xcond_W_cproj, L2_xcond_b_cproj, L2_xcond_W_mlp1, L2_xcond_b_mlp1, L2_xcond_W_mlp2, L2_xcond_b_mlp2, L3_xcond_Wq, L3_xcond_bq, L3_xcond_Wkv, L3_xcond_bkv, L3_xcond_Wp, L3_xcond_bp, L3_xcond_Wss_q, L3_xcond_bss_q, L3_xcond_Wss_kv, L3_xcond_bss_kv):
    import jax
    import jax.numpy as jnp

    def _L0_xcond_ref(x, cond_global, cond_tokens, adaLN_W, adaLN_b, norm1_w, qkv_W, attn_out_W, normc_w, cq_W, ck_W, cv_W, co_W, norm2_w, mlp_W1, mlp_b1, mlp_W2, mlp_b2, cond_kv_mask, attn_mask):
        import jax, jax.numpy as jnp
        import numpy as np
        B, N, D, H, LC = (2, 256, 256, 16, 77)
        HD = D // H
        BLOCK = 16
        ROPE_BASE = 10000.0
        EPS = 1e-05

        def _block_diff_mask(n, block_size):
            idx = np.arange(2 * n)
            q = idx[:, None]
            kv = idx[None, :]
            fq = q >= n
            fkv = kv >= n
            bq = np.where(fq, (q - n) // block_size, q // block_size)
            bkv = np.where(fkv, (kv - n) // block_size, kv // block_size)
            block_diagonal = (bq == bkv) & (fq == fkv)
            offset_block_causal = (bq > bkv) & fkv & ~fq
            block_causal = (bq >= bkv) & fq & fkv
            return jnp.asarray(block_diagonal | offset_block_causal | block_causal)

        def _rope_tables(n):
            inv_freq = 1.0 / ROPE_BASE ** (np.arange(0, HD, 2, dtype=np.float32) / HD)
            freqs = np.outer(np.arange(n, dtype=np.float32), inv_freq)
            emb = np.concatenate([freqs, freqs], axis=-1)
            cos = jnp.asarray(np.cos(emb), jnp.float32)[None, :, None, :]
            sin = jnp.asarray(np.sin(emb), jnp.float32)[None, :, None, :]
            return (cos, sin)

        def _ln(x, w):
            xf = x.astype(jnp.float32)
            mu = jnp.mean(xf, axis=-1, keepdims=True)
            var = jnp.mean(jnp.square(xf - mu), axis=-1, keepdims=True)
            y = (xf - mu) * jax.lax.rsqrt(var + EPS)
            return y * w[None, None, :]

        def _apply_rope(t, cos, sin):
            t1, t2 = jnp.split(t, 2, axis=-1)
            rot = jnp.concatenate([-t2, t1], axis=-1)
            return t * cos + rot * sin

        def _attn(q, k, v, mask):
            scale = 1.0 / np.sqrt(HD)
            s = jnp.einsum('bqhd,bkhd->bhqk', q, k) * scale
            s = jnp.where(mask, s, jnp.finfo(s.dtype).min)
            a = jax.nn.softmax(s, axis=-1)
            return jnp.einsum('bhqk,bkhd->bqhd', a, v)
        b, s, d = x.shape
        n = s // 2
        mod = (cond_global @ adaLN_W + adaLN_b)[:, None, :]
        sh_msa, sc_msa, g_msa, sh_x, sc_x, g_x, sh_mlp, sc_mlp, g_mlp = jnp.split(mod, 9, axis=-1)
        x_norm = _ln(x, norm1_w) * (1 + sc_msa) + sh_msa
        cos, sin = _rope_tables(n)

        def qkv(h):
            t = (h @ qkv_W).reshape(b, n, 3, H, HD)
            q, k, v = (t[:, :, 0], t[:, :, 1], t[:, :, 2])
            return (_apply_rope(q, cos, sin), _apply_rope(k, cos, sin), v)
        q1, k1, v1 = qkv(x_norm[:, :n])
        q2, k2, v2 = qkv(x_norm[:, n:])
        q = jnp.concatenate([q1, q2], axis=1)
        k = jnp.concatenate([k1, k2], axis=1)
        v = jnp.concatenate([v1, v2], axis=1)
        self_out = _attn(q, k, v, attn_mask[None, None]).reshape(b, s, d) @ attn_out_W
        x = x + g_msa * self_out
        xc = _ln(x, normc_w) * (1 + sc_x) + sh_x
        qc = (xc @ cq_W).reshape(b, s, H, HD)
        kc = (cond_tokens @ ck_W).reshape(b, LC, H, HD)
        vc = (cond_tokens @ cv_W).reshape(b, LC, H, HD)
        cross = _attn(qc, kc, vc, cond_kv_mask[:, None, None, :]).reshape(b, s, d) @ co_W
        x = x + g_x * cross
        xm = _ln(x, norm2_w) * (1 + sc_mlp) + sh_mlp
        h = jax.nn.gelu(xm @ mlp_W1 + mlp_b1, approximate=True)
        mlp_out = h @ mlp_W2 + mlp_b2
        return x + g_mlp * mlp_out

    def _L1_xcond_ref(mix_hidden_states, global_anchor, prototype_bank, ln_gamma, ln_beta, Wq, Wk, Wv, router_W, router_b, e_w1, e_b1, e_w2, e_b2, gate_w1, gate_b1, gate_w2, gate_b2, out_w, out_b):
        import jax, jax.numpy as jnp
        import numpy as np
        H = 256
        RH = 2 * H
        E = 3
        B, T, P = (8, 512, 64)
        LN_EPS = 1e-05

        def _layer_norm(x, gamma, beta):
            mu = jnp.mean(x, axis=-1, keepdims=True)
            var = jnp.mean(jnp.square(x - mu), axis=-1, keepdims=True)
            return (x - mu) * jax.lax.rsqrt(var + LN_EPS) * gamma + beta
        x = mix_hidden_states
        nx = _layer_norm(x, ln_gamma, ln_beta)
        q = nx @ Wq
        k = prototype_bank @ Wk
        v = prototype_bank @ Wv
        scores = jnp.einsum('bth,bph->btp', q, k) * H ** (-0.5)
        weights = jax.nn.softmax(scores, axis=-1)
        evidence = jnp.einsum('btp,bph->bth', weights, v)
        anchor = jnp.broadcast_to(global_anchor[:, None, :], nx.shape)
        combined = jnp.concatenate([nx, evidence, anchor], axis=-1)
        router_logits = combined @ router_W + router_b
        router_probs = jax.nn.softmax(router_logits, axis=-1)
        h = jax.nn.silu(jnp.einsum('btc,ecr->bter', combined, e_w1) + e_b1)
        expert_out = jnp.einsum('bter,erh->bteh', h, e_w2) + e_b2
        routed = jnp.sum(expert_out * router_probs[..., None], axis=-2)
        g = jax.nn.sigmoid(jax.nn.silu(combined @ gate_w1 + gate_b1) @ gate_w2 + gate_b2)
        refined_delta = g * (routed @ out_w + out_b)
        return x + refined_delta

    def _L2_xcond_ref(x, c, context, W_mod, b_mod, W_qkv, b_qkv, W_proj, b_proj, W_qc, b_qc, W_kvc, b_kvc, W_cproj, b_cproj, W_mlp1, b_mlp1, W_mlp2, b_mlp2):
        import jax, jax.numpy as jnp
        import numpy as np
        LN_EPS = 1e-06

        def _ln(x):
            mu = jnp.mean(x, axis=-1, keepdims=True)
            var = jnp.var(x, axis=-1, keepdims=True)
            return (x - mu) * jax.lax.rsqrt(var + LN_EPS)
        B, N, H = x.shape
        NH = 16
        hd = H // NH
        scale = hd ** (-0.5)
        c_proj = jax.nn.silu(c) @ W_mod + b_mod
        shift_a, scale_a, gate_a, shift_m, scale_m, gate_m = jnp.split(c_proj, 6, axis=-1)

        def modulate(t, shift, sc):
            return t * (1 + sc[:, None]) + shift[:, None]
        x_norm = modulate(_ln(x), shift_a, scale_a)
        qkv = x_norm @ W_qkv + b_qkv
        q, k, v = jnp.split(qkv, 3, axis=-1)
        q = q.reshape(B, N, NH, hd).transpose(0, 2, 1, 3)
        k = k.reshape(B, N, NH, hd).transpose(0, 2, 1, 3)
        v = v.reshape(B, N, NH, hd).transpose(0, 2, 1, 3)
        attn_w = jax.nn.softmax(jnp.einsum('bhqd,bhkd->bhqk', q, k) * scale, axis=-1)
        attn_out = jnp.einsum('bhqk,bhkd->bhqd', attn_w, v)
        attn_out = attn_out.transpose(0, 2, 1, 3).reshape(B, N, H)
        attn_out = attn_out @ W_proj + b_proj
        x = x + gate_a[:, None] * attn_out
        S = context.shape[1]
        q_c = _ln(x) @ W_qc + b_qc
        kv_c = _ln(context) @ W_kvc + b_kvc
        k_c, v_c = jnp.split(kv_c, 2, axis=-1)
        q_c = q_c.reshape(B, N, NH, hd).transpose(0, 2, 1, 3)
        k_c = k_c.reshape(B, S, NH, hd).transpose(0, 2, 1, 3)
        v_c = v_c.reshape(B, S, NH, hd).transpose(0, 2, 1, 3)
        c_attn_w = jax.nn.softmax(jnp.einsum('bhqd,bhsd->bhqs', q_c, k_c) * scale, axis=-1)
        c_attn_out = jnp.einsum('bhqs,bhsd->bhqd', c_attn_w, v_c)
        c_attn_out = c_attn_out.transpose(0, 2, 1, 3).reshape(B, N, H)
        c_attn_out = c_attn_out @ W_cproj + b_cproj
        x = x + c_attn_out
        x_norm2 = modulate(_ln(x), shift_m, scale_m)
        h = jax.nn.gelu(x_norm2 @ W_mlp1 + b_mlp1)
        h = h @ W_mlp2 + b_mlp2
        x = x + gate_m[:, None] * h
        return x

    def _L3_xcond_ref(x_q, x_kv, t_vec, Wq, bq, Wkv, bkv, Wp, bp, Wss_q, bss_q, Wss_kv, bss_kv):
        import jax, jax.numpy as jnp
        import numpy as np
        EPS = 1e-05

        def _ada_ln(x, c, W_ss, b_ss):
            mu = jnp.mean(x, axis=-1, keepdims=True)
            var = jnp.mean((x - mu) ** 2, axis=-1, keepdims=True)
            h = (x - mu) / jnp.sqrt(var + EPS)
            ss = jax.nn.silu(c) @ W_ss + b_ss
            scale, bias = jnp.split(ss, 2, axis=-1)
            return (1.0 + scale)[:, None, :] * h + bias[:, None, :]
        B, Lq, H = x_q.shape
        Lkv = x_kv.shape[1]
        nh = 16
        dh = H // nh
        xq = _ada_ln(x_q, t_vec, Wss_q, bss_q)
        xkv = _ada_ln(x_kv, t_vec, Wss_kv, bss_kv)
        q = (xq @ Wq + bq).reshape(B, Lq, nh, dh)
        kv = (xkv @ Wkv + bkv).reshape(B, Lkv, 2, nh, dh)
        k = kv[:, :, 0]
        v = kv[:, :, 1]
        scores = jnp.einsum('bqhd,bkhd->bhqk', q, k) / jnp.sqrt(jnp.float32(dh))
        attn = jax.nn.softmax(scores, axis=-1)
        out = jnp.einsum('bhqk,bkhd->bqhd', attn, v).reshape(B, Lq, H)
        return x_q + (out @ Wp + bp)
    x = _L0_xcond_ref(x, cond_1024, ctx_1024, L0_xcond_adaLN_W, L0_xcond_adaLN_b, L0_xcond_norm1_w, L0_xcond_qkv_W, L0_xcond_attn_out_W, L0_xcond_normc_w, L0_xcond_cq_W, L0_xcond_ck_W, L0_xcond_cv_W, L0_xcond_co_W, L0_xcond_norm2_w, L0_xcond_mlp_W1, L0_xcond_mlp_b1, L0_xcond_mlp_W2, L0_xcond_mlp_b2, mask_BxS2_bf1, mask_SxS_bk0)
    x = _L1_xcond_ref(x, cond_1024, ctx_1024, L1_xcond_ln_gamma, L1_xcond_ln_beta, L1_xcond_Wq, L1_xcond_Wk, L1_xcond_Wv, L1_xcond_router_W, L1_xcond_router_b, L1_xcond_e_w1, L1_xcond_e_b1, L1_xcond_e_w2, L1_xcond_e_b2, L1_xcond_gate_w1, L1_xcond_gate_b1, L1_xcond_gate_w2, L1_xcond_gate_b2, L1_xcond_out_w, L1_xcond_out_b)
    x = _L2_xcond_ref(x, cond_1024, ctx_1024, L2_xcond_W_mod, L2_xcond_b_mod, L2_xcond_W_qkv, L2_xcond_b_qkv, L2_xcond_W_proj, L2_xcond_b_proj, L2_xcond_W_qc, L2_xcond_b_qc, L2_xcond_W_kvc, L2_xcond_b_kvc, L2_xcond_W_cproj, L2_xcond_b_cproj, L2_xcond_W_mlp1, L2_xcond_b_mlp1, L2_xcond_W_mlp2, L2_xcond_b_mlp2)
    x = _L3_xcond_ref(x, ctx_1024, cond_1024, L3_xcond_Wq, L3_xcond_bq, L3_xcond_Wkv, L3_xcond_bkv, L3_xcond_Wp, L3_xcond_bp, L3_xcond_Wss_q, L3_xcond_bss_q, L3_xcond_Wss_kv, L3_xcond_bss_kv)
    return x

_drawn_inputs = setup_inputs


def setup_inputs(seed=0):
    import zlib

    import numpy as np

    out = dict(_drawn_inputs(seed))
    spreads = {'L0_xcond_norm1_w': (1.0, 0.6),
     'L0_xcond_normc_w': (1.0, 0.6),
     'L0_xcond_norm2_w': (1.0, 0.6),
     'L1_xcond_ln_gamma': (1.0, 0.6),
     'L1_xcond_ln_beta': (0.0, 0.594),
     'L1_xcond_router_b': (0.0, 0.372),
     'L1_xcond_e_b1': (0.0, 0.441),
     'L1_xcond_e_b2': (0.0, 0.1),
     'L1_xcond_gate_b1': (0.0, 0.8),
     'L1_xcond_gate_b2': (0.0, 0.8),
     'L1_xcond_out_b': (0.0, 0.1),
     'L2_xcond_b_mod': (0.0, 0.1),
     'L2_xcond_b_qkv': (0.0, 0.1),
     'L2_xcond_b_proj': (0.0, 0.1),
     'L2_xcond_b_qc': (0.0, 0.567),
     'L2_xcond_b_kvc': (0.0, 0.1),
     'L2_xcond_b_cproj': (0.0, 0.1),
     'L2_xcond_b_mlp1': (0.0, 0.267),
     'L2_xcond_b_mlp2': (0.0, 0.1),
     'L3_xcond_bq': (0.0, 2.0),
     'L3_xcond_bkv': (0.0, 0.351),
     'L3_xcond_bp': (0.0, 0.1),
     'L3_xcond_bss_q': (0.0, 2.0),
     'L3_xcond_bss_kv': (0.0, 0.8)}
    factors = {'L0_xcond_adaLN_b': 8.0,
     'L0_xcond_qkv_W': 2.87,
     'L0_xcond_attn_out_W': 2.769,
     'L0_xcond_cq_W': 8.0,
     'L0_xcond_ck_W': 8.0,
     'L0_xcond_cv_W': 3.136,
     'L0_xcond_co_W': 3.124,
     'L0_xcond_mlp_b1': 25.069,
     'L0_xcond_mlp_b2': 8.0,
     'L3_xcond_Wq': 8.0,
     'L3_xcond_Wss_q': 8.0,
     'L3_xcond_Wss_kv': 3.368}
    for name, (base, spread) in spreads.items():
        noise = np.random.default_rng([zlib.crc32(name.encode()), seed]).standard_normal(out[name].shape)
        drawn = base * np.exp(spread * noise) if base else spread * noise
        out[name] = jnp.asarray(drawn.astype(out[name].dtype))
    for name, factor in factors.items():
        out[name] = (out[name] * factor).astype(out[name].dtype)
    return out
```

```python
from contextlib import ExitStack

import numpy as np
import concourse.bass as bass
from concourse import mybir

F32 = mybir.dt.float32
BF16 = mybir.dt.bfloat16
FP8 = mybir.dt.float8e4
U8 = mybir.dt.uint8
ALU = mybir.AluOpType
ACT = mybir.ActivationFunctionType
AX = mybir.AxisListType

P = 128
NB, SEQ, D = 4, 1024, 256
NT = SEQ // P
KT = D // P
H, HD = 16, 16
HG = 4
NG = H // HG
HALF = 512
NH = SEQ // HALF
NC = 77
CTX = NB * NC
MLP = 4 * D
MT_ = MLP // P
E3, RH = 3, 512
RT = RH // P
ROPE_N = SEQ // 2
SCALE = 1.0 / float(np.sqrt(HD))
SCALE1 = float(D) ** -0.5
Q_PARTS = [0, 0, 0, 1, 1, 2]
K_PARTS = [0, 1, 2, 0, 1, 0]
MASK_ROW = len(Q_PARTS) * HD
MAX_ROW = MASK_ROW + 1
ROWS = MAX_ROW + 3
MASKED = -float(2 ** 100)

MOD0, MOD2, MODQ, MODK = 0, 9 * D, 15 * D, 17 * D
MODN = 19 * D
LN_EPS = [1e-5, 1e-5, 1e-5, 1e-5, 1e-6, 1e-6, 1e-6, 1e-5]

POOL_IDENT, POOL_AKV, POOL_WROT, POOL_CTX, POOL_ZERO = 1, 2, 3, 7, 9
MASK_TILES = [f"mask_{t}" for t in range(NT)]
PE_PREP = ["cond_T", "mod_a", "mod_b", "mod_T", "ctx_T", "kc", "l1_kv", "wq_T", "l1_a", "vc_0", "vc_1", "vc_2"] + MASK_TILES
DVE_PREP = ["zeros", "cond_T", "mod_a", "mod_b", "mod_T", "ab", "ctx_stats", "ctx_rows", "ctx_T", "kc", "kc_high", "kc_rest", "kc_middle", "kc_parts",
            "l1_kv", "wq_T", "l1_a", "vc_0", "vc_1", "vc_2", "mask_row_f", "mask_row"] + [m for t in range(NT) for m in (f"mask_bf_{t}", f"mask_{t}")] + ["v_ones"]


def pixart_kernel(nc, io):
    ctx = ExitStack()
    with ctx:
        ctx.enter_context(nc.allow_non_contiguous_dma(reason="vectors by feature, a few hundred elements each"))

        def sb(name, shape, dt=F32):
            return ctx.enter_context(nc.sbuf_tensor(name, shape, dt))

        def sem(name):
            return ctx.enter_context(nc.semaphore(name))

        X = sb("x_tok", [P, NB * NT, D])
        XN = sb("xn_tok", [P, NT, D])
        XT = sb("x_T", [P, KT, SEQ])
        BIG = sb("big", [P, 16384])
        PR = sb("probs", [P, 2, HG, SEQ])
        V = sb("v_self", [P, NT, H, 32])
        W = sb("weights", [P, 4096])
        MM = sb("mask_T", [P, NT, SEQ], FP8)
        VG = sb("v_group", [P, NT, HG, 32])
        OT = sb("o_T", [P, SEQ])
        WG = sb("w_gated", [P, KT, D])
        GATE = sb("gate_bc", [P, D])
        BIASB = sb("bias_bc", [P, D])
        BV = sb("bias_v_bc", [P, D])
        NHLF = sb("eps_tile", [P, NT])
        ident = sb("ident", [P, P])
        identb = sb("ident_b", [P, P], BF16)
        bigI = sb("ident_masked", [P, P], BF16)
        MODC = sb("mod_cols", [P, MODN // P, NB])
        AB = sb("ln_affine", [P, 8, KT, 2, NB])
        LNW = sb("ln_weights", [P, 5, KT])
        QB = sb("q_bias", [P, 8, KT])
        B1 = sb("mlp_b1", [P, 2, MT_])
        ST = sb("bn_stats", [P, NT, 6])
        MV = sb("mean_var", [P, NT, 2])
        RS = sb("rstd", [P, NT])
        MHALF = sb("minus_half", [P, NT])
        NMP = sb("max_halves", [P, HG, NT, NH])
        NM = sb("row_max", [P, H, NT])
        NMT = sb("row_max_T", [P, P])
        NMR = sb("row_max_rest", [P, P])
        NMB = sb("row_max_parts", [P, 3, P], BF16)
        REC = sb("recip", [P, NT, HG])
        condT = sb("cond_T", [P, KT, NB])
        csT = sb("silu_cond_T", [P, KT, NB])
        A1 = sb("l1_scores_w", [P, KT, NB, NC + E3])
        V1T = sb("l1_v_T", [P, KT, NB, NC])
        NMK = sb("ring_marks", [P, 2])
        AKV = sb("l3_kv_scale", [P, KT, NB])
        NMG = sb("group_max", [P, HG * NT])
        CST = sb("ctx_stats", [NC, NB, 6])
        CMV = sb("ctx_mean_var", [NC, NB, 2])
        MARK = sb("settled", [1, 136], BF16)
        CRS = sb("ctx_rstd", [NC, 2, NB])
        PS = ctx.enter_context(nc.psum_tensor("ps", [P, 8, HALF], F32))
        PSB = PS[:, :, :].bitcast(BF16)

        bigb = BIG[:, :].bitcast(BF16)
        QS = bigb[:, 0:16384].rearrange("p (h n) -> p h n", h=H)
        KS = bigb[:, 16384:32768].rearrange("p (h n) -> p h n", h=H)
        HT = BIG[:, 0:8192].rearrange("p (m n) -> p m n", m=MT_)
        W1 = BIG[:, 8192:10240].rearrange("p (k m) -> p k m", k=KT)
        W2 = BIG[:, 10240:12288].rearrange("p (k m) -> p k m", k=MT_)
        GATEM, BIASM = BIG[:, 12288:12544], BIG[:, 12544:12800]
        KC = BIG[:, 12800:13824].bitcast(BF16)[0:ROWS].rearrange("p (h n) -> p h n", h=H)
        VC = BIG[:, 13824:14336].rearrange("p (h d) -> p h d", h=H)
        prf = PR[:, :, :, :].rearrange("p a b c -> p (a b c)")
        QKP = prf[:, 0:6144].bitcast(BF16).rearrange("p (a t n) -> p a t n", a=3, t=4)
        FR = prf[:, 6144:7168].rearrange("p (a n) -> p a n", a=2)
        RR = prf[:, 7168:8192].rearrange("p (a n) -> p a n", a=2)
        T12 = OT[:, :].rearrange("p (a n) -> p a n", a=2)
        Wqkv = W[:, 0:1536].rearrange("p (k m) -> p k m", k=KT)
        Wrot = W[:, 1536:2560].rearrange("p (k m) -> p k m", k=KT)
        Wo = W[:, 2560:3072].rearrange("p (k m) -> p k m", k=KT)
        Wcq = W[:, 3072:3584].rearrange("p (k m) -> p k m", k=KT)
        Wco = W[:, 3584:4096].rearrange("p (k m) -> p k m", k=KT)
        xnf = XN[:, :, :].rearrange("p a b -> p (a b)")
        COS, SIN = xnf[:, 0:ROPE_N], xnf[:, ROPE_N:2 * ROPE_N]

        MWB = BIG[:, 0:KT * MODN].rearrange("p (k m) -> p k m", k=KT)
        MBIAS = BIG[0:NB, 9728:9728 + MODN]
        MROW = prf[0:NB, 0:MODN]
        KCW = prf[:, 4864:4864 + 3072].rearrange("p (l k m) -> p l k m", l=3, k=KT)
        vf = V[:, :, :, :].rearrange("p a b c -> p (a b c)")
        BV3 = prf[:, 7936:8192]
        CTK = vf[0:NC, 0:3072].rearrange("p (v b m) -> p v b m", v=3, b=NB)
        condR = vf[0:NB, 3072:3072 + D]
        CXT = xnf[:, 0:3 * KT * CTX].rearrange("p (v k n) -> p v k n", v=3, k=KT)
        xtf = XT[:, :, :].rearrange("p a b -> p (a b)")
        W1K = xtf[:, 0:512].rearrange("p (k m) -> p k m", k=KT)
        W1V = xtf[:, 512:1024].rearrange("p (k m) -> p k m", k=KT)
        W1Q = xtf[:, 1024:1536].rearrange("p (k m) -> p k m", k=KT)
        W1QT = xtf[:, 1536:2048].rearrange("p (k m) -> p k m", k=KT)
        KCF = BIG[:, 0:3072].rearrange("p (l k b n) -> p l k b n", l=3, k=KT, b=NB)
        KCR = BIG[:, 3072:6144].rearrange("p (l k b n) -> p l k b n", l=3, k=KT, b=NB)
        KCP = BIG[:, 6144:10752].bitcast(BF16).rearrange("p (a l k b n) -> p a l k b n", a=3, l=3, k=KT, b=NB)
        VCS = BIG[:, 10752:12800].rearrange("p (b h d) -> p b h d", b=NB, h=H)
        K1T = OT[:, 0:KT * CTX].rearrange("p (k n) -> p k n", k=KT)
        MKB = WG[:, :, :].rearrange("p a b -> p (a b)").bitcast(BF16)[:, 0:SEQ]
        MKU = VG[:, :, :, :].rearrange("p a b c -> p (a b c)").bitcast(U8)[:, 0:SEQ]
        MRU = GATE[0:NB, 0:32].bitcast(U8)[:, 0:NC]
        MRF = BIASB[0:NB, 0:P]
        MRB = NMR[0:NB, 0:64].bitcast(BF16)
        MRZ = NMT[0:NB, 0:64].bitcast(BF16)

        HE = BIG[:, 0:8192].rearrange("p (a r n) -> p a r n", a=2, r=RT)
        GT = BIG[:, 8192:10240].rearrange("p (r n) -> p r n", r=KT)
        ROU = BIG[:, 10240:12288].rearrange("p (t m) -> p t m", t=NT)
        PX = BIG[:, 12288:12288 + 640].rearrange("p (t n) -> p t n", t=NT)
        PT = BIG[:, 12928:13952]
        TG = BIG[:, 13952:14976].rearrange("p (a n) -> p a n", a=2)
        YG = BIG[:, 14976:16000].rearrange("p (a n) -> p a n", a=2)
        EW1 = prf[:, 0:6144].rearrange("p (k e m) -> p k e m", k=4, e=E3)
        GW1 = prf[:, 6144:7680].rearrange("p (k m) -> p k m", k=6)
        EW1A = vf[:, 0:3072].rearrange("p (k e m) -> p k e m", k=KT, e=E3)
        EW2 = W[:, 0:3072].rearrange("p (k m) -> p k m", k=E3 * RT)
        GW2 = W[:, 3072:3584].rearrange("p (k m) -> p k m", k=KT)
        OW = W[:, 3584:4096].rearrange("p (k m) -> p k m", k=KT)
        VE = vf[0:NC, 0:1796]
        mmf = MM[:, :, :].rearrange("p a b -> p (a b)").bitcast(F32)
        V1B = mmf[:, 0:KT * NC].rearrange("p (k n) -> p k n", k=KT)
        ANC = mmf[:, 160:160 + 14 * NB].rearrange("p (m b) -> p m b", m=14)
        ANB = mmf[:, 224:238]
        RWT = mmf[:, 240:240 + 6 * E3].rearrange("p (k e) -> p k e", k=6)
        RB = mmf[:, 260:263]
        RAC = mmf[:, 264:264 + NB * E3].rearrange("p (b e) -> p b e", b=NB)
        RL = mmf[:, 280:280 + NT * E3].rearrange("p (t e) -> p t e", t=NT)
        RM = mmf[:, 304:304 + NT]
        RP = mmf[:, 312:312 + NT * E3].rearrange("p (t e) -> p t e", t=NT)
        NX1 = mmf[:, 336:336 + NT]
        SX1 = mmf[:, 344:344 + NT]
        SR1 = mmf[:, 352:352 + NT]
        B2T = mmf[:, 360:360 + KT * E3].rearrange("p (k e) -> p k e", k=KT)
        B2O = mmf[0:E3, 368:368 + D]
        OBB = mmf[0:E3, 624:624 + D]
        GB2 = mmf[0:1, 880:880 + D]
        ONE = mmf[0:1, 1136:1136 + P]
        PTR = OT[0:E3, :]

        QKd = nc.dram_tensor("qk_parts", [3, 2 * D, SEQ], BF16, kind="Internal").ap()
        KCd = nc.dram_tensor("kc_parts", [3, 3, D, NB * P], BF16, kind="Internal").ap()
        VCd = nc.dram_tensor("vc_rows", [3, NB, P, H * 32], F32, kind="Internal").ap()
        MODd = nc.dram_tensor("mod_rows", [NB, MODN], F32, kind="Internal").ap()
        MKd = nc.dram_tensor("mask_rows", [2, NB, P], BF16, kind="Internal").ap()

        def sems(prefix, names):
            return [sem(prefix + n) for n in names.split()]

        x_in, cond_in, modw_in, ctx_in, l1w_in, const_in, small_in = sems("", "x_in cond_in mod_w_in ctx_in l1_w_in const_in small_in")
        mask_in, maskrow_in, kc_out, vc_out, mod_out, mrow_out = sems("", "mask_in mask_row_in kc_out vc_out mod_out mask_row_out")
        pe_prep, dve_prep, pool_prep, act_prep, pool_go = sems("", "pe_prep dve_prep pool_prep act_prep ctx_mean_var")
        w_in = [sem(f"w_in{l}") for l in range(4)]
        ln_st, ln_mv, ln_ep, ln_rs, ln_norm, ln_tp, ln_xt_a, ln_xt_d = sems("ln_", "stats mean_var eps rstd rows turned xT_act xT_dve")
        qk_ps, qk_t, qk_f, qk_h, qk_r, qk_m, qk_l, qk_out, cq_out = sems("qk_", "ps products full high rest middle low out cross_out")
        cs_in, krow_in, cst_a, cst_b = sems("", "cos_sin_in const_rows_in cross_stack0_in cross_stack1_in")
        stack_in = [sem(f"stack_in{g}") for g in range(NG)]
        v_ps, v_sb, vg_in, ring_full, ring_free = sems("", "v_ps v_rows v_group_in ring_full ring_free")
        nm_done, nmt_sb, nm_p1, nm_p2, nm_p3, nm_p4, nm_in = sems("nm_", "done turned high rest middle low in")
        st_full, ex_done, pv_done, acc_out, rec_done, at_done = sems("", "scores_T_full exp_done pv_done acc_out recip_done att_rows")
        c_full, c_free, c_nmT, c_nmt, c_p1, c_p2, c_p3, c_p4, c_nm_in = sems("c_", "max_full max_free nm_turned nm_sb nm_high nm_rest nm_middle nm_low nm_in")
        c_st, c_ex, c_pv, c_acc, c_tp, c_rec, c_at, kc_in = sems("c_", "scores_full exp_done pv_done acc_out turned recip att_rows kc_in")
        o_tp, o_xt_a, o_xt_d, o_ps, o_done = sems("o_", "turned xT_act xT_dve ps added")
        gate_in, bias_in, wg_done, bg_done, biased = sems("", "gate_in bias_in w_gated bias_gated biased")
        mg_in, mw_in, m_ps, m_h, m_ops, m_done, m_w2g, m_bg, m_biased = sems("m_", "gate_in w_in ps hidden out_ps added w2_gated bias_gated biased")
        v_zero, v_one = sems("", "v_zeroed v_ones")
        (e_v1b, e_ve, e_vesb, e_sc, e_mx, e_mxs, e_rl, e_px, e_sr, e_pxn, e_pt, e_ptsb, e_rt, e_r1, e_r2, e_r3, e_rex, e_r4, e_r5, e_rp, e_rpt, e_rptsb, e_hps, e_hsb, e_ops,
         e_ho, e_rot, e_rx_a, e_rx_d, e_fin, e_tg, e_yg, e_fd, e_pro, e_prd) = sems(
            "e_", "v_batch ve_ps ve_sb scores max max_scaled logits exp recip probs_n turned turned_sb router r_sum r_max r_shift r_exp r_den r_recip r_probs r_turned r_turned_sb "
            "hidden_ps hidden out_ps mixed mix_turned mixT_act mixT_dve fin_ps tanh gated added anchors_ps anchors")
        y_out = sem("y_out")

        mod_chunks = [(a, min(a + HALF, z)) for lo, z in ((MOD0, MOD2), (MOD2, MODQ), (MODQ, MODK), (MODK, MODN)) for a in range(lo, z, HALF)]

        places = []

        def settle(eng):
            places.append(eng)
            own = MARK[:, len(places) - 1:len(places)]
            if eng is nc.scalar:
                eng.activation(own, ident[0:1, 0:1], ACT.Copy)
            elif eng is nc.vector:
                eng.memset(own, 0.0)
            else:
                eng.tensor_tensor(own, ident[0:1, 0:1], ident[0:1, 0:1], ALU.add)

        def at(names, name):
            return names.index(name) + 1

        def colview(ap):
            return ap.rearrange("(c p) -> p c", p=P)

        def rowsview(ap):
            return ap.rearrange("(k p) m -> p k m", p=P)

        def bcast(ap, n=P):
            return ap.rearrange("(a m) -> a m", a=1).broadcast_to([n, ap.shape[0]])

        block = ctx.enter_context(nc.Block())
        L = ["L0_xcond_", "L1_xcond_", "L2_xcond_", "L3_xcond_"]
        L0, L1, L2, L3 = L

        def norm(l, b, i):
            return {0: 3 * b, 1: b + 12, 2: 3 * b + 16, 3: b + 28}[l] + i

        def selfs(l, b):
            return {0: b, 2: b + 4}[l]

        def crosses(l, b):
            return {0: b, 2: b + 4, 3: b + 8}[l]

        def outs(l, b, i):
            return {0: 2 * b, 2: 2 * b + 8, 3: b + 16}[l] + i

        def qsteps(l, b, i):
            return {0: 12 * b, 2: 12 * b + 48, 3: 4 * b + 96}[l] + 8 * i

        def krows(l, b, i):
            return 24 + b + 1 if l == 3 else {0: 0, 2: 12}[l] + 3 * b + 2 + i

        def mlps(l, b):
            return {0: b, 2: b + 4}[l]

        def gates(l, b, i):
            return {0: 2 * b, 2: b + 8}[l] + i

        def biases(l, b, i):
            return {2: 2 * b, 3: b + 8}[l] + i

        def ring_plan(with_max, with_tail):
            units = [("max", j, qt, hf) for j in range(HG) for qt in range(NT) for hf in range(NH)] if with_max else []
            steps, used = [], 0
            for k in range(NT * HG):
                ops = []
                if with_tail and k == 7:
                    ops.append(("tail",))
                upto = min(len(units), len(units) * (k + 1) // 28)
                ops += units[used:upto]
                used = upto
                if with_max and k == 28:
                    ops.append(("nm",))
                steps.append(ops)
            return steps

        def ring_use(op):
            return 1 if op[0] == "max" else 2

        MAXN = HG * NT * NH
        PRO = MAXN + 2
        BODY = MAXN + 2 + 2
        RINGN = PRO + (BODY - 2) + 2 * BODY + 2 + 2

        def ring_at(s, g):
            if isinstance(g, int) and g == 0:
                return s * RINGN + PRO
            return s * RINGN + PRO + (BODY - 2) + (g - 1) * BODY

        @block.sync
        def _(sp):
            sp.dma_start(condR, io["cond_1024"]).then_inc(cond_in, 16)
            sp.dma_start(ident[:, :], io["ident"]).then_inc(const_in, 16)
            sp.dma_start(MWB[:, :, MOD0:MOD2], rowsview(io[L0 + "adaLN_W"])).then_inc(modw_in, 16)
            sp.dma_start(MWB[:, :, MOD2:MODQ], rowsview(io[L2 + "W_mod"])).then_inc(modw_in, 16)
            sp.dma_start(MWB[:, :, MODQ:MODK], rowsview(io[L3 + "Wss_q"])).then_inc(modw_in, 16)
            sp.dma_start(MWB[:, :, MODK:MODN], rowsview(io[L3 + "Wss_kv"])).then_inc(modw_in, 16)
            for a, z, n in ((MOD0, MOD2, L0 + "adaLN_b"), (MOD2, MODQ, L2 + "b_mod"), (MODQ, MODK, L3 + "bss_q"), (MODK, MODN, L3 + "bss_kv")):
                sp.dma_start(MBIAS[:, a:z], bcast(io[n], NB)).then_inc(modw_in, 16)
            sp.dma_start(CTK[:, 0], io["ctx_1024"].rearrange("b s d -> s b d")).then_inc(ctx_in, 16)
            for i, n in enumerate((L0 + "norm1_w", L0 + "normc_w", L0 + "norm2_w", L1 + "ln_gamma", L1 + "ln_beta")):
                sp.dma_start(LNW[:, i, :], colview(io[n])).then_inc(small_in, 16)
            for i, ap in enumerate((io[L2 + "b_qkv"][0:D], io[L2 + "b_qkv"][D:2 * D], io[L2 + "b_qc"], io[L3 + "bq"], io[L2 + "b_kvc"][0:D], io[L3 + "bkv"][0:D])):
                sp.dma_start(QB[:, i, :], colview(ap)).then_inc(small_in, 16)
            sp.dma_start(B1[:, 0, :], colview(io[L0 + "mlp_b1"])).then_inc(small_in, 16)
            sp.dma_start(B1[:, 1, :], colview(io[L2 + "b_mlp1"])).then_inc(small_in, 16)
            sp.dma_start(BV[:, :], bcast(io[L2 + "b_kvc"][D:2 * D])).then_inc(small_in, 16)
            sp.dma_start(BV3, bcast(io[L3 + "bkv"][D:2 * D])).then_inc(small_in, 16)
            sp.dma_start(MRU, io["cross_mask"]).then_inc(maskrow_in, 16)
            sp.dma_start(KCW[:, 0, :, 0:D], rowsview(io[L0 + "ck_W"])).then_inc(ctx_in, 16)
            sp.dma_start(KCW[:, 0, :, D:2 * D], rowsview(io[L0 + "cv_W"])).then_inc(ctx_in, 16)
            sp.dma_start(KCW[:, 1], rowsview(io[L2 + "W_kvc"])).then_inc(ctx_in, 16)
            sp.dma_start(KCW[:, 2], rowsview(io[L3 + "Wkv"])).then_inc(ctx_in, 16)
            for w, n in ((W1K, "Wk"), (W1V, "Wv"), (W1Q, "Wq")):
                sp.dma_start(w, rowsview(io[L1 + n])).then_inc(l1w_in, 16)
            for b in range(NB):
                sp.dma_start(A1[:, :, b, NC:NC + E3], rowsview(io[L1 + "router_W"][0:D, :])).then_inc(l1w_in, 16)
            for b in range(NB):
                sp.dma_start(X[:, b * NT:(b + 1) * NT, :], io["x"][b].rearrange("(t p) d -> p t d", p=P)).then_inc(x_in, 16)
            sp.dma_start(Wqkv, rowsview(io[L0 + "qkv_W"])).then_inc(w_in[0], 16)
            for w, n in ((Wo, "attn_out_W"), (Wcq, "cq_W"), (Wco, "co_W")):
                sp.dma_start(w, rowsview(io[L0 + n])).then_inc(w_in[0], 16)
            sp.wait_ge(dve_prep, at(DVE_PREP, "mod_b"))
            sp.dma_start(MODd, MROW).then_inc(mod_out, 16)
            sp.wait_ge(dve_prep, at(DVE_PREP, "kc_parts"))
            for a in range(3):
                for l in range(3):
                    sp.dma_start(KCd[a, l].rearrange("(k p) n -> p k n", p=P), KCP[:, a, l].rearrange("p k b n -> p k (b n)")).then_inc(kc_out, 16)
            for l in range(3):
                sp.wait_ge(dve_prep, at(DVE_PREP, f"vc_{l}"))
                sp.dma_start(VCd[l].rearrange("b p n -> p b n"), VCS.rearrange("p b h d -> p b (h d)")).then_inc(vc_out, 16)
            sp.wait_ge(dve_prep, at(DVE_PREP, "mask_row"))
            sp.dma_start(MKd[0], MRB).then_inc(mrow_out, 16)
            sp.dma_start(MKd[1], MRZ).then_inc(mrow_out, 16)
            for t in range(NT):
                if t:
                    sp.wait_ge(dve_prep, at(DVE_PREP, f"mask_bf_{t - 1}"))
                sp.dma_start(MKU, io["self_mask"][t * P:(t + 1) * P, :]).then_inc(mask_in, 16)
            sp.wait_ge(mod_out, 16)
            sp.wait_ge(kc_out, 9 * 16)
            sp.wait_ge(vc_out, 3 * 16)
            sp.wait_ge(mrow_out, 2 * 16)
            sp.wait_ge(pe_prep, len(PE_PREP))
            sp.wait_ge(dve_prep, len(DVE_PREP))

            def load_gate(l, b, chunk, dst, done):
                base = {0: MOD0, 2: MOD2}[l]
                sp.dma_start(dst[:, :], MODd[bass.ds(b, 1), base + chunk * D:base + (chunk + 1) * D].broadcast_to([P, D])).then_inc(done, 16)

            def self_dma(l, b):
                s, n = selfs(l, b), norm(l, b, 0)
                sp.wait_ge(ln_tp, 2 * n + 2)
                if l == 0:
                    sp.dma_start(COS, io["cos"]).then_inc(cs_in, 16)
                    sp.dma_start(SIN, io["sin"]).then_inc(cs_in, 16)
                load_gate(l, b, 2, GATE, gate_in)
                if l == 2:
                    sp.dma_start(BIASB[:, :], bcast(io[L2 + "b_proj"])).then_inc(bias_in, 16)
                sp.dma_start(QS[MASK_ROW:ROWS], io["q_rows"].rearrange("r (h n) -> r h n", h=H)).then_inc(krow_in, 16)
                sp.dma_start(KS[MASK_ROW:ROWS], io["k_rows"].rearrange("r (h n) -> r h n", h=H)).then_inc(krow_in, 16)
                for tile in range(4):
                    sp.wait_ge(qk_l, qsteps(l, b, 0) + 2 * tile + 2)
                    sp.dma_start(QKd[:, tile * P:(tile + 1) * P, :].rearrange("a p n -> p a n"), QKP[:, :, tile, :]).then_inc(qk_out, 16)
                    if tile % 2 == 0:
                        continue
                    sp.wait_ge(qk_out, s * 64 + 16 * tile + 16)
                    for g in (tile - 1, tile):
                        for r in range(6):
                            for st, part, f0 in ((QS, Q_PARTS[r], (tile - 1) * P), (KS, K_PARTS[r], tile * P)):
                                src = QKd[part, f0 + (g % 2) * 64:f0 + (g % 2) * 64 + 64, :].rearrange("(h d) n -> d h n", d=HD)
                                sp.dma_start(st[r * HD:(r + 1) * HD, g * HG:(g + 1) * HG, :], src).then_inc(stack_in[g], 16)
                for g in range(NG):
                    sp.wait_ge(nm_p4, s * NG + g + 1)
                    for a in range(3):
                        sp.dma_start(QS[MAX_ROW + a:MAX_ROW + a + 1, g * HG:(g + 1) * HG, :].rearrange("p h (t n) -> p (h t) n", n=P),
                                     NMB[0:HG * NT, a, :]).then_inc(nm_in, 16)

            def cross_dma(l, b):
                c, n = crosses(l, b), norm(l, b, 0 if l == 3 else 1)
                li = {0: 0, 2: 1, 3: 2}[l]
                sp.wait_ge(ln_tp, 2 * n + 2)
                if l == 0:
                    load_gate(l, b, 5, GATE, gate_in)
                else:
                    sp.dma_start(BIASB[:, :], bcast(io[L2 + "b_cproj"] if l == 2 else io[L3 + "bp"])).then_inc(bias_in, 16)
                sp.dma_start(QS[MASK_ROW:ROWS], io["q_rows"].rearrange("r (h n) -> r h n", h=H)).then_inc(krow_in, 16)
                for r in range(6):
                    sp.dma_start(KC[r * HD:(r + 1) * HD, :, :], KCd[K_PARTS[r], li][:, bass.ts(b, P)].rearrange("(h d) n -> d h n", d=HD)).then_inc(kc_in, 16)
                sp.dma_start(KC[MASK_ROW:MASK_ROW + 1, :, :], MKd[0 if l == 0 else 1, bass.ds(b, 1), :].rearrange("a (c n) -> a c n", c=1).broadcast_to([1, H, P])).then_inc(kc_in, 16)
                sp.dma_start(KC[MAX_ROW:ROWS, :, :], io["k_rows"][1:4, 0:H * P].rearrange("r (h n) -> r h n", h=H)).then_inc(kc_in, 16)
                sp.dma_start(VC[:, :, :], VCd[li, bass.ds(b, 1)].rearrange("a p (h d) -> p (a h) d", h=H)).then_inc(kc_in, 16)
                if l != 3:
                    load_gate(l, b, 8 if l == 0 else 5, GATEM, mg_in)
                    sp.dma_start(BIASM[:, :], bcast(io[L[l] + ("mlp_b2" if l == 0 else "b_mlp2")])).then_inc(mg_in, 16)
                    sp.dma_start(W1, rowsview(io[L[l] + ("mlp_W1" if l == 0 else "W_mlp1")])).then_inc(mw_in, 16)
                    sp.dma_start(W2, rowsview(io[L[l] + ("mlp_W2" if l == 0 else "W_mlp2")])).then_inc(mw_in, 16)
                for ft in range(KT):
                    sp.wait_ge(qk_l, qsteps(l, b, 0 if l == 3 else 1) + 2 * ft + 2)
                    sp.dma_start(QKd[:, ft * P:(ft + 1) * P, :].rearrange("a p n -> p a n"), QKP[:, :, ft, :]).then_inc(cq_out, 16)
                    sp.wait_ge(cq_out, c * 32 + 16 * ft + 16)
                    for r in range(6):
                        src = QKd[Q_PARTS[r], ft * P:(ft + 1) * P, :].rearrange("(h d) n -> d h n", d=HD)
                        sp.dma_start(QS[r * HD:(r + 1) * HD, ft * 8:ft * 8 + 8, :], src).then_inc((cst_a, cst_b)[ft], 16)
                sp.wait_ge(c_p4, c + 1)
                for a in range(3):
                    sp.dma_start(QS[MAX_ROW + a:MAX_ROW + a + 1, :, :].rearrange("p h (t n) -> p (h t) n", n=P), NMB[:, a, :]).then_inc(c_nm_in, 16)

            with sp.Fori(0, NB) as b:
                self_dma(0, b)
                cross_dma(0, b)

            sp.wait_ge(m_done, 4 * NB)
            for e in range(E3):
                sp.dma_start(EW1[:, :, e, :], rowsview(io[L1 + "e_w1"][e, 0:4 * P, :])).then_inc(w_in[1], 16)
                sp.dma_start(EW1A[:, :, e, :], rowsview(io[L1 + "e_w1"][e, 4 * P:6 * P, :])).then_inc(w_in[1], 16)
                sp.dma_start(EW2[:, e * RT:(e + 1) * RT, :], rowsview(io[L1 + "e_w2"][e])).then_inc(w_in[1], 16)
                sp.dma_start(ANB[:, e * RT:(e + 1) * RT], colview(io[L1 + "e_b1"][e])).then_inc(w_in[1], 16)
                sp.dma_start(B2T[:, :, e], colview(io[L1 + "e_b2"][e])).then_inc(w_in[1], 16)
            sp.dma_start(GW1, rowsview(io[L1 + "gate_w1"])).then_inc(w_in[1], 16)
            sp.dma_start(GW2, rowsview(io[L1 + "gate_w2"])).then_inc(w_in[1], 16)
            sp.dma_start(OW, rowsview(io[L1 + "out_w"])).then_inc(w_in[1], 16)
            sp.dma_start(ANB[:, 12:14], colview(io[L1 + "gate_b1"])).then_inc(w_in[1], 16)
            sp.dma_start(RWT, rowsview(io[L1 + "router_W"])).then_inc(w_in[1], 16)
            sp.dma_start(RB, bcast(io[L1 + "router_b"])).then_inc(w_in[1], 16)
            sp.dma_start(OBB, bcast(io[L1 + "out_b"], E3)).then_inc(w_in[1], 16)
            sp.dma_start(GB2, bcast(io[L1 + "gate_b2"], 1)).then_inc(w_in[1], 16)

            sp.wait_ge(e_fd, 4 * NB)
            sp.dma_start(Wqkv, rowsview(io[L2 + "W_qkv"])).then_inc(w_in[2], 16)
            for w, n in ((Wo, "W_proj"), (Wcq, "W_qc"), (Wco, "W_cproj")):
                sp.dma_start(w, rowsview(io[L2 + n])).then_inc(w_in[2], 16)
            sp.dma_start(BV[:, :], bcast(io[L2 + "b_qkv"][2 * D:3 * D])).then_inc(w_in[2], 16)
            with sp.Fori(0, NB) as b:
                self_dma(2, b)
                cross_dma(2, b)

            sp.wait_ge(m_done, 8 * NB)
            sp.dma_start(Wcq, rowsview(io[L3 + "Wq"])).then_inc(w_in[3], 16)
            sp.dma_start(Wco, rowsview(io[L3 + "Wp"])).then_inc(w_in[3], 16)
            with sp.Fori(0, NB) as b:
                cross_dma(3, b)
                sp.wait_ge(o_done, outs(3, b, 0) * 4 + 4)
                sp.dma_start(io["y"][bass.ds(b, 1)].rearrange("a (t p) d -> p (a t) d", p=P), X[:, bass.ts(b, NT), :]).then_inc(y_out, 16)
            sp.wait_ge(y_out, 16 * NB)

        @block.tensor
        def _(pe):
            def mm(out, lhsT, rhs, first=True, last=True):
                return pe.matmul(out, lhsT, rhs, start=first, stop=last)

            pe.wait_ge(cond_in, 16)
            pe.wait_ge(const_in, 16)
            for kt in range(KT):
                last = pe.transpose(PS[:, 0, kt * NB:(kt + 1) * NB], condR[:, kt * P:(kt + 1) * P], ident[0:NB, 0:NB])
            last.then_inc(pe_prep, 1)
            pe.wait_ge(modw_in, 8 * 16)
            pe.wait_ge(dve_prep, at(DVE_PREP, "cond_T"))
            pe.wait_ge(act_prep, 1)
            for i in range(10):
                if i == 5:
                    pe.wait_ge(dve_prep, at(DVE_PREP, "mod_a"))
                lo, hi = mod_chunks[i]
                for kt in range(KT):
                    last = mm(PS[0:NB, 1 + i % 5, 0:hi - lo], (condT if hi <= MOD2 else csT)[:, kt, :], MWB[:, kt, lo:hi], kt == 0, kt == 1)
                if i in (4, 9):
                    last.then_inc(pe_prep, 1)
            pe.wait_ge(dve_prep, at(DVE_PREP, "mod_b"))
            for c in range(MODN // P):
                last = pe.transpose(PS[:, 0, c * NB:(c + 1) * NB], MROW[:, c * P:(c + 1) * P], ident[0:NB, 0:NB])
            last.then_inc(pe_prep, 1)
            pe.wait_ge(dve_prep, at(DVE_PREP, "ctx_rows"))
            for v in range(3):
                for kt in range(KT):
                    for b in range(NB):
                        last = pe.transpose(PS[:, 1 + v * KT + kt, b * NC:(b + 1) * NC], CTK[:, v, b, kt * P:(kt + 1) * P], ident[0:NC, 0:NC])
            last.then_inc(pe_prep, 1)
            pe.wait_ge(dve_prep, at(DVE_PREP, "ctx_T"))
            for l in range(3):
                for m in range(KT):
                    for kt in range(KT):
                        last = mm(PS[:, 1 + l * KT + m, 0:CTX], KCW[:, l, kt, m * P:(m + 1) * P], CXT[:, l, kt, :], kt == 0, kt == 1)
            last.then_inc(pe_prep, 1)
            pe.wait_ge(dve_prep, at(DVE_PREP, "kc"))
            pe.wait_ge(l1w_in, 7 * 16)
            for i, w in enumerate((W1K, W1V)):
                for m in range(KT):
                    for kt in range(KT):
                        last = mm(PS[:, 1 + i * KT + m, 0:CTX], w[:, kt, m * P:(m + 1) * P], CXT[:, 0, kt, :], kt == 0, kt == 1)
            last.then_inc(pe_prep, 1)
            for m in range(KT):
                for kt in range(KT):
                    last = pe.transpose(PS[:, 5, (m * KT + kt) * P:(m * KT + kt + 1) * P], W1Q[:, kt, m * P:(m + 1) * P], ident[:, :])
            last.then_inc(pe_prep, 1)
            pe.wait_ge(dve_prep, at(DVE_PREP, "wq_T"))
            for m in range(KT):
                for kt in range(KT):
                    last = mm(PS[:, 6 + m, 0:CTX], W1QT[:, kt, m * P:(m + 1) * P], K1T[:, kt, :], kt == 0, kt == 1)
            last.then_inc(pe_prep, 1)
            pe.wait_ge(dve_prep, at(DVE_PREP, "l1_kv"))
            for l in range(3):
                if l:
                    pe.wait_ge(dve_prep, at(DVE_PREP, f"vc_{l - 1}"))
                for b in range(NB):
                    for kt in range(KT):
                        last = mm(PS[0:NC, 1 + b // 2, (b % 2) * D:(b % 2 + 1) * D], CXT[:, l, kt, b * NC:(b + 1) * NC], KCW[:, l, kt, D:2 * D], kt == 0, kt == 1)
                last.then_inc(pe_prep, 1)
            for t in range(NT):
                pe.wait_ge(dve_prep, at(DVE_PREP, f"mask_bf_{t}"))
                for k in range(NT):
                    last = pe.transpose(PSB[:, 4 + (t % 2) * 2 + k // 4, (k % 4) * P:(k % 4 + 1) * P], MKB[:, k * P:(k + 1) * P], identb[:, :])
                last.then_inc(pe_prep, 1)

            def norm_pe(n):
                for t in range(NT):
                    pe.wait_ge(ln_norm, n * 8 + t + 1)
                    for ft in range(KT):
                        last = pe.transpose(PS[:, ft * 2 + t // 4, (t % 4) * P:(t % 4 + 1) * P], XN[:, t, ft * P:(ft + 1) * P], ident[:, :])
                    if t % 4 == 3:
                        last.then_inc(ln_tp, 1)

            def project_pe(n, tiles, free, f0):
                for i, (w, col, rot) in enumerate(tiles):
                    for hf in range(NH):
                        st = 2 * i + hf
                        if i == 0:
                            pe.wait_ge(ln_xt_a, n * 2 + hf + 1)
                            pe.wait_ge(ln_xt_d, n * 2 + hf + 1)
                        if st >= 2:
                            pe.wait_ge(free, f0 + st - 1)
                        bank = 4 + 2 * (st % 2)
                        for kt in range(KT):
                            last = mm(PS[:, bank, :], w[:, kt, col:col + P], XT[:, kt, hf * HALF:(hf + 1) * HALF], kt == 0, kt == 1)
                        if rot is not None:
                            for kt in range(KT):
                                last = mm(PS[:, bank + 1, :], Wrot[:, kt, rot:rot + P], XT[:, kt, hf * HALF:(hf + 1) * HALF], kt == 0, kt == 1)
                        last.then_inc(qk_ps, 1)

            def self_pe(l, b):
                s, n = selfs(l, b), norm(l, b, 0)
                tiles = [(Wqkv, m * P + a * D, (m * P + a * D) if l == 0 else None) for m in range(KT) for a in range(2)]
                project_pe(n, tiles, qk_t if l == 0 else qk_f, 8 * b if l == 0 else qsteps(l, b, 0))
                for t in range(NT):
                    for kt in range(KT):
                        last = mm(PS[:, t // 2, (t % 2) * D:(t % 2 + 1) * D], XT[:, kt, t * P:(t + 1) * P], Wqkv[:, kt, 2 * D:3 * D], kt == 0, kt == 1)
                    if t % 2:
                        last.then_inc(v_ps, 1)
                pe.wait_ge(v_sb, s * 4 + 4)
                masked = l == 0

                def ring_op(op, u, g):
                    bank = op[4]
                    if op[0] == "max":
                        _, j, qt, hf = op[:4]
                        pe.wait_ge(ring_free, u - 1)
                        h = g * HG + j
                        last = mm(PS[:, bank, :], QS[0:MASK_ROW, bass.ds(h, 1), qt * P:(qt + 1) * P].rearrange("p a n -> p (a n)"),
                                  KS[0:MASK_ROW, bass.ds(h, 1), hf * HALF:(hf + 1) * HALF].rearrange("p a n -> p (a n)"), True, not masked)
                        if masked:
                            for i in range(4):
                                last = mm(PS[:, bank, i * P:(i + 1) * P], MM[:, hf * 4 + i, qt * P:(qt + 1) * P], bigI[:, :], False, i == 3)
                        last.then_inc(ring_full, 1)
                    elif op[0] == "nm":
                        pe.wait_ge(nm_done, s * NG + g + 1)
                        pe.transpose(PS[0:HG * NT, 0, 0:P], NMG[:, :], ident[:, :]).then_inc(ring_full, 2)
                    else:
                        pe.wait_ge(ring_free, u)
                        pe.wait_ge(acc_out, s * NG + g + 1)
                        for qt in range(NT):
                            last = pe.transpose(PS[:, qt // 4, (qt % 4) * P:(qt % 4 + 1) * P], OT[:, qt * P:(qt + 1) * P], ident[:, :])
                        last.then_inc(ring_full, 2)

                def run_ring(ops, u, g, gtail):
                    for op in ops:
                        ring_op(tuple(op) + (None,) * (4 - len(op)) + (u[1] % 2,), u[0] + u[1], gtail if op[0] == "tail" else g)
                        u[1] += ring_use(op)

                def pv(g, kt, peeled0):
                    pe.wait_ge(ex_done, (s * NG + g) * 32 + 4 * kt + 4)
                    if kt == 0:
                        pe.wait_ge(vg_in, s * NG + g + 1)
                        if not peeled0:
                            pe.wait_ge(acc_out, s * NG + g)
                    for hf in range(NH):
                        for j in range(HG):
                            last = mm(PS[32 * j:32 * j + 32, 6 + hf, :], VG[:, kt, j, :], PR[:, kt % 2, j, hf * HALF:(hf + 1) * HALF], kt == 0, kt == NT - 1)
                    last.then_inc(pv_done, 1)

                def body(g, with_max, with_tail, peeled0=False):
                    u = [ring_at(s, g), 0]
                    plan = ring_plan(with_max, with_tail)
                    if with_max:
                        wait_stack(g + 1)
                    pe.wait_ge(nm_in, (s * NG + g + 1) * 48)
                    for k in range(32):
                        kt, j = k // 4, k % 4
                        if k >= 2 or not peeled0:
                            pe.wait_ge(ex_done, (s * NG + g) * 32 + k - 1)
                        h = g * HG + j
                        for hf in range(NH):
                            last = mm(PS[:, 2 + 2 * (k % 2) + hf, :], KS[0:ROWS, bass.ds(h, 1), kt * P:(kt + 1) * P].rearrange("p a n -> p (a n)"),
                                      QS[0:ROWS, bass.ds(h, 1), hf * HALF:(hf + 1) * HALF].rearrange("p a n -> p (a n)"), True, not masked)
                            if masked:
                                last = mm(PS[:, 2 + 2 * (k % 2) + hf, :], bigI[:, :], MM[:, kt, hf * HALF:(hf + 1) * HALF], False, True)
                        last.then_inc(st_full, 1)
                        run_ring(plan[k], u, g + 1, g - 1)
                        if j == 1 and kt >= 1:
                            pv(g, kt - 1, peeled0)
                    pv(g, NT - 1, peeled0)

                def wait_stack(g):
                    if isinstance(g, int):
                        pe.wait_ge(stack_in[g], (s + 1) * 192)
                    else:
                        for i in range(NG):
                            pe.wait_ge(stack_in[i], (s + 1) * 192)

                pe.wait_ge(krow_in, krows(l, b, 0) * 16)
                wait_stack(0)
                u = [s * RINGN, 0]
                for j in range(HG):
                    for qt in range(NT):
                        for hf in range(NH):
                            if u[1] < 2:
                                first_max(pe, mm, l, j, qt, hf, u[1])
                            else:
                                ring_op(("max", j, qt, hf, u[1] % 2), u[0] + u[1], 0)
                            u[1] += 1
                ring_op(("nm", None, None, None, 0), u[0] + u[1], 0)
                body(0, True, False, peeled0=True)
                with pe.Fori(1, NG - 1) as g:
                    body(g, True, True)
                body(NG - 1, False, True)
                ring_op(("tail", None, None, None, 0), ring_at(s, NG - 1) + 2, NG - 1)

            def first_max(pe, mm, l, j, qt, hf, bank):
                last = mm(PS[:, bank, :], QS[0:MASK_ROW, j, qt * P:(qt + 1) * P], KS[0:MASK_ROW, j, hf * HALF:(hf + 1) * HALF], True, l != 0)
                if l == 0:
                    for i in range(4):
                        last = mm(PS[:, bank, i * P:(i + 1) * P], MM[:, hf * 4 + i, qt * P:(qt + 1) * P], bigI[:, :], False, i == 3)
                last.then_inc(ring_full, 1)

            def out_pe(l, b, i, att_sem, att_val, w, gated):
                o = outs(l, b, i)
                pe.wait_ge(att_sem, att_val)
                for t in range(NT):
                    for ft in range(KT):
                        last = pe.transpose(PS[:, ft * 2 + t // 4, (t % 4) * P:(t % 4 + 1) * P], XN[:, t, ft * P:(ft + 1) * P], ident[:, :])
                    if t % 4 == 3:
                        last.then_inc(o_tp, 1)
                if gated is not None:
                    pe.wait_ge(wg_done, gated + 1)
                for t in range(NT):
                    if t % 4 == 0:
                        pe.wait_ge(o_xt_a, o * 2 + t // 4 + 1)
                        pe.wait_ge(o_xt_d, o * 2 + t // 4 + 1)
                    for kt in range(KT):
                        last = mm(PS[:, 4 + t // 2, (t % 2) * D:(t % 2 + 1) * D], XT[:, kt, t * P:(t + 1) * P], w[:, kt, :], kt == 0, kt == 1)
                    if t % 2:
                        last.then_inc(o_ps, 1)

            def cross_pe(l, b):
                c, n = crosses(l, b), norm(l, b, 0 if l == 3 else 1)
                project_pe(n, [(Wcq, m * P, None) for m in range(KT)], qk_f, qsteps(l, b, 0 if l == 3 else 1))
                pe.wait_ge(krow_in, krows(l, b, 1) * 16)
                pe.wait_ge(kc_in, (c + 1) * 9 * 16)
                for r in range(32):
                    g, qt = r // 8, r % 8
                    if r in (0, 16):
                        pe.wait_ge((cst_a, cst_b)[r // 16], (c + 1) * 96)
                    if r >= 2:
                        pe.wait_ge(c_free, c * 32 + r - 1)
                    for j in range(HG):
                        last = mm(PS[:, r % 2, j * NC:(j + 1) * NC], QS[0:MAX_ROW, g * HG + j, qt * P:(qt + 1) * P], KC[0:MAX_ROW, g * HG + j, 0:NC])
                    last.then_inc(c_full, 1)
                pe.wait_ge(c_free, c * 32 + 32)
                pe.transpose(PS[:, 0, 0:P], NM[:, :, :].rearrange("p h t -> p (h t)"), ident[:, :]).then_inc(c_nmT, 1)
                pe.wait_ge(c_nm_in, (c + 1) * 48)

                def pv(g):
                    pe.wait_ge(c_ex, c * H + 4 * g + 4)
                    if g:
                        pe.wait_ge(c_acc, c * NG + g)
                    for hf in range(NH):
                        for j in range(HG):
                            last = mm(PS[32 * j:32 * j + 32, 6 + hf, :], VC[:, g * HG + j, :], PR[:, g % 2, j, hf * HALF:(hf + 1) * HALF])
                    last.then_inc(c_pv, 1)

                def tail(g):
                    pe.wait_ge(c_acc, c * NG + g + 1)
                    if g:
                        pe.wait_ge(c_at, c * 8 + 2 * g)
                    for qt in range(NT):
                        last = pe.transpose(PS[:, qt // 4, (qt % 4) * P:(qt % 4 + 1) * P], OT[:, qt * P:(qt + 1) * P], ident[:, :])
                    last.then_inc(c_tp, 1)

                for h in range(H):
                    if h >= 2:
                        pe.wait_ge(c_ex, c * H + h - 1)
                    for hf in range(NH):
                        last = mm(PS[:, 2 + 2 * (h % 2) + hf, :], KC[0:ROWS, h, :], QS[0:ROWS, h, hf * HALF:(hf + 1) * HALF])
                    last.then_inc(c_st, 1)
                    if h >= 5 and h % 4 == 1:
                        pv(h // 4 - 1)
                    if h >= 7 and h % 4 == 3:
                        tail(h // 4 - 1)
                pv(NG - 1)
                tail(NG - 1)

            def mlp_pe(l, b):
                m_, n = mlps(l, b), norm(l, b, 2)
                pe.wait_ge(mw_in, (m_ + 1) * 32)
                for i in range(MT_ * NH):
                    m, hf = i // 2, i % 2
                    if i < 2:
                        pe.wait_ge(ln_xt_a, n * 2 + hf + 1)
                        pe.wait_ge(ln_xt_d, n * 2 + hf + 1)
                    if i >= 4:
                        pe.wait_ge(m_h, m_ * 16 + i - 3)
                    for kt in range(KT):
                        last = mm(PS[:, 4 + i % 4, :], W1[:, kt, m * P:(m + 1) * P], XT[:, kt, hf * HALF:(hf + 1) * HALF], kt == 0, kt == 1)
                    last.then_inc(m_ps, 1)
                pe.wait_ge(m_w2g, m_ + 1)
                pe.wait_ge(m_h, m_ * 16 + 16)
                for t in range(NT):
                    for kt in range(MT_):
                        last = mm(PS[:, t // 2, (t % 2) * D:(t % 2 + 1) * D], HT[:, kt, t * P:(t + 1) * P], W2[:, kt, :], kt == 0, kt == MT_ - 1)
                    if t % 2:
                        last.then_inc(m_ops, 1)

            def layer02_pe(l, b):
                norm_pe(norm(l, b, 0))
                self_pe(l, b)
                out_pe(l, b, 0, at_done, (selfs(l, b) + 1) * 8, WG, gates(l, b, 0))
                norm_pe(norm(l, b, 1))
                cross_pe(l, b)
                out_pe(l, b, 1, c_at, (crosses(l, b) + 1) * 8, WG if l == 0 else Wco, gates(l, b, 1) if l == 0 else None)
                norm_pe(norm(l, b, 2))
                mlp_pe(l, b)

            pe.wait_ge(w_in[0], 4 * 16)
            pe.wait_ge(pool_prep, POOL_WROT)
            with pe.Fori(0, NB) as b:
                layer02_pe(0, b)

            pe.wait_ge(w_in[1], (E3 * 5 + 8) * 16)
            for m in range(14):
                for kt in range(KT):
                    w = EW1A[:, kt, m // RT, (m % RT) * P:(m % RT + 1) * P] if m < 12 else GW1[:, 4 + kt, (m - 12) * P:(m - 11) * P]
                    mm(PS[:, 4, m * NB:(m + 1) * NB], w, condT[:, kt, :], kt == 0, kt == 1)
            for b in range(NB):
                for kt in range(KT):
                    mm(PS[:, 5, b * 4:b * 4 + E3], condT[:, kt, b:b + 1].broadcast_to([P, P]), RWT[:, 4 + kt, :], kt == 0, kt == 1)
            for kt in range(KT):
                last = mm(PS[0:E3, 6, 0:D], B2T[:, kt, :], OW[:, kt, :], kt == 0, kt == 1)
            last.then_inc(e_pro, 1)
            pe.wait_ge(e_prd, 4)

            def layer1_pe(b):
                n = norm(1, b, 0)
                norm_pe(n)
                pe.wait_ge(e_v1b, b + 1)
                for i in range(3):
                    for kt in range(KT):
                        mm(PS[0:NC, 4 + i, :], V1B[:, kt, :], EW1[:, 2 + kt, i, :], kt == 0, kt == 1)
                for kt in range(KT):
                    mm(PS[0:NC, 7, 0:D], V1B[:, kt, :], GW1[:, 2 + kt, :], kt == 0, kt == 1)
                for kt in range(KT):
                    last = mm(PS[0:NC, 7, D:D + E3], V1B[:, kt, :], RWT[:, 2 + kt, :], kt == 0, kt == 1)
                last.then_inc(e_ve, 1)
                pe.wait_ge(ln_xt_a, n * 2 + 2)
                pe.wait_ge(ln_xt_d, n * 2 + 2)
                for t in range(NT):
                    for kt in range(KT):
                        last = mm(PS[:, t // 4, (t % 4) * 80:(t % 4) * 80 + 80], XT[:, kt, t * P:(t + 1) * P],
                                  A1[:, kt, bass.ds(b, 1), :].rearrange("p a n -> p (a n)"), kt == 0, kt == 1)
                last.then_inc(e_sc, 1)
                pe.wait_ge(e_pxn, b + 1)
                for t in range(NT):
                    last = pe.transpose(PS[0:NC, 2 + t // 4, (t % 4) * P:(t % 4 + 1) * P], PX[:, t, 0:NC], ident[:, :])
                last.then_inc(e_pt, 1)
                pe.wait_ge(e_ptsb, b + 1)
                pe.wait_ge(e_vesb, b * 2 + 2)
                for t in range(NT):
                    last = mm(PS[:, 0, t * 4:t * 4 + E3], PT[0:NC, t * P:(t + 1) * P], VE[:, 1792:1792 + E3])
                last.then_inc(e_rt, 1)

                def hidden(q, w, col):
                    hf = q % 2
                    if q >= 4:
                        pe.wait_ge(e_hsb, b * 28 + q - 3)
                    for kt in range(KT):
                        mm(PS[:, 4 + q % 4, :], w(kt), XT[:, kt, hf * HALF:(hf + 1) * HALF], kt == 0, False)
                    mm(PS[:, 4 + q % 4, :], VE[:, col:col + P], PT[0:NC, hf * HALF:(hf + 1) * HALF], False, True).then_inc(e_hps, 1)

                def expert_out(e):
                    pe.wait_ge(e_hsb, b * 28 + 4 + 8 * e + 8)
                    for t in range(NT):
                        o = e * NT + t
                        if o >= 4:
                            pe.wait_ge(e_ho, b * 24 + o - 3)
                        for r in range(RT):
                            last = mm(PS[:, o % 4, 0:D], HE[:, e % 2, r, t * P:(t + 1) * P], EW2[:, e * RT + r, :], r == 0, r == RT - 1)
                        last.then_inc(e_ops, 1)

                for q in range(4):
                    r = q // 2
                    hidden(q, lambda kt: GW1[:, kt, r * P:(r + 1) * P], 1536 + r * P)
                for e in range(E3):
                    for q in range(8):
                        r = q // 2
                        hidden(4 + 8 * e + q, lambda kt: EW1[:, kt, e, r * P:(r + 1) * P], e * RH + r * P)
                    if e == 0:
                        pe.wait_ge(e_rp, b + 1)
                        for t in range(NT):
                            last = pe.transpose(PS[0:E3, t // 4, (t % 4) * P:(t % 4 + 1) * P], RP[:, t, :], ident[:, :])
                        last.then_inc(e_rpt, 1)
                        pe.wait_ge(e_rptsb, b + 1)
                    else:
                        expert_out(e - 1)
                expert_out(E3 - 1)
                pe.wait_ge(e_ho, b * 24 + 24)
                for t in range(NT):
                    for ft in range(KT):
                        last = pe.transpose(PS[:, ft * 2 + t // 4, (t % 4) * P:(t % 4 + 1) * P], ROU[:, t, ft * P:(ft + 1) * P], ident[:, :])
                    if t % 4 == 3:
                        last.then_inc(e_rot, 1)
                for i in range(4):
                    if i % 2 == 0:
                        pe.wait_ge(e_rx_a, b * 2 + i // 2 + 1)
                        pe.wait_ge(e_rx_d, b * 2 + i // 2 + 1)
                    if i >= 2:
                        pe.wait_ge(e_fd, b * 4 + i - 1)
                    for t in (2 * i, 2 * i + 1):
                        c0 = (t % 2) * D
                        for kt in range(KT):
                            mm(PS[:, 4 + (i % 2) * 2, c0:c0 + D], XT[:, kt, t * P:(t + 1) * P], OW[:, kt, :], kt == 0, False)
                        mm(PS[:, 4 + (i % 2) * 2, c0:c0 + D], PTR[:, t * P:(t + 1) * P], B2O, False, True)
                        for kt in range(KT):
                            mm(PS[:, 5 + (i % 2) * 2, c0:c0 + D], GT[:, kt, t * P:(t + 1) * P], GW2[:, kt, :], kt == 0, False)
                        last = mm(PS[:, 5 + (i % 2) * 2, c0:c0 + D], ONE, GB2, False, True)
                    last.then_inc(e_fin, 1)

            with pe.Fori(0, NB) as b:
                layer1_pe(b)

            pe.wait_ge(w_in[2], 5 * 16)
            with pe.Fori(0, NB) as b:
                layer02_pe(2, b)

            pe.wait_ge(w_in[3], 2 * 16)
            with pe.Fori(0, NB) as b:
                norm_pe(norm(3, b, 0))
                cross_pe(3, b)
                out_pe(3, b, 0, c_at, (crosses(3, b) + 1) * 8, Wco, None)

        @block.vector
        def _(dve):
            def step(ins, name):
                ins.then_inc(dve_prep, 1)
                assert done.append(name) is None and DVE_PREP[len(done) - 1] == name, name

            def wait(name):
                dve.wait_ge(dve_prep, at(DVE_PREP, name))

            done = []
            dve.memset(CRS[:, :, :], 0.0)
            dve.memset(MRZ, 0.0)
            step(dve.memset(MHALF[:, :], -0.5), "zeros")
            dve.wait_ge(pe_prep, at(PE_PREP, "cond_T"))
            step(dve.tensor_copy(condT[:, :, :], PS[:, 0, 0:KT * NB].rearrange("p (k b) -> p k b", k=KT)), "cond_T")
            dve.wait_ge(modw_in, 8 * 16)
            for i, (lo, hi) in enumerate(mod_chunks):
                if i in (0, 5):
                    dve.wait_ge(pe_prep, at(PE_PREP, "mod_a" if i == 0 else "mod_b"))
                last = dve.tensor_tensor(MROW[:, lo:hi], PS[0:NB, 1 + i % 5, 0:hi - lo], MBIAS[:, lo:hi], ALU.add)
                if i in (4, 9):
                    step(last, "mod_a" if i == 4 else "mod_b")
            dve.wait_ge(pe_prep, at(PE_PREP, "mod_T"))
            step(dve.tensor_copy(MODC[:, :, :], PS[:, 0, 0:MODN // P * NB].rearrange("p (c b) -> p c b", b=NB)), "mod_T")
            dve.wait_ge(small_in, 15 * 16)
            wait("mod_T")
            for n, scale, shift in ((0, MOD0 + D, MOD0), (1, MOD0 + 4 * D, MOD0 + 3 * D), (2, MOD0 + 7 * D, MOD0 + 6 * D), (3, None, None),
                                    (4, MOD2 + D, MOD2), (5, None, None), (6, MOD2 + 4 * D, MOD2 + 3 * D), (7, MODQ, MODQ + D)):
                for kt in range(KT):
                    A, B = AB[:, n, kt, 0, :], AB[:, n, kt, 1, :]
                    if n < 3:
                        dve.tensor_scalar(A, MODC[:, scale // P + kt, :], 1.0, LNW[:, n, kt:kt + 1], ALU.add, ALU.mult)
                    elif n == 3:
                        dve.tensor_scalar(A, MODC[:, 0, :], 0.0, LNW[:, 3, kt:kt + 1], ALU.mult, ALU.add)
                    elif n == 5:
                        dve.memset(A, 1.0)
                    else:
                        dve.tensor_scalar(A, MODC[:, scale // P + kt, :], 1.0, None, ALU.add)
                    if n == 3:
                        last = dve.tensor_scalar(B, MODC[:, 0, :], 0.0, LNW[:, 4, kt:kt + 1], ALU.mult, ALU.add)
                    elif n == 5:
                        last = dve.memset(B, 0.0)
                    else:
                        last = dve.tensor_copy(B, MODC[:, shift // P + kt, :])
            step(last, "ab")
            dve.wait_ge(ctx_in, 5 * 16)
            for b in range(NB):
                last = dve.bn_stats(CST[:, b, :], CTK[:, 0, b, :])
            step(last, "ctx_stats")
            wait("ctx_stats")
            for b in range(NB):
                last = dve.bn_aggr(CMV[:, b, :], CST[:, b, :])
            last.then_inc(pool_go, 1)
            dve.wait_ge(pool_go, 1)
            dve.wait_ge(pool_prep, POOL_CTX)
            for v in range(2):
                for b in range(NB):
                    last = dve.tensor_scalar(CTK[:, 1 + v, b, :], CTK[:, 0, b, :], CMV[:, b, 0:1], CRS[:, v, b:b + 1], ALU.subtract, ALU.mult)
            step(last, "ctx_rows")
            dve.wait_ge(pe_prep, at(PE_PREP, "ctx_T"))
            for kt in range(KT):
                dve.tensor_copy(CXT[:, 0, kt, :], PS[:, 1 + kt, 0:CTX])
                dve.tensor_copy(CXT[:, 1, kt, :], PS[:, 1 + KT + kt, 0:CTX])
                for b in range(NB):
                    last = dve.tensor_scalar(CXT[:, 2, kt, b * NC:(b + 1) * NC], PS[:, 1 + 2 * KT + kt, b * NC:(b + 1) * NC], AKV[:, kt, b:b + 1],
                                             MODC[:, (MODK + D) // P + kt, b:b + 1], ALU.mult, ALU.add)
            step(last, "ctx_T")
            dve.wait_ge(pe_prep, at(PE_PREP, "kc"))
            dve.wait_ge(pool_prep, POOL_ZERO)
            for l in range(3):
                for m in range(KT):
                    src = PS[:, 1 + l * KT + m, 0:CTX].rearrange("p (b n) -> p b n", b=NB)
                    if l == 0:
                        last = dve.tensor_copy(KCF[:, l, m, :, 0:NC], src)
                    else:
                        last = dve.tensor_scalar(KCF[:, l, m, :, 0:NC], src, QB[:, 3 + l, m:m + 1], None, ALU.add)
            step(last, "kc")
            wait("kc")
            full, rest = BIG[:, 0:3072], BIG[:, 3072:6144]
            part = [BIG[:, 6144 + a * 1536:6144 + (a + 1) * 1536].bitcast(BF16) for a in range(3)]
            step(dve.tensor_copy(part[0], full), "kc_high")
            wait("kc_high")
            step(dve.tensor_tensor(rest, full, part[0], ALU.subtract), "kc_rest")
            wait("kc_rest")
            step(dve.tensor_copy(part[1], rest), "kc_middle")
            wait("kc_middle")
            step(dve.tensor_tensor(part[2], rest, part[1], ALU.subtract), "kc_parts")
            dve.wait_ge(pe_prep, at(PE_PREP, "l1_kv"))
            for m in range(KT):
                dve.tensor_copy(K1T[:, m, :], PS[:, 1 + m, 0:CTX])
                last = dve.tensor_copy(V1T[:, m, :, :], PS[:, 3 + m, 0:CTX].rearrange("p (b n) -> p b n", b=NB))
            step(last, "l1_kv")
            dve.wait_ge(pe_prep, at(PE_PREP, "wq_T"))
            step(dve.tensor_copy(W1QT.rearrange("p k m -> p (k m)"), PS[:, 5, :]), "wq_T")
            dve.wait_ge(pe_prep, at(PE_PREP, "l1_a"))
            for m in range(KT):
                last = dve.tensor_copy(A1[:, m, :, 0:NC], PS[:, 6 + m, 0:CTX].rearrange("p (b n) -> p b n", b=NB))
            step(last, "l1_a")
            for l in range(3):
                dve.wait_ge(pe_prep, at(PE_PREP, f"vc_{l}"))
                if l:
                    dve.wait_ge(vc_out, l * 16)
                for b in range(NB):
                    src = PS[0:NC, 1 + b // 2, (b % 2) * D:(b % 2 + 1) * D].rearrange("p (h d) -> p h d", h=H)
                    if l == 0:
                        last = dve.tensor_copy(VCS[0:NC, b, :, 0:HD], src)
                    else:
                        last = dve.tensor_tensor(VCS[0:NC, b, :, 0:HD], src, (BV, BV3)[l - 1][0:NC, :].rearrange("p (h d) -> p h d", h=H), ALU.add)
                step(last, f"vc_{l}")
            dve.wait_ge(maskrow_in, 16)
            dve.memset(MRF[:, NC:P], 0.0)
            step(dve.tensor_copy(MRF[:, 0:NC], MRU), "mask_row_f")
            wait("mask_row_f")
            dve.tensor_scalar(MRB, MRF, 1.0, -MASKED, ALU.subtract, ALU.mult)
            step(dve.memset(MRZ[:, NC:P], MASKED), "mask_row")
            for t in range(NT):
                dve.wait_ge(mask_in, (t + 1) * 16)
                if t:
                    dve.wait_ge(pe_prep, at(PE_PREP, f"mask_{t - 1}"))
                step(dve.tensor_scalar(MKB, MKU, -1.0, 1.0, ALU.mult, ALU.add), f"mask_bf_{t}")
                dve.wait_ge(pe_prep, at(PE_PREP, f"mask_{t}"))
                for i in range(2):
                    last = dve.tensor_copy(MM[:, i * 4:(i + 1) * 4, t * P:(t + 1) * P], PSB[:, 4 + (t % 2) * 2 + i, 0:HALF].rearrange("p (k q) -> p k q", q=P), saturate=False)
                step(last, f"mask_{t}")
            dve.wait_ge(v_zero, 1)
            step(dve.memset(V[:, :, :, HD:HD + 1], 1.0), "v_ones")
            assert len(done) == len(DVE_PREP)

            def norm_dve(n, b, ln, x_sem, x_val):
                dve.wait_ge(x_sem, x_val)
                settle(dve)
                x = X[:, bass.ts(b, NT), :]
                for t in range(NT):
                    last = dve.bn_stats(ST[:, t, :], x[:, t, :])
                last.then_inc(ln_st, 1)
                dve.wait_ge(ln_st, n + 1)
                settle(dve)
                for t in range(NT):
                    last = dve.bn_aggr(MV[:, t, :], ST[:, t, :])
                last.then_inc(ln_mv, 1)
                dve.wait_ge(ln_rs, n + 1)
                for t in range(NT):
                    dve.tensor_scalar(XN[:, t, :], x[:, t, :], MV[:, t, 0:1], RS[:, t:t + 1], ALU.subtract, ALU.mult).then_inc(ln_norm, 1)
                for hf in range(NH):
                    dve.wait_ge(ln_tp, n * 2 + hf + 1)
                    dve.tensor_scalar(XT[:, 1, hf * HALF:(hf + 1) * HALF], PS[:, 2 + hf, :], AB[:, ln, 1, 0, bass.ds(b, 1)], AB[:, ln, 1, 1, bass.ds(b, 1)],
                                      ALU.mult, ALU.add).then_inc(ln_xt_d, 1)

            def parts_dve(q0, st, steps):
                if 1 <= st <= steps:
                    k = st - 1
                    if k >= 2:
                        dve.wait_ge(qk_l, q0 + k - 1)
                    dve.wait_ge(qk_h, q0 + k + 1)
                    dve.tensor_tensor(RR[:, k % 2, :], FR[:, k % 2, :], QKP[:, 0, k // 2, (k % 2) * HALF:(k % 2 + 1) * HALF], ALU.subtract).then_inc(qk_r, 1)
                if 2 <= st <= steps + 1:
                    k = st - 2
                    dve.wait_ge(qk_m, q0 + k + 1)
                    dve.tensor_tensor(QKP[:, 2, k // 2, (k % 2) * HALF:(k % 2 + 1) * HALF], RR[:, k % 2, :], QKP[:, 1, k // 2, (k % 2) * HALF:(k % 2 + 1) * HALF],
                                      ALU.subtract).then_inc(qk_l, 1)

            def self_dve(l, b):
                s, q0 = selfs(l, b), qsteps(l, b, 0)
                if l == 0:
                    dve.wait_ge(cs_in, (b + 1) * 32)
                for st in range(10):
                    if l == 0 and st < 8:
                        bank = 4 + 2 * (st % 2)
                        dve.wait_ge(qk_ps, q0 + st + 1)
                        if st:
                            dve.wait_ge(qk_f, q0 + st)
                        dve.tensor_tensor(T12[:, 0, :], PS[:, bank, :], COS, ALU.mult)
                        dve.tensor_tensor(T12[:, 1, :], PS[:, bank + 1, :], SIN, ALU.mult).then_inc(qk_t, 1)
                        dve.wait_ge(qk_t, b * 8 + st + 1)
                        dve.tensor_tensor(FR[:, st % 2, :], T12[:, 0, :], T12[:, 1, :], ALU.add).then_inc(qk_f, 1)
                    parts_dve(q0, st, 8)
                for i in range(4):
                    dve.wait_ge(v_ps, s * 4 + i + 1)
                    src = PS[:, i, :].rearrange("p (t h d) -> p t h d", t=2, h=H)
                    for t in range(2):
                        if l == 0:
                            last = dve.tensor_copy(V[:, 2 * i + t, :, 0:HD], src[:, t])
                        else:
                            last = dve.tensor_tensor(V[:, 2 * i + t, :, 0:HD], src[:, t], BV[:, :].rearrange("p (h d) -> p h d", h=H), ALU.add)
                    last.then_inc(v_sb, 1)

                def ring_op(op, u, g, rc, tails):
                    bank = u[1] % 2
                    if op[0] == "max":
                        _, j, qt, hf = op
                        dve.wait_ge(ring_full, u[0] + u[1] + 1)
                        last = dve.tensor_reduce(NMP[:, j, qt, hf:hf + 1], PS[:, bank, :], AX.X, ALU.max, negate=True)
                        last.then_inc(ring_free, 1)
                        if (j, qt, hf) == (HG - 1, NT - 1, NH - 1):
                            dve.wait_ge(ring_free, u[0] + u[1] + 1)
                            dve.tensor_tensor(NMG[:, :], NMP[:, :, :, 0].rearrange("p j t -> p (j t)"), NMP[:, :, :, 1].rearrange("p j t -> p (j t)"), ALU.min).then_inc(nm_done, 1)
                    elif op[0] == "nm":
                        dve.wait_ge(ring_full, u[0] + u[1] + 2)
                        dve.tensor_copy(NMT[0:HG * NT, :], PS[0:HG * NT, 0, 0:P]).then_inc(nmt_sb, 1)
                        dve.wait_ge(nmt_sb, s * NG + g + 1)
                        dve.tensor_copy(NMK[0:HG * NT, 0:1], NMT[0:HG * NT, 0:1]).then_inc(ring_free, 2)
                    else:
                        dve.wait_ge(ring_full, u[0] + u[1] + 2)
                        for hf in range(NH):
                            src = PS[:, hf, :].rearrange("p (t j m) -> p t j m", t=4, j=HG)
                            dve.reciprocal(REC[:, hf * 4:hf * 4 + 4, :], src[:, :, :, HD]).then_inc(rec_done, 1)
                        dve.wait_ge(rec_done, (s * NG + g) * 2 + 2)
                        for t in range(NT):
                            src = PS[:, t // 4, :].rearrange("p (t j m) -> p t j m", t=4, j=HG)
                            last = dve.tensor_tensor(XN[:, t, bass.ts(g, HG * HD)].rearrange("p (j d) -> p j d", j=HG), src[:, t % 4, :, 0:HD],
                                                     REC[:, t, :].rearrange("p (j a) -> p j a", a=1).broadcast_to([P, HG, HD]), ALU.mult)
                            if t % 4 == 3:
                                last.then_inc(at_done, 1)
                        dve.wait_ge(at_done, (s * NG + g) * 2 + 2)
                        dve.tensor_copy(NMK[:, 0:1], REC[:, 0, 0:1]).then_inc(ring_free, 2)

                def run(g, with_max, with_tail):
                    u = [ring_at(s, g), 0]
                    for ops in ring_plan(with_max, with_tail):
                        for op in ops:
                            ring_op(op, u, g - 1 if op[0] == "tail" else g + 1, None, None)
                            u[1] += ring_use(op)

                u = [s * RINGN, 0]
                for j in range(HG):
                    for qt in range(NT):
                        for hf in range(NH):
                            ring_op(("max", j, qt, hf), u, 0, None, None)
                            u[1] += 1
                ring_op(("nm",), u, 0, None, None)
                run(0, True, False)
                with dve.Fori(1, NG - 1) as g:
                    run(g, True, True)
                run(NG - 1, False, True)
                ring_op(("tail",), [ring_at(s, NG - 1), 2], NG - 1, None, None)

            def out_dve(l, b, i, biased_i):
                o = outs(l, b, i)
                for hf in range(NH):
                    dve.wait_ge(o_tp, o * 2 + hf + 1)
                    dve.tensor_copy(XT[:, 1, hf * HALF:(hf + 1) * HALF], PS[:, 2 + hf, :]).then_inc(o_xt_d, 1)
                if biased_i is not None:
                    dve.wait_ge(biased, biased_i + 1)
                for k in range(4):
                    dve.wait_ge(o_ps, o * 4 + k + 1)
                    x = X[:, bass.ds(b * NT + 2 * k, 2), :].rearrange("p a d -> p (a d)")
                    dve.tensor_tensor(x, PS[:, 4 + k, :], x, ALU.add).then_inc(o_done, 1)

            def cross_dve(l, b):
                c, q0 = crosses(l, b), qsteps(l, b, 0 if l == 3 else 1)
                for st in range(6):
                    parts_dve(q0, st, 4)
                for r in range(32):
                    g, qt = r // 8, r % 8
                    dve.wait_ge(c_full, c * 32 + r + 1)
                    dve.tensor_reduce(NM[:, g * HG:(g + 1) * HG, qt], PS[:, r % 2, 0:HG * NC].rearrange("p (j n) -> p j n", j=HG), AX.X, ALU.max, negate=True).then_inc(c_free, 1)
                dve.wait_ge(c_nmT, c + 1)
                dve.tensor_copy(NMT[:, :], PS[:, 0, 0:P]).then_inc(c_nmt, 1)
                for g in range(NG):
                    dve.wait_ge(c_pv, c * NG + g + 1)
                    if g:
                        dve.wait_ge(c_tp, c * NG + g)
                    dve.tensor_copy(OT[:, :].rearrange("p (a n) -> p a n", a=2), PS[:, 6:8, :]).then_inc(c_acc, 1)
                    dve.wait_ge(c_tp, c * NG + g + 1)
                    for hf in range(NH):
                        src = PS[:, hf, :].rearrange("p (t j m) -> p t j m", t=4, j=HG)
                        dve.reciprocal(REC[:, hf * 4:hf * 4 + 4, :], src[:, :, :, HD]).then_inc(c_rec, 1)
                    dve.wait_ge(c_rec, (c * NG + g) * 2 + 2)
                    for t in range(NT):
                        src = PS[:, t // 4, :].rearrange("p (t j m) -> p t j m", t=4, j=HG)
                        last = dve.tensor_tensor(XN[:, t, g * HG * HD:(g + 1) * HG * HD].rearrange("p (j d) -> p j d", j=HG), src[:, t % 4, :, 0:HD],
                                                 REC[:, t, :].rearrange("p (j a) -> p j a", a=1).broadcast_to([P, HG, HD]), ALU.mult)
                        if t % 4 == 3:
                            last.then_inc(c_at, 1)

            def mlp_dve(l, b):
                m_ = mlps(l, b)
                dve.wait_ge(m_biased, m_ + 1)
                for k in range(4):
                    dve.wait_ge(m_ops, m_ * 4 + k + 1)
                    x = X[:, bass.ds(b * NT + 2 * k, 2), :].rearrange("p a d -> p (a d)")
                    dve.tensor_tensor(x, PS[:, k, :], x, ALU.add).then_inc(m_done, 1)

            def layer02_dve(l, b, x_sem, x_val):
                norm_dve(norm(l, b, 0), b, 0 if l == 0 else 4, x_sem, x_val)
                self_dve(l, b)
                out_dve(l, b, 0, biases(l, b, 0) if l == 2 else None)
                norm_dve(norm(l, b, 1), b, 1 if l == 0 else 5, o_done, outs(l, b, 0) * 4 + 4)
                cross_dve(l, b)
                out_dve(l, b, 1, biases(l, b, 1) if l == 2 else None)
                norm_dve(norm(l, b, 2), b, 2 if l == 0 else 6, o_done, outs(l, b, 1) * 4 + 4)
                mlp_dve(l, b)

            dve.wait_ge(dve_prep, len(DVE_PREP))
            with dve.Fori(0, NB) as b:
                layer02_dve(0, b, x_in, NB * 16)

            dve.wait_ge(w_in[1], (E3 * 5 + 8) * 16)
            dve.memset(ONE, 1.0).then_inc(e_prd, 1)
            dve.wait_ge(e_pro, 1)
            dve.tensor_tensor(ANC, PS[:, 4, 0:14 * NB].rearrange("p (m b) -> p m b", m=14), ANB.rearrange("p (m a) -> p m a", a=1).broadcast_to([P, 14, NB]), ALU.add).then_inc(e_prd, 1)
            dve.tensor_tensor(RAC, PS[:, 5, 0:16].rearrange("p (b e) -> p b e", e=4)[:, :, 0:E3], RB.rearrange("p (a e) -> p a e", a=1).broadcast_to([P, NB, E3]), ALU.add).then_inc(e_prd, 1)
            dve.tensor_tensor(B2O, PS[0:E3, 6, 0:D], OBB, ALU.add).then_inc(e_prd, 1)
            dve.wait_ge(e_prd, 4)

            def layer1_dve(b):
                n = norm(1, b, 0)
                dve.tensor_copy(V1B, V1T[:, :, bass.ds(b, 1), :].rearrange("p k a n -> p k (a n)")).then_inc(e_v1b, 1)
                norm_dve(n, b, 3, m_done, 4 * NB)
                dve.wait_ge(e_sc, b + 1)
                for i in range(2):
                    ps = PS[:, i, 0:320].rearrange("p (t n) -> p t n", n=80)
                    dve.tensor_tensor(RL[:, i * 4:(i + 1) * 4, :], ps[:, :, NC:NC + E3], RAC[:, bass.ds(b, 1), :].broadcast_to([P, 4, E3]), ALU.add).then_inc(e_rl, 1)
                    dve.tensor_reduce(NX1[:, i * 4:(i + 1) * 4], ps[:, :, 0:NC], AX.X, ALU.max, negate=True).then_inc(e_mx, 1)
                dve.wait_ge(e_mx, b * 2 + 2)
                dve.tensor_scalar(SR1, NX1, SCALE1, None, ALU.mult).then_inc(e_mxs, 1)
                dve.wait_ge(e_px, b * NT + NT)
                dve.reciprocal(NX1, SX1).then_inc(e_sr, 1)
                dve.wait_ge(e_sr, b + 1)
                dve.tensor_tensor(PX[:, :, 0:NC], PX[:, :, 0:NC], NX1.rearrange("p (t a) -> p t a", a=1).broadcast_to([P, NT, NC]), ALU.mult).then_inc(e_pxn, 1)
                dve.wait_ge(e_rt, b + 1)
                dve.wait_ge(e_rl, b * 2 + 2)
                dve.tensor_tensor(RL, PS[:, 0, 0:NT * 4].rearrange("p (t e) -> p t e", e=4)[:, :, 0:E3], RL, ALU.add).then_inc(e_r1, 1)
                dve.wait_ge(e_r1, b + 1)
                dve.tensor_reduce(RM, RL, AX.X, ALU.max, negate=True).then_inc(e_r2, 1)
                dve.wait_ge(e_r2, b + 1)
                bc = RM.rearrange("p (t a) -> p t a", a=1).broadcast_to([P, NT, E3])
                dve.tensor_tensor(RL, RL, bc, ALU.add).then_inc(e_r3, 1)
                dve.wait_ge(e_rex, b + 1)
                dve.tensor_reduce(RM, RP, AX.X, ALU.add).then_inc(e_r4, 1)
                dve.wait_ge(e_r4, b + 1)
                dve.reciprocal(SX1, RM).then_inc(e_r5, 1)
                dve.wait_ge(e_r5, b + 1)
                dve.tensor_tensor(RP, RP, SX1.rearrange("p (t a) -> p t a", a=1).broadcast_to([P, NT, E3]), ALU.mult).then_inc(e_rp, 1)
                dve.wait_ge(e_rpt, b + 1)
                dve.tensor_copy(PTR.rearrange("p (a n) -> p a n", a=2), PS[0:E3, 0:2, :]).then_inc(e_rptsb, 1)
                for e in range(E3):
                    for t in range(NT):
                        o = e * NT + t
                        dve.wait_ge(e_ops, b * 24 + o + 1)
                        if e == 0:
                            dve.tensor_scalar(ROU[:, t, :], PS[:, o % 4, 0:D], RP[:, t, 0:1], None, ALU.mult).then_inc(e_ho, 1)
                        else:
                            dve.wait_ge(e_ho, b * 24 + o - NT + 1)
                            dve.scalar_tensor_tensor(ROU[:, t, :], PS[:, o % 4, 0:D], RP[:, t, e:e + 1], ROU[:, t, :], ALU.mult, ALU.add).then_inc(e_ho, 1)
                for hf in range(NH):
                    dve.wait_ge(e_rot, b * 2 + hf + 1)
                    dve.tensor_copy(XT[:, 1, hf * HALF:(hf + 1) * HALF], PS[:, 2 + hf, :]).then_inc(e_rx_d, 1)
                for i in range(4):
                    dve.wait_ge(e_tg, b * 4 + i + 1)
                    if i >= 2:
                        dve.wait_ge(e_fd, b * 4 + i - 1)
                    dve.scalar_tensor_tensor(YG[:, i % 2, :], TG[:, i % 2, :], 1.0, PS[:, 4 + (i % 2) * 2, :], ALU.add, ALU.mult).then_inc(e_yg, 1)
                    dve.wait_ge(e_yg, b * 4 + i + 1)
                    x = X[:, bass.ds(b * NT + 2 * i, 2), :].rearrange("p a d -> p (a d)")
                    dve.scalar_tensor_tensor(x, YG[:, i % 2, :], 0.5, x, ALU.mult, ALU.add).then_inc(e_fd, 1)

            with dve.Fori(0, NB) as b:
                layer1_dve(b)

            dve.wait_ge(w_in[2], 5 * 16)
            dve.wait_ge(v_zero, 2)
            dve.memset(V[:, :, :, HD:HD + 1], 1.0).then_inc(v_one, 1)
            with dve.Fori(0, NB) as b:
                layer02_dve(2, b, e_fd, 4 * NB)

            with dve.Fori(0, NB) as b:
                norm_dve(norm(3, b, 0), b, 7, m_done, 8 * NB)
                cross_dve(3, b)
                out_dve(3, b, 0, biases(3, b, 0))

        @block.scalar
        def _(act):
            def copy(out, in_):
                return act.activation(out, in_, ACT.Copy)

            act.wait_ge(dve_prep, at(DVE_PREP, "cond_T"))
            act.activation(csT[:, :, :], condT[:, :, :], ACT.Silu).then_inc(act_prep, 1)

            def norm_act(n, b, ln):
                for hf in range(NH):
                    act.wait_ge(ln_tp, n * 2 + hf + 1)
                    settle(act)
                    act.activation(XT[:, 0, hf * HALF:(hf + 1) * HALF], PS[:, hf, :], ACT.Identity, bias=AB[:, ln, 0, 1, bass.ds(b, 1)],
                                   scale=AB[:, ln, 0, 0, bass.ds(b, 1)]).then_inc(ln_xt_a, 1)

            def parts_act(q0, steps, bias):
                for st in range(steps + 1):
                    if st < steps:
                        k = st
                        if bias is None:
                            act.wait_ge(qk_f, q0 + k + 1)
                        else:
                            act.wait_ge(qk_ps, q0 + k + 1)
                            if k >= 2:
                                act.wait_ge(qk_r, q0 + k - 1)
                            act.activation(FR[:, k % 2, :], PS[:, 4 + 2 * (k % 2), :], ACT.Identity, bias=bias[k // 2]).then_inc(qk_f, 1)
                            act.wait_ge(qk_f, q0 + k + 1)
                        copy(QKP[:, 0, k // 2, (k % 2) * HALF:(k % 2 + 1) * HALF], FR[:, k % 2, :]).then_inc(qk_h, 1)
                    if st >= 1:
                        k = st - 1
                        act.wait_ge(qk_r, q0 + k + 1)
                        copy(QKP[:, 1, k // 2, (k % 2) * HALF:(k % 2 + 1) * HALF], RR[:, k % 2, :]).then_inc(qk_m, 1)

            def self_act(l, b):
                s = selfs(l, b)
                parts_act(qsteps(l, b, 0), 8, None if l == 0 else [QB[:, a, m:m + 1] for m in range(KT) for a in range(2)])
                act.preload_act_table(ACT.Exp)

                def evacuate(g):
                    act.wait_ge(pv_done, (s * NG + g) * 8 + 8)
                    copy(OT[:, :].rearrange("p (a n) -> p a n", a=2), PS[:, 6:8, :]).then_inc(acc_out, 1)

                def body(g, peeled0=False):
                    for k in range(32):
                        kt, j = k // 4, k % 4
                        act.wait_ge(st_full, (s * NG + g) * 32 + k + 1)
                        if j == 0 and (kt >= 2 or not peeled0):
                            act.wait_ge(pv_done, (s * NG + g) * 8 + kt - 1)
                        act.activation(PR[:, kt % 2, j, :].rearrange("p (a n) -> p a n", a=2), PS[:, 2 + 2 * (k % 2):4 + 2 * (k % 2), :], ACT.Exp, scale=SCALE).then_inc(ex_done, 1)
                        if k == 1 and not peeled0:
                            evacuate(g - 1)

                body(0, True)
                with act.Fori(1, NG) as g:
                    body(g)
                evacuate(NG - 1)

            def out_act(l, b, i):
                o = outs(l, b, i)
                for hf in range(NH):
                    act.wait_ge(o_tp, o * 2 + hf + 1)
                    copy(XT[:, 0, hf * HALF:(hf + 1) * HALF], PS[:, hf, :]).then_inc(o_xt_a, 1)

            def cross_act(l, b):
                c = crosses(l, b)
                parts_act(qsteps(l, b, 0 if l == 3 else 1), 4, [0.0, 0.0] if l == 0 else [QB[:, 2 if l == 2 else 3, m:m + 1] for m in range(KT)])
                for h in range(H):
                    g = h // 4
                    act.wait_ge(c_st, c * H + h + 1)
                    if g >= 2 and h % 4 == 0:
                        act.wait_ge(c_pv, c * NG + g - 1)
                    act.activation(PR[:, g % 2, h % 4, :].rearrange("p (a n) -> p a n", a=2), PS[:, 2 + 2 * (h % 2):4 + 2 * (h % 2), :], ACT.Exp, scale=SCALE).then_inc(c_ex, 1)

            def mlp_act(l, b):
                m_ = mlps(l, b)
                for i in range(MT_ * NH):
                    m, hf = i // 2, i % 2
                    act.wait_ge(m_ps, m_ * 16 + i + 1)
                    act.activation(HT[:, m, hf * HALF:(hf + 1) * HALF], PS[:, 4 + i % 4, :], ACT.Gelu_apprx_tanh, bias=B1[:, 0 if l == 0 else 1, m:m + 1]).then_inc(m_h, 1)

            def layer02_act(l, b):
                norm_act(norm(l, b, 0), b, 0 if l == 0 else 4)
                self_act(l, b)
                out_act(l, b, 0)
                norm_act(norm(l, b, 1), b, 1 if l == 0 else 5)
                cross_act(l, b)
                out_act(l, b, 1)
                norm_act(norm(l, b, 2), b, 2 if l == 0 else 6)
                mlp_act(l, b)

            act.wait_ge(dve_prep, len(DVE_PREP))
            with act.Fori(0, NB) as b:
                layer02_act(0, b)

            act.wait_ge(e_prd, 4)

            def layer1_act(b):
                n = norm(1, b, 0)
                norm_act(n, b, 3)
                act.wait_ge(e_ve, b + 1)
                copy(VE[:, 0:1536].rearrange("p (a n) -> p a n", a=3), PS[0:NC, 4:7, :]).then_inc(e_vesb, 1)
                copy(VE[:, 1536:1536 + D + E3], PS[0:NC, 7, 0:D + E3]).then_inc(e_vesb, 1)
                act.wait_ge(e_mxs, b + 1)
                for t in range(NT):
                    act.activation(PX[:, t, 0:NC], PS[:, t // 4, (t % 4) * 80:(t % 4) * 80 + NC], ACT.Exp, bias=SR1[:, t:t + 1], scale=SCALE1,
                                   accum_out=SX1[:, t:t + 1]).then_inc(e_px, 1)
                act.wait_ge(e_pt, b + 1)
                copy(PT[0:NC, :].rearrange("p (a n) -> p a n", a=2), PS[0:NC, 2:4, :]).then_inc(e_ptsb, 1)
                act.wait_ge(e_r3, b + 1)
                act.activation(RP, RL, ACT.Exp).then_inc(e_rex, 1)
                for q in range(28):
                    r, hf = (q // 2, q % 2) if q < 4 else ((q - 4) % 8 // 2, q % 2)
                    e = (q - 4) // 8
                    dst = GT[:, r, hf * HALF:(hf + 1) * HALF] if q < 4 else HE[:, e % 2, r, hf * HALF:(hf + 1) * HALF]
                    m = 12 + r if q < 4 else e * RT + r
                    act.wait_ge(e_hps, b * 28 + q + 1)
                    if q == 4 + 16:
                        act.wait_ge(e_ops, b * 24 + NT)
                    settle(act)
                    act.activation(dst, PS[:, 4 + q % 4, :], ACT.Silu, bias=ANC[:, m, bass.ds(b, 1)]).then_inc(e_hsb, 1)
                for hf in range(NH):
                    act.wait_ge(e_rot, b * 2 + hf + 1)
                    copy(XT[:, 0, hf * HALF:(hf + 1) * HALF], PS[:, hf, :]).then_inc(e_rx_a, 1)
                for i in range(4):
                    act.wait_ge(e_fin, b * 4 + i + 1)
                    if i >= 2:
                        act.wait_ge(e_fd, b * 4 + i - 1)
                    act.activation(TG[:, i % 2, :], PS[:, 5 + (i % 2) * 2, :], ACT.Tanh, scale=0.5).then_inc(e_tg, 1)

            with act.Fori(0, NB) as b:
                layer1_act(b)
            act.wait_ge(v_one, 1)
            with act.Fori(0, NB) as b:
                layer02_act(2, b)
            with act.Fori(0, NB) as b:
                norm_act(norm(3, b, 0), b, 7)
                cross_act(3, b)
                out_act(3, b, 0)

        @block.gpsimd
        def _(pool):
            pool.wait_ge(const_in, 16)
            pool.tensor_copy(identb[:, :], ident[:, :])
            pool.tensor_scalar(bigI[:, :], ident[:, :], MASKED, 0.0, ALU.mult, ALU.add).then_inc(pool_prep, 1)
            pool.wait_ge(dve_prep, at(DVE_PREP, "mod_T"))
            pool.tensor_scalar(AKV[:, :, :], MODC[:, MODK // P:MODK // P + KT, :], 1.0, 0.0, ALU.add, ALU.add).then_inc(pool_prep, 1)
            pool.wait_ge(w_in[0], 4 * 16)
            for kt in range(KT):
                src = Wqkv[:, kt, 0:2 * D].rearrange("p (h a d) -> p h a d", a=2, d=HD // 2)
                dst = Wrot[:, kt, :].rearrange("p (h a d) -> p h a d", a=2, d=HD // 2)
                pool.tensor_scalar(dst[:, :, 0, :], src[:, :, 1, :], -1.0, 0.0, ALU.mult, ALU.add)
                last = pool.tensor_copy(dst[:, :, 1, :], src[:, :, 0, :])
            last.then_inc(pool_prep, 1)
            pool.wait_ge(pool_go, 1)
            for v, eps in enumerate((1e-6, 1e-5)):
                pool.tensor_scalar(CRS[:, v, :], CMV[:, :, 1], eps, 0.0, ALU.add, ALU.add).then_inc(pool_prep, 1)
            pool.wait_ge(pool_prep, 5)
            for v in range(2):
                pool.tensor_tensor(CRS[:, v, :], CRS[:, v, :], MHALF[0:NC, 0:NB], ALU.pow).then_inc(pool_prep, 1)
            pool.wait_ge(dve_prep, at(DVE_PREP, "mod_b"))
            pool.memset(BIG[:, 0:3072], 0.0)
            pool.memset(VCS, 0.0).then_inc(pool_prep, 1)
            pool.wait_ge(pool_prep, 8)
            pool.memset(VCS[0:NC, :, :, HD:HD + 1], 1.0).then_inc(pool_prep, 1)
            pool.wait_ge(pe_prep, at(PE_PREP, "ctx_T"))
            pool.memset(V[:, :, :, :], 0.0).then_inc(v_zero, 1)

            def norm_pool(n, ln):
                pool.wait_ge(ln_mv, n + 1)
                settle(pool)
                pool.tensor_scalar(NHLF[:, :], MV[:, :, 1], LN_EPS[ln], 0.0, ALU.add, ALU.add).then_inc(ln_ep, 1)
                pool.wait_ge(ln_ep, n + 1)
                settle(pool)
                pool.tensor_tensor(RS[:, :], NHLF[:, :], MHALF[:, :], ALU.pow).then_inc(ln_rs, 1)

            def add_bias(b, n, bias, done):
                pool.wait_ge(ln_norm, n * 8 + 8)
                settle(pool)
                x = X[:, bass.ts(b, NT), :]
                pool.tensor_tensor(x, x, bias[:, :].rearrange("p (a d) -> p a d", a=1).broadcast_to([P, NT, D]), ALU.add).then_inc(done, 1)

            def gate_weights(gi, w):
                pool.wait_ge(gate_in, (gi + 1) * 16)
                settle(pool)
                pool.tensor_tensor(WG[:, :, :], w, GATE[:, :].rearrange("p (a d) -> p a d", a=1).broadcast_to([P, KT, D]), ALU.mult).then_inc(wg_done, 1)

            def max_parts(src, rows, waits, base, first, p1, p2, p3, p4):
                pool.wait_ge(first, base + 1)
                settle(pool)
                pool.tensor_copy(NMB[0:rows, 0, :], src[0:rows, :]).then_inc(p1, 1)
                pool.wait_ge(p1, base + 1)
                settle(pool)
                pool.tensor_tensor(NMR[0:rows, :], src[0:rows, :], NMB[0:rows, 0, :], ALU.subtract).then_inc(p2, 1)
                pool.wait_ge(p2, base + 1)
                settle(pool)
                pool.tensor_copy(NMB[0:rows, 1, :], NMR[0:rows, :]).then_inc(p3, 1)
                pool.wait_ge(p3, base + 1)
                settle(pool)
                pool.tensor_tensor(NMB[0:rows, 2, :], NMR[0:rows, :], NMB[0:rows, 1, :], ALU.subtract).then_inc(p4, 1)

            def self_pool(l, b):
                s, n = selfs(l, b), norm(l, b, 0)
                gate_weights(gates(l, b, 0), Wo)
                if l == 2:
                    pool.wait_ge(bias_in, (biases(l, b, 0) + 1) * 16)
                    settle(pool)
                    pool.tensor_tensor(BIASB[:, :], BIASB[:, :], GATE[:, :], ALU.mult).then_inc(bg_done, 1)
                    pool.wait_ge(bg_done, b + 1)
                    add_bias(b, n, BIASB, biased)

                def group(g, peeled0=False):
                    if peeled0:
                        pool.wait_ge(v_sb, s * 4 + 4)
                    else:
                        pool.wait_ge(pv_done, (s * NG + g) * 8)
                    settle(pool)
                    pool.tensor_copy(VG[:, :, :, :].rearrange("p t j d -> p t (j d)"), V[:, :, bass.ds(g * HG, HG), :].rearrange("p t j d -> p t (j d)")).then_inc(vg_in, 1)

                max_parts(NMT, HG * NT, None, s * NG, nmt_sb, nm_p1, nm_p2, nm_p3, nm_p4)
                group(0, True)
                max_parts(NMT, HG * NT, None, s * NG + 1, nmt_sb, nm_p1, nm_p2, nm_p3, nm_p4)
                with pool.Fori(1, NG - 1) as g:
                    group(g)
                    max_parts(NMT, HG * NT, None, s * NG + g + 1, nmt_sb, nm_p1, nm_p2, nm_p3, nm_p4)
                group(NG - 1)

            def cross_pool(l, b):
                c, n = crosses(l, b), norm(l, b, 0 if l == 3 else 1)
                if l == 0:
                    gate_weights(gates(l, b, 1), Wco)
                else:
                    bi = biases(l, b, 0 if l == 3 else 1)
                    pool.wait_ge(bias_in, (bi + 1) * 16)
                    add_bias(b, n, BIASB, biased)
                max_parts(NMT, P, None, c, c_nmt, c_p1, c_p2, c_p3, c_p4)

            def mlp_pool(l, b):
                m_, n = mlps(l, b), norm(l, b, 2)
                pool.wait_ge(mg_in, (m_ + 1) * 32)
                settle(pool)
                pool.tensor_tensor(BIASM[:, :], BIASM[:, :], GATEM[:, :], ALU.mult).then_inc(m_bg, 1)
                pool.wait_ge(mw_in, (m_ + 1) * 32)
                settle(pool)
                pool.tensor_tensor(W2, W2, GATEM[:, :].rearrange("p (a d) -> p a d", a=1).broadcast_to([P, MT_, D]), ALU.mult).then_inc(m_w2g, 1)
                pool.wait_ge(m_bg, m_ + 1)
                add_bias(b, n, BIASM, m_biased)

            def layer02_pool(l, b):
                norm_pool(norm(l, b, 0), 0 if l == 0 else 4)
                self_pool(l, b)
                norm_pool(norm(l, b, 1), 1 if l == 0 else 5)
                cross_pool(l, b)
                norm_pool(norm(l, b, 2), 2 if l == 0 else 6)
                mlp_pool(l, b)

            pool.wait_ge(dve_prep, len(DVE_PREP))
            with pool.Fori(0, NB) as b:
                layer02_pool(0, b)
            with pool.Fori(0, NB) as b:
                norm_pool(norm(1, b, 0), 3)
            pool.wait_ge(e_fd, 4 * NB)
            pool.memset(V[:, :, :, :], 0.0).then_inc(v_zero, 1)
            pool.wait_ge(w_in[2], 5 * 16)
            with pool.Fori(0, NB) as b:
                layer02_pool(2, b)
            with pool.Fori(0, NB) as b:
                norm_pool(norm(3, b, 0), 7)
                cross_pool(3, b)




def kernel(**inputs):
    import ml_dtypes
    import concourse.bacc as _bacc
    from concourse.bass_utils import run_bass_kernel_spmd as _run

    nc = _bacc.Bacc("TRN2", target_bir_lowering=False, num_devices=1)
    arrays = {}
    for name, a in inputs.items():
        a = np.ascontiguousarray(a)
        if name == "mask_BxS2_bf1":
            name = "cross_mask"
        if name == "mask_SxS_bk0":
            name = "self_mask"
        arrays[name] = a
    arrays["ident"] = np.eye(P, dtype=np.float32)
    inv = 1.0 / 10000.0 ** (np.arange(0, HD, 2, dtype=np.float32) / HD)
    freqs = np.outer(np.arange(ROPE_N, dtype=np.float32), inv)
    emb = np.concatenate([freqs, freqs], axis=-1).T
    arrays["cos"] = np.ascontiguousarray(np.tile(np.cos(emb), (P // HD, 1)), np.float32)
    arrays["sin"] = np.ascontiguousarray(np.tile(np.sin(emb), (P // HD, 1)), np.float32)
    ones = np.ones((4, H * SEQ), ml_dtypes.bfloat16)
    arrays["q_rows"] = ones
    krows = ones.copy()
    krows[0] = 0
    arrays["k_rows"] = krows
    io = {n: nc.dram_tensor(f"in_{n}", a.shape, mybir.dt.from_np(a.dtype), kind="ExternalInput").ap() for n, a in arrays.items()}
    io["y"] = nc.dram_tensor("out_y", (NB, SEQ, D), F32, kind="ExternalOutput").ap()
    pixart_kernel(nc, io)
    r = _run(nc, [{f"in_{n}": a for n, a in arrays.items()}], core_ids=[0])
    return r.results[0]["out_y"]
```

```python
from contextlib import ExitStack

import numpy as np
import concourse.bass as bass
from concourse import mybir

F32 = mybir.dt.float32
BF16 = mybir.dt.bfloat16
FP8 = mybir.dt.float8e4
U8 = mybir.dt.uint8
ALU = mybir.AluOpType
ACT = mybir.ActivationFunctionType
AX = mybir.AxisListType

P = 128
NB, SEQ, D = 4, 1024, 256
NT = SEQ // P
KT = D // P
H, HD = 16, 16
HG = 4
NG = H // HG
HALF = 512
NH = SEQ // HALF
NC = 77
CTX = NB * NC
MLP = 4 * D
MT_ = MLP // P
E3, RH = 3, 512
RT = RH // P
ROPE_N = SEQ // 2
SCALE = 1.0 / float(np.sqrt(HD))
SCALE1 = float(D) ** -0.5
Q_PARTS = [0, 0, 0, 1, 1, 2]
K_PARTS = [0, 1, 2, 0, 1, 0]
MASK_ROW = len(Q_PARTS) * HD
MAX_ROW = MASK_ROW + 1
ROWS = MAX_ROW + 3
LIVE = 2
LIVE_W = NT // LIVE
PACE, PACE_FEW = 0.76, 0.7
MASKED = -float(2 ** 100)

MOD0, MOD2, MODQ, MODK = 0, 9 * D, 15 * D, 17 * D
MODN = 19 * D
LN_EPS = [1e-5, 1e-5, 1e-5, 1e-5, 1e-6, 1e-6, 1e-6, 1e-5]

POOL_IDENT, POOL_AKV, POOL_WROT, POOL_CTX, POOL_ZERO = 1, 2, 3, 7, 9
MASK_TILES = [f"mask_{t}" for t in range(NT)]
PE_PREP = ["cond_T"] + MASK_TILES + ["few_sum", "mod_a", "mod_b", "mod_T", "ctx_T", "kc", "l1_kv", "wq_T", "l1_a", "vc_0", "vc_1", "vc_2"]
DVE_PREP = (["zeros", "cond_T"] + [m for t in range(NT) for m in (f"mask_bf_{t}", f"mask_{t}")]
            + ["few_rows", "few", "mod_a", "mod_b", "mod_T", "ab", "ctx_stats", "ctx_rows", "ctx_T", "kc", "kc_high", "kc_rest", "kc_middle", "kc_parts",
               "l1_kv", "wq_T", "l1_a", "vc_0", "vc_1", "vc_2", "mask_row_f", "mask_row", "v_ones"])


def pixart_kernel(nc, io):
    ctx = ExitStack()
    with ctx:
        ctx.enter_context(nc.allow_non_contiguous_dma(reason="vectors by feature, a few hundred elements each"))

        def sb(name, shape, dt=F32):
            return ctx.enter_context(nc.sbuf_tensor(name, shape, dt))

        def sem(name):
            return ctx.enter_context(nc.semaphore(name))

        X = sb("x_tok", [P, NB * NT, D])
        XN = sb("xn_tok", [P, NT, D])
        XT = sb("x_T", [P, KT, SEQ])
        BIG = sb("big", [P, 16384])
        PR = sb("probs", [P, 2, HG, SEQ])
        V = sb("v_self", [P, NT, H, 32])
        W = sb("weights", [P, 4096])
        MM = sb("mask_T", [P, NT, SEQ], FP8)
        VG = sb("v_group", [P, NT, HG, 32])
        OT = sb("o_T", [P, SEQ])
        WG = sb("w_gated", [P, KT, D])
        GATE = sb("gate_bc", [P, D])
        BIASB = sb("bias_bc", [P, D])
        BV = sb("bias_v_bc", [P, D])
        NHLF = sb("eps_tile", [P, NT])
        ident = sb("ident", [P, P])
        identb = sb("ident_b", [P, P], BF16)
        bigI = sb("ident_masked", [P, P], BF16)
        MODC = sb("mod_cols", [P, MODN // P, NB])
        AB = sb("ln_affine", [P, 8, KT, 2, NB])
        LNW = sb("ln_weights", [P, 5, KT])
        QB = sb("q_bias", [P, 8, KT])
        B1 = sb("mlp_b1", [P, 2, MT_])
        ST = sb("bn_stats", [P, NT, 6])
        MV = sb("mean_var", [P, NT, 2])
        RS = sb("rstd", [P, NT])
        MHALF = sb("minus_half", [P, NT])
        NMP = sb("max_halves", [P, HG, NT, NH])
        NM = sb("row_max", [P, H, NT])
        NMT = sb("row_max_T", [P, P])
        NMR = sb("row_max_rest", [P, P])
        NMB = sb("row_max_parts", [P, 3, P], BF16)
        REC = sb("recip", [P, NT, HG])
        condT = sb("cond_T", [P, KT, NB])
        csT = sb("silu_cond_T", [P, KT, NB])
        A1 = sb("l1_scores_w", [P, KT, NB, NC + E3])
        V1T = sb("l1_v_T", [P, KT, NB, NC])
        NMK = sb("ring_marks", [P, 2])
        AKV = sb("l3_kv_scale", [P, KT, NB])
        NMG = sb("group_max", [P, HG * NT])
        CST = sb("ctx_stats", [NC, NB, 6])
        CMV = sb("ctx_mean_var", [NC, NB, 2])
        MARK = sb("settled", [P, 136], BF16)
        CRS = sb("ctx_rstd", [NC, 2, NB])
        PS = ctx.enter_context(nc.psum_tensor("ps", [P, 8, HALF], F32))
        PSB = PS[:, :, :].bitcast(BF16)

        bigb = BIG[:, :].bitcast(BF16)
        QS = bigb[:, 0:16384].rearrange("p (h n) -> p h n", h=H)
        KS = bigb[:, 16384:32768].rearrange("p (h n) -> p h n", h=H)
        HT = BIG[:, 0:8192].rearrange("p (m n) -> p m n", m=MT_)
        W1 = BIG[:, 8192:10240].rearrange("p (k m) -> p k m", k=KT)
        W2 = BIG[:, 10240:12288].rearrange("p (k m) -> p k m", k=MT_)
        GATEM, BIASM = BIG[:, 12288:12544], BIG[:, 12544:12800]
        KC = BIG[:, 12800:13824].bitcast(BF16)[0:ROWS].rearrange("p (h n) -> p h n", h=H)
        VC = BIG[:, 13824:14336].rearrange("p (h d) -> p h d", h=H)
        prf = PR[:, :, :, :].rearrange("p a b c -> p (a b c)")
        QKP = prf[:, 0:6144].bitcast(BF16).rearrange("p (a t n) -> p a t n", a=3, t=4)
        FR = prf[:, 6144:7168].rearrange("p (a n) -> p a n", a=2)
        RR = prf[:, 7168:8192].rearrange("p (a n) -> p a n", a=2)
        T12 = OT[:, :].rearrange("p (a n) -> p a n", a=2)
        Wqkv = W[:, 0:1536].rearrange("p (k m) -> p k m", k=KT)
        Wrot = W[:, 1536:2560].rearrange("p (k m) -> p k m", k=KT)
        Wo = W[:, 2560:3072].rearrange("p (k m) -> p k m", k=KT)
        Wcq = W[:, 3072:3584].rearrange("p (k m) -> p k m", k=KT)
        Wco = W[:, 3584:4096].rearrange("p (k m) -> p k m", k=KT)
        xnf = XN[:, :, :].rearrange("p a b -> p (a b)")
        COS, SIN = xnf[:, 0:ROPE_N], xnf[:, ROPE_N:2 * ROPE_N]

        MWB = BIG[:, 0:KT * MODN].rearrange("p (k m) -> p k m", k=KT)
        MBIAS = BIG[0:NB, 9728:9728 + MODN]
        MROW = prf[0:NB, 0:MODN]
        KCW = prf[:, 4864:4864 + 3072].rearrange("p (l k m) -> p l k m", l=3, k=KT)
        vf = V[:, :, :, :].rearrange("p a b c -> p (a b c)")
        BV3 = prf[:, 7936:8192]
        CTK = vf[0:NC, 0:3072].rearrange("p (v b m) -> p v b m", v=3, b=NB)
        condR = vf[0:NB, 3072:3072 + D]
        CXT = xnf[:, 0:3 * KT * CTX].rearrange("p (v k n) -> p v k n", v=3, k=KT)
        xtf = XT[:, :, :].rearrange("p a b -> p (a b)")
        W1K = xtf[:, 0:512].rearrange("p (k m) -> p k m", k=KT)
        W1V = xtf[:, 512:1024].rearrange("p (k m) -> p k m", k=KT)
        W1Q = xtf[:, 1024:1536].rearrange("p (k m) -> p k m", k=KT)
        W1QT = xtf[:, 1536:2048].rearrange("p (k m) -> p k m", k=KT)
        KCF = BIG[:, 0:3072].rearrange("p (l k b n) -> p l k b n", l=3, k=KT, b=NB)
        KCR = BIG[:, 3072:6144].rearrange("p (l k b n) -> p l k b n", l=3, k=KT, b=NB)
        KCP = BIG[:, 6144:10752].bitcast(BF16).rearrange("p (a l k b n) -> p a l k b n", a=3, l=3, k=KT, b=NB)
        VCS = BIG[:, 10752:12800].rearrange("p (b h d) -> p b h d", b=NB, h=H)
        K1T = OT[:, 0:KT * CTX].rearrange("p (k n) -> p k n", k=KT)
        MKB = WG[:, :, :].rearrange("p a b -> p (a b)").bitcast(BF16)[:, 0:SEQ]
        MKU = xnf.bitcast(U8).rearrange("p (t n) -> p t n", t=NT)
        MRU = GATE[0:NB, 0:32].bitcast(U8)[:, 0:NC]
        MRF = BIASB[0:NB, 0:P]
        MRB = NMR[0:NB, 0:64].bitcast(BF16)
        MRZ = NMT[0:NB, 0:64].bitcast(BF16)

        FEW_T, FEW_D, FEW_Q = NMP[:, 0], NMP[:, 1, :, 0], NMP[:, 2, 0, 0:1]
        FEW = NMP[0:1, 3, 0, 0:1].bitcast(mybir.dt.int32)

        HE = BIG[:, 0:8192].rearrange("p (a r n) -> p a r n", a=2, r=RT)
        GT = BIG[:, 8192:10240].rearrange("p (r n) -> p r n", r=KT)
        ROU = BIG[:, 10240:12288].rearrange("p (t m) -> p t m", t=NT)
        PX = BIG[:, 12288:12288 + 640].rearrange("p (t n) -> p t n", t=NT)
        PT = BIG[:, 12928:13952]
        TG = BIG[:, 13952:14976].rearrange("p (a n) -> p a n", a=2)
        YG = BIG[:, 14976:16000].rearrange("p (a n) -> p a n", a=2)
        EW1 = prf[:, 0:6144].rearrange("p (k e m) -> p k e m", k=4, e=E3)
        GW1 = prf[:, 6144:7680].rearrange("p (k m) -> p k m", k=6)
        EW1A = vf[:, 0:3072].rearrange("p (k e m) -> p k e m", k=KT, e=E3)
        EW2 = W[:, 0:3072].rearrange("p (k m) -> p k m", k=E3 * RT)
        GW2 = W[:, 3072:3584].rearrange("p (k m) -> p k m", k=KT)
        OW = W[:, 3584:4096].rearrange("p (k m) -> p k m", k=KT)
        VE = vf[0:NC, 0:1796]
        mmf = MM[:, :, :].rearrange("p a b -> p (a b)").bitcast(F32)
        V1B = mmf[:, 0:KT * NC].rearrange("p (k n) -> p k n", k=KT)
        ANC = mmf[:, 160:160 + 14 * NB].rearrange("p (m b) -> p m b", m=14)
        ANB = mmf[:, 224:238]
        RWT = mmf[:, 240:240 + 6 * E3].rearrange("p (k e) -> p k e", k=6)
        RB = mmf[:, 260:263]
        RAC = mmf[:, 264:264 + NB * E3].rearrange("p (b e) -> p b e", b=NB)
        RL = mmf[:, 280:280 + NT * E3].rearrange("p (t e) -> p t e", t=NT)
        RM = mmf[:, 304:304 + NT]
        RP = mmf[:, 312:312 + NT * E3].rearrange("p (t e) -> p t e", t=NT)
        NX1 = mmf[:, 336:336 + NT]
        SX1 = mmf[:, 344:344 + NT]
        SR1 = mmf[:, 352:352 + NT]
        B2T = mmf[:, 360:360 + KT * E3].rearrange("p (k e) -> p k e", k=KT)
        B2O = mmf[0:E3, 368:368 + D]
        OBB = mmf[0:E3, 624:624 + D]
        GB2 = mmf[0:1, 880:880 + D]
        ONE = mmf[0:1, 1136:1136 + P]
        PTR = OT[0:E3, :]

        QKd = nc.dram_tensor("qk_parts", [3, 2 * D, SEQ], BF16, kind="Internal").ap()
        KCd = nc.dram_tensor("kc_parts", [3, 3, D, NB * P], BF16, kind="Internal").ap()
        VCd = nc.dram_tensor("vc_rows", [3, NB, P, H * 32], F32, kind="Internal").ap()
        MODd = nc.dram_tensor("mod_rows", [NB, MODN], F32, kind="Internal").ap()
        MKd = nc.dram_tensor("mask_rows", [2, NB, P], BF16, kind="Internal").ap()

        def sems(prefix, names):
            return [sem(prefix + n) for n in names.split()]

        x_in, cond_in, modw_in, ctx_in, l1w_in, const_in, small_in = sems("", "x_in cond_in mod_w_in ctx_in l1_w_in const_in small_in")
        mask_in = sems("mask_in_", "first second")
        maskrow_in, kc_out, vc_out, mod_out, mrow_out = sems("", "mask_row_in kc_out vc_out mod_out mask_row_out")
        pe_prep, dve_prep, pool_prep, act_prep, pool_go = sems("", "pe_prep dve_prep pool_prep act_prep ctx_mean_var")
        w_in = [sem(f"w_in{l}") for l in range(4)]
        ln_st, ln_mv, ln_ep, ln_rs, ln_norm, ln_tp, ln_xt_a, ln_xt_d = sems("ln_", "stats mean_var eps rstd rows turned xT_act xT_dve")
        qk_ps, qk_t, qk_f, qk_h, qk_r, qk_m, qk_l, qk_out, cq_out = sems("qk_", "ps products full high rest middle low out cross_out")
        cs_in, krow_in, cst_a, cst_b = sems("", "cos_sin_in const_rows_in cross_stack0_in cross_stack1_in")
        stack_in = [sem(f"stack_in{g}") for g in range(NG)]
        v_ps, v_sb, vg_in, ring_full, ring_free = sems("", "v_ps v_rows v_group_in ring_full ring_free")
        nm_done, nmt_sb, nm_p1, nm_p2, nm_p3, nm_p4, nm_in = sems("nm_", "done turned high rest middle low in")
        st_full, ex_done, pv_done, acc_out, rec_done, at_done = sems("", "scores_T_full exp_done pv_done acc_out recip_done att_rows")
        c_full, c_free, c_nmT, c_nmt, c_p1, c_p2, c_p3, c_p4, c_nm_in = sems("c_", "max_full max_free nm_turned nm_sb nm_high nm_rest nm_middle nm_low nm_in")
        c_st, c_ex, c_pv, c_acc, c_tp, c_rec, c_at, kc_in = sems("c_", "scores_full exp_done pv_done acc_out turned recip att_rows kc_in")
        o_tp, o_xt_a, o_xt_d, o_ps, o_done = sems("o_", "turned xT_act xT_dve ps added")
        gate_in, bias_in, wg_done, bg_done, biased = sems("", "gate_in bias_in w_gated bias_gated biased")
        mg_in, mw_in, m_ps, m_h, m_ops, m_done, m_w2g, m_bg, m_biased = sems("m_", "gate_in w_in ps hidden out_ps added w2_gated bias_gated biased")
        v_zero, v_one, few_own = sems("", "v_zeroed v_ones few_differences")
        (e_v1b, e_ve, e_vesb, e_sc, e_mx, e_mxs, e_rl, e_px, e_sr, e_pxn, e_pt, e_ptsb, e_rt, e_r1, e_r2, e_r3, e_rex, e_r4, e_r5, e_rp, e_rpt, e_rptsb, e_hps, e_hsb, e_ops,
         e_ho, e_rot, e_rx_a, e_rx_d, e_fin, e_tg, e_yg, e_fd, e_pro, e_prd) = sems(
            "e_", "v_batch ve_ps ve_sb scores max max_scaled logits exp recip probs_n turned turned_sb router r_sum r_max r_shift r_exp r_den r_recip r_probs r_turned r_turned_sb "
            "hidden_ps hidden out_ps mixed mix_turned mixT_act mixT_dve fin_ps tanh gated added anchors_ps anchors")
        y_out = sem("y_out")

        mod_chunks = [(a, min(a + HALF, z)) for lo, z in ((MOD0, MOD2), (MOD2, MODQ), (MODQ, MODK), (MODK, MODN)) for a in range(lo, z, HALF)]

        places = [0, 0, 0]

        def settle(eng):
            e = 2 if eng is nc.scalar else 1 if eng is nc.vector else 0
            own, one = MARK[32 * e:32 * e + 1, places[e]:places[e] + 1], ident[32 * e:32 * e + 1, 0:1]
            places[e] += 1
            if eng is nc.scalar:
                eng.activation(own, one, ACT.Copy)
            elif eng is nc.vector:
                eng.memset(own, 0.0)
            else:
                eng.tensor_tensor(own, one, one, ALU.add)

        def at(names, name):
            return names.index(name) + 1

        def colview(ap):
            return ap.rearrange("(c p) -> p c", p=P)

        def rowsview(ap):
            return ap.rearrange("(k p) m -> p k m", p=P)

        def bcast(ap, n=P):
            return ap.rearrange("(a m) -> a m", a=1).broadcast_to([n, ap.shape[0]])

        block = ctx.enter_context(nc.Block())
        L = ["L0_xcond_", "L1_xcond_", "L2_xcond_", "L3_xcond_"]
        L0, L1, L2, L3 = L

        def norm(l, b, i):
            return {0: 3 * b, 1: b + 12, 2: 3 * b + 16, 3: b + 28}[l] + i

        def selfs(l, b):
            return {0: b, 2: b + 4}[l]

        def crosses(l, b):
            return {0: b, 2: b + 4, 3: b + 8}[l]

        def outs(l, b, i):
            return {0: 2 * b, 2: 2 * b + 8, 3: b + 16}[l] + i

        def qsteps(l, b, i):
            return {0: 12 * b, 2: 12 * b + 48, 3: 4 * b + 96}[l] + 8 * i

        def krows(l, b, i):
            return 24 + b + 1 if l == 3 else {0: 0, 2: 12}[l] + 3 * b + 2 + i

        def mlps(l, b):
            return {0: b, 2: b + 4}[l]

        def gates(l, b, i):
            return {0: 2 * b, 2: b + 8}[l] + i

        def biases(l, b, i):
            return {2: 2 * b, 3: b + 8}[l] + i

        def key_tiles(few):
            return list(range(NT - LIVE, NT)) if few else list(range(NT))

        def weight(few):
            return LIVE_W if few else 1

        def max_uses(few):
            if few:
                return [("max", j, 2 * i, None) for j in range(HG) for i in range(NT // 2)]
            return [("max", j, qt, hf) for j in range(HG) for qt in range(NT) for hf in range(NH)]

        def ring_order(few, with_max, with_tail):
            units = max_uses(few) if with_max else []
            at = min(len(units), 3 if few else 8)
            return units[:at] + ([("tail",)] if with_tail else []) + units[at:] + ([("nm",)] if with_max else [])

        class Pace:

            def __init__(self, few, with_max, with_tail):
                self.order, self.done, self.work = ring_order(few, with_max, with_tail), 0, 0
                cost = [4 if op[0] == "tail" else 1 for op in self.order]
                self.before = [sum(cost[:i + 1]) / sum(cost) if cost[i] == 1 else sum(cost[:i]) / sum(cost) for i in range(len(cost))]
                scores, pv = len(key_tiles(few)) * HG * NH * (2 if few else 1), len(key_tiles(few)) * NH * 4
                self.until = (scores + pv) * (PACE_FEW if few else PACE)
                self.evacuated = 2 * NH * (2 if few else 1)

            def due(self, work):
                self.work += work
                upto = self.done
                while upto < len(self.order) and self.before[upto] <= self.work / self.until + 1e-9 and (self.order[upto][0] != "tail" or self.work > self.evacuated):
                    upto += 1
                ops, self.done = self.order[self.done:upto], upto
                return ops

        class Ring:

            def __init__(self, start, few, banks=2):
                self.start, self.few, self.banks, self.used, self.n, self.back = start, few, banks, 0, 0, 1

            def count(self):
                return self.start + self.used

            def bank(self):
                return self.n % self.banks

            def use(self, op):
                if op[0] == "max":
                    self.used += weight(self.few)
                    self.n += 1
                    self.back = weight(self.few) * (self.banks - 1)
                else:
                    self.used += 2
                    self.back = 1

        PRO_BANKS = 4
        MAXN = HG * NT * NH
        PRO = MAXN + 2
        BODY = MAXN + 2 + 2
        RINGN = PRO + (BODY - 2) + 2 * BODY + 2 + 2

        def ring_at(s, g):
            if isinstance(g, int) and g == 0:
                return s * RINGN + PRO
            return s * RINGN + PRO + (BODY - 2) + (g - 1) * BODY

        @block.sync
        def _(sp):
            sp.dma_start(condR, io["cond_1024"]).then_inc(cond_in, 16)
            sp.dma_start(ident[:, :], io["ident"]).then_inc(const_in, 16)
            for t in range(0, NT, 4):
                sp.dma_start(MKU[:, t:t + 4, :], io["self_mask"][t * P:(t + 4) * P, :].rearrange("(t p) k -> p t k", p=P)).then_inc(mask_in[t // 4], 16)
            sp.dma_start(MWB[:, :, MOD0:MOD2], rowsview(io[L0 + "adaLN_W"])).then_inc(modw_in, 16)
            sp.dma_start(MWB[:, :, MOD2:MODQ], rowsview(io[L2 + "W_mod"])).then_inc(modw_in, 16)
            sp.dma_start(MWB[:, :, MODQ:MODK], rowsview(io[L3 + "Wss_q"])).then_inc(modw_in, 16)
            sp.dma_start(MWB[:, :, MODK:MODN], rowsview(io[L3 + "Wss_kv"])).then_inc(modw_in, 16)
            for a, z, n in ((MOD0, MOD2, L0 + "adaLN_b"), (MOD2, MODQ, L2 + "b_mod"), (MODQ, MODK, L3 + "bss_q"), (MODK, MODN, L3 + "bss_kv")):
                sp.dma_start(MBIAS[:, a:z], bcast(io[n], NB)).then_inc(modw_in, 16)
            sp.dma_start(CTK[:, 0], io["ctx_1024"].rearrange("b s d -> s b d")).then_inc(ctx_in, 16)
            for i, n in enumerate((L0 + "norm1_w", L0 + "normc_w", L0 + "norm2_w", L1 + "ln_gamma", L1 + "ln_beta")):
                sp.dma_start(LNW[:, i, :], colview(io[n])).then_inc(small_in, 16)
            for i, ap in enumerate((io[L2 + "b_qkv"][0:D], io[L2 + "b_qkv"][D:2 * D], io[L2 + "b_qc"], io[L3 + "bq"], io[L2 + "b_kvc"][0:D], io[L3 + "bkv"][0:D])):
                sp.dma_start(QB[:, i, :], colview(ap)).then_inc(small_in, 16)
            sp.dma_start(B1[:, 0, :], colview(io[L0 + "mlp_b1"])).then_inc(small_in, 16)
            sp.dma_start(B1[:, 1, :], colview(io[L2 + "b_mlp1"])).then_inc(small_in, 16)
            sp.dma_start(BV[:, :], bcast(io[L2 + "b_kvc"][D:2 * D])).then_inc(small_in, 16)
            sp.dma_start(BV3, bcast(io[L3 + "bkv"][D:2 * D])).then_inc(small_in, 16)
            sp.dma_start(MRU, io["cross_mask"]).then_inc(maskrow_in, 16)
            sp.dma_start(KCW[:, 0, :, 0:D], rowsview(io[L0 + "ck_W"])).then_inc(ctx_in, 16)
            sp.dma_start(KCW[:, 0, :, D:2 * D], rowsview(io[L0 + "cv_W"])).then_inc(ctx_in, 16)
            sp.dma_start(KCW[:, 1], rowsview(io[L2 + "W_kvc"])).then_inc(ctx_in, 16)
            sp.dma_start(KCW[:, 2], rowsview(io[L3 + "Wkv"])).then_inc(ctx_in, 16)
            for w, n in ((W1K, "Wk"), (W1V, "Wv"), (W1Q, "Wq")):
                sp.dma_start(w, rowsview(io[L1 + n])).then_inc(l1w_in, 16)
            for b in range(NB):
                sp.dma_start(A1[:, :, b, NC:NC + E3], rowsview(io[L1 + "router_W"][0:D, :])).then_inc(l1w_in, 16)
            for b in range(NB):
                sp.dma_start(X[:, b * NT:(b + 1) * NT, :], io["x"][b].rearrange("(t p) d -> p t d", p=P)).then_inc(x_in, 16)
            sp.dma_start(Wqkv, rowsview(io[L0 + "qkv_W"])).then_inc(w_in[0], 16)
            for w, n in ((Wo, "attn_out_W"), (Wcq, "cq_W"), (Wco, "co_W")):
                sp.dma_start(w, rowsview(io[L0 + n])).then_inc(w_in[0], 16)
            sp.wait_ge(dve_prep, at(DVE_PREP, "mod_b"))
            sp.dma_start(MODd, MROW).then_inc(mod_out, 16)
            sp.wait_ge(dve_prep, at(DVE_PREP, "kc_parts"))
            for a in range(3):
                for l in range(3):
                    sp.dma_start(KCd[a, l].rearrange("(k p) n -> p k n", p=P), KCP[:, a, l].rearrange("p k b n -> p k (b n)")).then_inc(kc_out, 16)
            for l in range(3):
                sp.wait_ge(dve_prep, at(DVE_PREP, f"vc_{l}"))
                sp.dma_start(VCd[l].rearrange("b p n -> p b n"), VCS.rearrange("p b h d -> p b (h d)")).then_inc(vc_out, 16)
            sp.wait_ge(dve_prep, at(DVE_PREP, "mask_row"))
            sp.dma_start(MKd[0], MRB).then_inc(mrow_out, 16)
            sp.dma_start(MKd[1], MRZ).then_inc(mrow_out, 16)
            sp.wait_ge(mod_out, 16)
            sp.wait_ge(kc_out, 9 * 16)
            sp.wait_ge(vc_out, 3 * 16)
            sp.wait_ge(mrow_out, 2 * 16)
            sp.wait_ge(pe_prep, len(PE_PREP))
            sp.wait_ge(dve_prep, len(DVE_PREP))

            def load_gate(l, b, chunk, dst, done):
                base = {0: MOD0, 2: MOD2}[l]
                sp.dma_start(dst[:, :], MODd[bass.ds(b, 1), base + chunk * D:base + (chunk + 1) * D].broadcast_to([P, D])).then_inc(done, 16)

            def self_dma(l, b):
                s, n = selfs(l, b), norm(l, b, 0)
                sp.wait_ge(ln_tp, 2 * n + 2)
                if l == 0:
                    sp.dma_start(COS, io["cos"]).then_inc(cs_in, 16)
                    sp.dma_start(SIN, io["sin"]).then_inc(cs_in, 16)
                load_gate(l, b, 2, GATE, gate_in)
                if l == 2:
                    sp.dma_start(BIASB[:, :], bcast(io[L2 + "b_proj"])).then_inc(bias_in, 16)
                sp.dma_start(QS[MASK_ROW:ROWS], io["q_rows"].rearrange("r (h n) -> r h n", h=H)).then_inc(krow_in, 16)
                sp.dma_start(KS[MASK_ROW:ROWS], io["k_rows"].rearrange("r (h n) -> r h n", h=H)).then_inc(krow_in, 16)
                for tile in range(4):
                    sp.wait_ge(qk_l, qsteps(l, b, 0) + 2 * tile + 2)
                    sp.dma_start(QKd[:, tile * P:(tile + 1) * P, :].rearrange("a p n -> p a n"), QKP[:, :, tile, :]).then_inc(qk_out, 16)
                    if tile % 2 == 0:
                        continue
                    sp.wait_ge(qk_out, s * 64 + 16 * tile + 16)
                    for g in (tile - 1, tile):
                        for r in range(6):
                            for st, part, f0 in ((QS, Q_PARTS[r], (tile - 1) * P), (KS, K_PARTS[r], tile * P)):
                                src = QKd[part, f0 + (g % 2) * 64:f0 + (g % 2) * 64 + 64, :].rearrange("(h d) n -> d h n", d=HD)
                                sp.dma_start(st[r * HD:(r + 1) * HD, g * HG:(g + 1) * HG, :], src).then_inc(stack_in[g], 16)
                for g in range(NG):
                    sp.wait_ge(nm_p4, s * NG + g + 1)
                    for a in range(3):
                        sp.dma_start(QS[MAX_ROW + a:MAX_ROW + a + 1, g * HG:(g + 1) * HG, :].rearrange("p h (t n) -> p (h t) n", n=P),
                                     NMB[0:HG * NT, a, :]).then_inc(nm_in, 16)

            def cross_dma(l, b):
                c, n = crosses(l, b), norm(l, b, 0 if l == 3 else 1)
                li = {0: 0, 2: 1, 3: 2}[l]
                sp.wait_ge(ln_tp, 2 * n + 2)
                if l == 0:
                    load_gate(l, b, 5, GATE, gate_in)
                else:
                    sp.dma_start(BIASB[:, :], bcast(io[L2 + "b_cproj"] if l == 2 else io[L3 + "bp"])).then_inc(bias_in, 16)
                sp.dma_start(QS[MASK_ROW:ROWS], io["q_rows"].rearrange("r (h n) -> r h n", h=H)).then_inc(krow_in, 16)
                for r in range(6):
                    sp.dma_start(KC[r * HD:(r + 1) * HD, :, :], KCd[K_PARTS[r], li][:, bass.ts(b, P)].rearrange("(h d) n -> d h n", d=HD)).then_inc(kc_in, 16)
                sp.dma_start(KC[MASK_ROW:MASK_ROW + 1, :, :], MKd[0 if l == 0 else 1, bass.ds(b, 1), :].rearrange("a (c n) -> a c n", c=1).broadcast_to([1, H, P])).then_inc(kc_in, 16)
                sp.dma_start(KC[MAX_ROW:ROWS, :, :], io["k_rows"][1:4, 0:H * P].rearrange("r (h n) -> r h n", h=H)).then_inc(kc_in, 16)
                sp.dma_start(VC[:, :, :], VCd[li, bass.ds(b, 1)].rearrange("a p (h d) -> p (a h) d", h=H)).then_inc(kc_in, 16)
                if l != 3:
                    load_gate(l, b, 8 if l == 0 else 5, GATEM, mg_in)
                    sp.dma_start(BIASM[:, :], bcast(io[L[l] + ("mlp_b2" if l == 0 else "b_mlp2")])).then_inc(mg_in, 16)
                    sp.dma_start(W1, rowsview(io[L[l] + ("mlp_W1" if l == 0 else "W_mlp1")])).then_inc(mw_in, 16)
                    sp.dma_start(W2, rowsview(io[L[l] + ("mlp_W2" if l == 0 else "W_mlp2")])).then_inc(mw_in, 16)
                for ft in range(KT):
                    sp.wait_ge(qk_l, qsteps(l, b, 0 if l == 3 else 1) + 2 * ft + 2)
                    sp.dma_start(QKd[:, ft * P:(ft + 1) * P, :].rearrange("a p n -> p a n"), QKP[:, :, ft, :]).then_inc(cq_out, 16)
                    sp.wait_ge(cq_out, c * 32 + 16 * ft + 16)
                    for r in range(6):
                        src = QKd[Q_PARTS[r], ft * P:(ft + 1) * P, :].rearrange("(h d) n -> d h n", d=HD)
                        sp.dma_start(QS[r * HD:(r + 1) * HD, ft * 8:ft * 8 + 8, :], src).then_inc((cst_a, cst_b)[ft], 16)
                sp.wait_ge(c_p4, c + 1)
                for a in range(3):
                    sp.dma_start(QS[MAX_ROW + a:MAX_ROW + a + 1, :, :].rearrange("p h (t n) -> p (h t) n", n=P), NMB[:, a, :]).then_inc(c_nm_in, 16)

            with sp.Fori(0, NB) as b:
                self_dma(0, b)
                cross_dma(0, b)

            sp.wait_ge(m_done, 4 * NB)
            for e in range(E3):
                sp.dma_start(EW1[:, :, e, :], rowsview(io[L1 + "e_w1"][e, 0:4 * P, :])).then_inc(w_in[1], 16)
                sp.dma_start(EW1A[:, :, e, :], rowsview(io[L1 + "e_w1"][e, 4 * P:6 * P, :])).then_inc(w_in[1], 16)
                sp.dma_start(EW2[:, e * RT:(e + 1) * RT, :], rowsview(io[L1 + "e_w2"][e])).then_inc(w_in[1], 16)
                sp.dma_start(ANB[:, e * RT:(e + 1) * RT], colview(io[L1 + "e_b1"][e])).then_inc(w_in[1], 16)
                sp.dma_start(B2T[:, :, e], colview(io[L1 + "e_b2"][e])).then_inc(w_in[1], 16)
            sp.dma_start(GW1, rowsview(io[L1 + "gate_w1"])).then_inc(w_in[1], 16)
            sp.dma_start(GW2, rowsview(io[L1 + "gate_w2"])).then_inc(w_in[1], 16)
            sp.dma_start(OW, rowsview(io[L1 + "out_w"])).then_inc(w_in[1], 16)
            sp.dma_start(ANB[:, 12:14], colview(io[L1 + "gate_b1"])).then_inc(w_in[1], 16)
            sp.dma_start(RWT, rowsview(io[L1 + "router_W"])).then_inc(w_in[1], 16)
            sp.dma_start(RB, bcast(io[L1 + "router_b"])).then_inc(w_in[1], 16)
            sp.dma_start(OBB, bcast(io[L1 + "out_b"], E3)).then_inc(w_in[1], 16)
            sp.dma_start(GB2, bcast(io[L1 + "gate_b2"], 1)).then_inc(w_in[1], 16)

            sp.wait_ge(e_fd, 4 * NB)
            sp.dma_start(Wqkv, rowsview(io[L2 + "W_qkv"])).then_inc(w_in[2], 16)
            for w, n in ((Wo, "W_proj"), (Wcq, "W_qc"), (Wco, "W_cproj")):
                sp.dma_start(w, rowsview(io[L2 + n])).then_inc(w_in[2], 16)
            sp.dma_start(BV[:, :], bcast(io[L2 + "b_qkv"][2 * D:3 * D])).then_inc(w_in[2], 16)
            with sp.Fori(0, NB) as b:
                self_dma(2, b)
                cross_dma(2, b)

            sp.wait_ge(m_done, 8 * NB)
            sp.dma_start(Wcq, rowsview(io[L3 + "Wq"])).then_inc(w_in[3], 16)
            sp.dma_start(Wco, rowsview(io[L3 + "Wp"])).then_inc(w_in[3], 16)
            with sp.Fori(0, NB) as b:
                cross_dma(3, b)
                sp.wait_ge(o_done, outs(3, b, 0) * 4 + 4)
                sp.dma_start(io["y"][bass.ds(b, 1)].rearrange("a (t p) d -> p (a t) d", p=P), X[:, bass.ts(b, NT), :]).then_inc(y_out, 16)
            sp.wait_ge(y_out, 16 * NB)

        @block.tensor
        def _(pe):
            def mm(out, lhsT, rhs, first=True, last=True):
                return pe.matmul(out, lhsT, rhs, start=first, stop=last)

            pe.wait_ge(cond_in, 16)
            pe.wait_ge(const_in, 16)
            for kt in range(KT):
                last = pe.transpose(PS[:, 0, kt * NB:(kt + 1) * NB], condR[:, kt * P:(kt + 1) * P], ident[0:NB, 0:NB])
            last.then_inc(pe_prep, 1)
            for t in range(NT):
                pe.wait_ge(dve_prep, at(DVE_PREP, f"mask_bf_{t}"))
                if t == 0:
                    pe.wait_ge(pool_prep, POOL_IDENT)
                for k in range(NT):
                    last = pe.transpose(PSB[:, 4 + (t % 2) * 2 + k // 4, (k % 4) * P:(k % 4 + 1) * P], MKB[:, k * P:(k + 1) * P], identb[:, :])
                last.then_inc(pe_prep, 1)
            pe.wait_ge(dve_prep, at(DVE_PREP, "few_rows"))
            mm(PS[0:1, 7, 0:1], FEW_Q, MHALF[:, 0:1]).then_inc(pe_prep, 1)
            pe.wait_ge(modw_in, 8 * 16)
            pe.wait_ge(dve_prep, at(DVE_PREP, "cond_T"))
            pe.wait_ge(act_prep, 1)
            for i in range(10):
                if i == 5:
                    pe.wait_ge(dve_prep, at(DVE_PREP, "mod_a"))
                lo, hi = mod_chunks[i]
                for kt in range(KT):
                    last = mm(PS[0:NB, 1 + i % 5, 0:hi - lo], (condT if hi <= MOD2 else csT)[:, kt, :], MWB[:, kt, lo:hi], kt == 0, kt == 1)
                if i in (4, 9):
                    last.then_inc(pe_prep, 1)
            pe.wait_ge(dve_prep, at(DVE_PREP, "mod_b"))
            for c in range(MODN // P):
                last = pe.transpose(PS[:, 0, c * NB:(c + 1) * NB], MROW[:, c * P:(c + 1) * P], ident[0:NB, 0:NB])
            last.then_inc(pe_prep, 1)
            pe.wait_ge(dve_prep, at(DVE_PREP, "ctx_rows"))
            for v in range(3):
                for kt in range(KT):
                    for b in range(NB):
                        last = pe.transpose(PS[:, 1 + v * KT + kt, b * NC:(b + 1) * NC], CTK[:, v, b, kt * P:(kt + 1) * P], ident[0:NC, 0:NC])
            last.then_inc(pe_prep, 1)
            pe.wait_ge(dve_prep, at(DVE_PREP, "ctx_T"))
            for l in range(3):
                for m in range(KT):
                    for kt in range(KT):
                        last = mm(PS[:, 1 + l * KT + m, 0:CTX], KCW[:, l, kt, m * P:(m + 1) * P], CXT[:, l, kt, :], kt == 0, kt == 1)
            last.then_inc(pe_prep, 1)
            pe.wait_ge(dve_prep, at(DVE_PREP, "kc"))
            pe.wait_ge(l1w_in, 7 * 16)
            for i, w in enumerate((W1K, W1V)):
                for m in range(KT):
                    for kt in range(KT):
                        last = mm(PS[:, 1 + i * KT + m, 0:CTX], w[:, kt, m * P:(m + 1) * P], CXT[:, 0, kt, :], kt == 0, kt == 1)
            last.then_inc(pe_prep, 1)
            for m in range(KT):
                for kt in range(KT):
                    last = pe.transpose(PS[:, 5, (m * KT + kt) * P:(m * KT + kt + 1) * P], W1Q[:, kt, m * P:(m + 1) * P], ident[:, :])
            last.then_inc(pe_prep, 1)
            pe.wait_ge(dve_prep, at(DVE_PREP, "wq_T"))
            for m in range(KT):
                for kt in range(KT):
                    last = mm(PS[:, 6 + m, 0:CTX], W1QT[:, kt, m * P:(m + 1) * P], K1T[:, kt, :], kt == 0, kt == 1)
            last.then_inc(pe_prep, 1)
            pe.wait_ge(dve_prep, at(DVE_PREP, "l1_kv"))
            for l in range(3):
                if l:
                    pe.wait_ge(dve_prep, at(DVE_PREP, f"vc_{l - 1}"))
                for b in range(NB):
                    for kt in range(KT):
                        last = mm(PS[0:NC, 1 + b // 2, (b % 2) * D:(b % 2 + 1) * D], CXT[:, l, kt, b * NC:(b + 1) * NC], KCW[:, l, kt, D:2 * D], kt == 0, kt == 1)
                last.then_inc(pe_prep, 1)
            few_pe = pe.value_load(FEW)

            def norm_pe(n):
                for t in range(NT):
                    pe.wait_ge(ln_norm, n * 8 + t + 1)
                    for ft in range(KT):
                        last = pe.transpose(PS[:, ft * 2 + t // 4, (t % 4) * P:(t % 4 + 1) * P], XN[:, t, ft * P:(ft + 1) * P], ident[:, :])
                    if t % 4 == 3:
                        last.then_inc(ln_tp, 1)

            def project_pe(n, tiles, free, f0):
                for i, (w, col, rot) in enumerate(tiles):
                    for hf in range(NH):
                        st = 2 * i + hf
                        if i == 0:
                            pe.wait_ge(ln_xt_a, n * 2 + hf + 1)
                            pe.wait_ge(ln_xt_d, n * 2 + hf + 1)
                        if st >= 2:
                            pe.wait_ge(free, f0 + st - 1)
                        bank = 4 + 2 * (st % 2)
                        for kt in range(KT):
                            last = mm(PS[:, bank, :], w[:, kt, col:col + P], XT[:, kt, hf * HALF:(hf + 1) * HALF], kt == 0, kt == 1)
                        if rot is not None:
                            for kt in range(KT):
                                last = mm(PS[:, bank + 1, :], Wrot[:, kt, rot:rot + P], XT[:, kt, hf * HALF:(hf + 1) * HALF], kt == 0, kt == 1)
                        last.then_inc(qk_ps, 1)

            def self_pe(l, b):
                s, n = selfs(l, b), norm(l, b, 0)
                tiles = [(Wqkv, m * P + a * D, (m * P + a * D) if l == 0 else None) for m in range(KT) for a in range(2)]
                project_pe(n, tiles, qk_t if l == 0 else qk_f, 8 * b if l == 0 else qsteps(l, b, 0))
                for t in range(NT):
                    for kt in range(KT):
                        last = mm(PS[:, t // 2, (t % 2) * D:(t % 2 + 1) * D], XT[:, kt, t * P:(t + 1) * P], Wqkv[:, kt, 2 * D:3 * D], kt == 0, kt == 1)
                    if t % 2:
                        last.then_inc(v_ps, 1)
                pe.wait_ge(v_sb, s * 4 + 4)
                pe.wait_ge(krow_in, krows(l, b, 0) * 16)
                if l == 0:
                    with pe.If(few_pe == 1):
                        attend_pe(l, s, True)
                    with pe.Else():
                        attend_pe(l, s, False)
                else:
                    attend_pe(l, s, False)

            def attend_pe(l, s, few):
                masked = l == 0
                tiles, w = key_tiles(few), weight(few)

                def max_scores(h, qt, hf, bank):
                    k0, n = ((NT - LIVE) * P, LIVE * P) if few else (hf * HALF, HALF)
                    for i in range(HALF // n):
                        q = slice((qt + i) * P, (qt + i + 1) * P)
                        last = mm(PS[:, bank, i * n:(i + 1) * n], QS[0:MASK_ROW, h, q].rearrange("p a n -> p (a n)"),
                                  KS[0:MASK_ROW, h, k0:k0 + n].rearrange("p a n -> p (a n)"), True, not masked)
                        if masked:
                            for m in range(n // P):
                                last = mm(PS[:, bank, i * n + m * P:i * n + (m + 1) * P], MM[:, k0 // P + m, q], bigI[:, :], False, m == n // P - 1)
                    last.then_inc(ring_full, w)

                def ring_op(op, ring, g):
                    if op[0] == "max":
                        pe.wait_ge(ring_free, ring.count() - ring.back)
                        max_scores(bass.ds(g * HG + op[1], 1), op[2], op[3], ring.bank())
                    elif op[0] == "nm":
                        pe.wait_ge(nm_done, s * NG + g + 1)
                        pe.transpose(PS[0:HG * NT, 0, 0:P], NMG[:, :], ident[:, :]).then_inc(ring_full, 2)
                    else:
                        pe.wait_ge(ring_free, ring.count())
                        pe.wait_ge(acc_out, s * NG + g + 1)
                        for qt in range(NT):
                            last = pe.transpose(PS[:, qt // 4, (qt % 4) * P:(qt % 4 + 1) * P], OT[:, qt * P:(qt + 1) * P], ident[:, :])
                        last.then_inc(ring_full, 2)
                    ring.use(op)

                def pv(g, i, hf, peeled0):
                    if hf == 0:
                        pe.wait_ge(ex_done, (s * NG + g) * 32 + (4 * i + 4) * w)
                    if i == 0 and hf == 0:
                        pe.wait_ge(vg_in, s * NG + g + 1)
                        if not peeled0:
                            pe.wait_ge(acc_out, s * NG + g)
                    for j in range(HG):
                        last = mm(PS[32 * j:32 * j + 32, 6 + hf, :], VG[:, tiles[i], j, :], PR[:, i % 2, j, hf * HALF:(hf + 1) * HALF], i == 0, i == len(tiles) - 1)
                    if hf:
                        last.then_inc(pv_done, w)

                def body(g, with_max, with_tail, peeled0=False):
                    ring = Ring(ring_at(s, g), few)
                    pace = Pace(few, with_max, with_tail)
                    if with_max:
                        wait_stack(g + 1)

                    def turn(work):
                        for op in pace.due(work):
                            ring_op(op, ring, g - 1 if op[0] == "tail" else g + 1)

                    pe.wait_ge(nm_in, (s * NG + g + 1) * 48)
                    for k in range(len(tiles) * HG):
                        i, j = k // HG, k % HG
                        kt = tiles[i]
                        if k >= 2 or not peeled0:
                            pe.wait_ge(ex_done, (s * NG + g) * 32 + (k - 1) * w)
                        h = g * HG + j
                        for hf in range(NH):
                            last = mm(PS[:, 2 + 2 * (k % 2) + hf, :], KS[0:ROWS, bass.ds(h, 1), kt * P:(kt + 1) * P].rearrange("p a n -> p (a n)"),
                                      QS[0:ROWS, bass.ds(h, 1), hf * HALF:(hf + 1) * HALF].rearrange("p a n -> p (a n)"), True, not masked)
                            if masked:
                                last = mm(PS[:, 2 + 2 * (k % 2) + hf, :], bigI[:, :], MM[:, kt, hf * HALF:(hf + 1) * HALF], False, True)
                            if hf:
                                last.then_inc(st_full, w)
                            turn(2 if few else 1)
                        if j in (1, 2) and i >= 1:
                            pv(g, i - 1, j - 1, peeled0)
                            turn(HG)
                    for hf in range(NH):
                        pv(g, len(tiles) - 1, hf, peeled0)
                        turn(HG)
                    assert pace.done == len(pace.order)

                def wait_stack(g):
                    if isinstance(g, int):
                        pe.wait_ge(stack_in[g], (s + 1) * 192)
                    else:
                        for i in range(NG):
                            pe.wait_ge(stack_in[i], (s + 1) * 192)

                wait_stack(0)
                ring = Ring(s * RINGN, few, PRO_BANKS)
                for n, op in enumerate(max_uses(few)):
                    if n < PRO_BANKS:
                        max_scores(slice(op[1], op[1] + 1), op[2], op[3], n)
                        ring.use(op)
                    else:
                        ring_op(op, ring, 0)
                ring_op(("nm",), ring, 0)
                body(0, True, False, peeled0=True)
                with pe.Fori(1, NG - 1) as g:
                    body(g, True, True)
                body(NG - 1, False, True)
                ring = Ring(ring_at(s, NG - 1) + 2, few)
                ring_op(("tail",), ring, NG - 1)

            def out_pe(l, b, i, att_sem, att_val, w, gated):
                o = outs(l, b, i)
                pe.wait_ge(att_sem, att_val)
                for t in range(NT):
                    for ft in range(KT):
                        last = pe.transpose(PS[:, ft * 2 + t // 4, (t % 4) * P:(t % 4 + 1) * P], XN[:, t, ft * P:(ft + 1) * P], ident[:, :])
                    if t % 4 == 3:
                        last.then_inc(o_tp, 1)
                if gated is not None:
                    pe.wait_ge(wg_done, gated + 1)
                for t in range(NT):
                    if t % 4 == 0:
                        pe.wait_ge(o_xt_a, o * 2 + t // 4 + 1)
                        pe.wait_ge(o_xt_d, o * 2 + t // 4 + 1)
                    for kt in range(KT):
                        last = mm(PS[:, 4 + t // 2, (t % 2) * D:(t % 2 + 1) * D], XT[:, kt, t * P:(t + 1) * P], w[:, kt, :], kt == 0, kt == 1)
                    if t % 2:
                        last.then_inc(o_ps, 1)

            def cross_pe(l, b):
                c, n = crosses(l, b), norm(l, b, 0 if l == 3 else 1)
                project_pe(n, [(Wcq, m * P, None) for m in range(KT)], qk_f, qsteps(l, b, 0 if l == 3 else 1))
                pe.wait_ge(krow_in, krows(l, b, 1) * 16)
                pe.wait_ge(kc_in, (c + 1) * 9 * 16)
                for r in range(16):
                    g, qt = r // 8 * 2, r % 8
                    if qt == 0:
                        pe.wait_ge((cst_a, cst_b)[r // 8], (c + 1) * 96)
                    if r >= 2:
                        pe.wait_ge(c_free, c * 16 + r - 1)
                    for j in range(2 * HG):
                        last = mm(PS[:, r % 2 * 2 + j // HG, j % HG * NC:(j % HG + 1) * NC], QS[0:MAX_ROW, g * HG + j, qt * P:(qt + 1) * P],
                                  KC[0:MAX_ROW, g * HG + j, 0:NC])
                    last.then_inc(c_full, 1)
                pe.wait_ge(c_free, c * 16 + 16)
                pe.transpose(PS[:, 0, 0:P], NM[:, :, :].rearrange("p h t -> p (h t)"), ident[:, :]).then_inc(c_nmT, 1)
                pe.wait_ge(c_nm_in, (c + 1) * 48)

                def pv(g):
                    pe.wait_ge(c_ex, c * H + 4 * g + 4)
                    if g:
                        pe.wait_ge(c_acc, c * NG + g)
                    for hf in range(NH):
                        for j in range(HG):
                            last = mm(PS[32 * j:32 * j + 32, 6 + hf, :], VC[:, g * HG + j, :], PR[:, g % 2, j, hf * HALF:(hf + 1) * HALF])
                    last.then_inc(c_pv, 1)

                def tail(g):
                    pe.wait_ge(c_acc, c * NG + g + 1)
                    if g:
                        pe.wait_ge(c_at, c * 8 + 2 * g)
                    for qt in range(NT):
                        last = pe.transpose(PS[:, qt // 4, (qt % 4) * P:(qt % 4 + 1) * P], OT[:, qt * P:(qt + 1) * P], ident[:, :])
                    last.then_inc(c_tp, 1)

                for h in range(H):
                    if h >= 2:
                        pe.wait_ge(c_ex, c * H + h - 1)
                    for hf in range(NH):
                        last = mm(PS[:, 2 + 2 * (h % 2) + hf, :], KC[0:ROWS, h, :], QS[0:ROWS, h, hf * HALF:(hf + 1) * HALF])
                    last.then_inc(c_st, 1)
                    if h >= 5 and h % 4 == 1:
                        pv(h // 4 - 1)
                    if h >= 7 and h % 4 == 3:
                        tail(h // 4 - 1)
                pv(NG - 1)
                tail(NG - 1)

            def mlp_pe(l, b):
                m_, n = mlps(l, b), norm(l, b, 2)
                pe.wait_ge(mw_in, (m_ + 1) * 32)
                for i in range(MT_ * NH):
                    m, hf = i // 2, i % 2
                    if i < 2:
                        pe.wait_ge(ln_xt_a, n * 2 + hf + 1)
                        pe.wait_ge(ln_xt_d, n * 2 + hf + 1)
                    if i >= 4:
                        pe.wait_ge(m_h, m_ * 16 + i - 3)
                    for kt in range(KT):
                        last = mm(PS[:, 4 + i % 4, :], W1[:, kt, m * P:(m + 1) * P], XT[:, kt, hf * HALF:(hf + 1) * HALF], kt == 0, kt == 1)
                    last.then_inc(m_ps, 1)
                pe.wait_ge(m_w2g, m_ + 1)
                pe.wait_ge(m_h, m_ * 16 + 16)
                for t in range(NT):
                    for kt in range(MT_):
                        last = mm(PS[:, t // 2, (t % 2) * D:(t % 2 + 1) * D], HT[:, kt, t * P:(t + 1) * P], W2[:, kt, :], kt == 0, kt == MT_ - 1)
                    if t % 2:
                        last.then_inc(m_ops, 1)

            def layer02_pe(l, b):
                norm_pe(norm(l, b, 0))
                self_pe(l, b)
                out_pe(l, b, 0, at_done, (selfs(l, b) + 1) * 8, WG, gates(l, b, 0))
                norm_pe(norm(l, b, 1))
                cross_pe(l, b)
                out_pe(l, b, 1, c_at, (crosses(l, b) + 1) * 8, WG if l == 0 else Wco, gates(l, b, 1) if l == 0 else None)
                norm_pe(norm(l, b, 2))
                mlp_pe(l, b)

            pe.wait_ge(w_in[0], 4 * 16)
            pe.wait_ge(pool_prep, POOL_WROT)
            with pe.Fori(0, NB) as b:
                layer02_pe(0, b)

            pe.wait_ge(w_in[1], (E3 * 5 + 8) * 16)
            for m in range(14):
                for kt in range(KT):
                    w = EW1A[:, kt, m // RT, (m % RT) * P:(m % RT + 1) * P] if m < 12 else GW1[:, 4 + kt, (m - 12) * P:(m - 11) * P]
                    mm(PS[:, 4, m * NB:(m + 1) * NB], w, condT[:, kt, :], kt == 0, kt == 1)
            for b in range(NB):
                for kt in range(KT):
                    mm(PS[:, 5, b * 4:b * 4 + E3], condT[:, kt, b:b + 1].broadcast_to([P, P]), RWT[:, 4 + kt, :], kt == 0, kt == 1)
            for kt in range(KT):
                last = mm(PS[0:E3, 6, 0:D], B2T[:, kt, :], OW[:, kt, :], kt == 0, kt == 1)
            last.then_inc(e_pro, 1)
            pe.wait_ge(e_prd, 4)

            def layer1_pe(b):
                n = norm(1, b, 0)
                norm_pe(n)
                pe.wait_ge(e_v1b, b + 1)
                for i in range(3):
                    for kt in range(KT):
                        mm(PS[0:NC, 4 + i, :], V1B[:, kt, :], EW1[:, 2 + kt, i, :], kt == 0, kt == 1)
                for kt in range(KT):
                    mm(PS[0:NC, 7, 0:D], V1B[:, kt, :], GW1[:, 2 + kt, :], kt == 0, kt == 1)
                for kt in range(KT):
                    last = mm(PS[0:NC, 7, D:D + E3], V1B[:, kt, :], RWT[:, 2 + kt, :], kt == 0, kt == 1)
                last.then_inc(e_ve, 1)
                pe.wait_ge(ln_xt_a, n * 2 + 2)
                pe.wait_ge(ln_xt_d, n * 2 + 2)
                for t in range(NT):
                    for kt in range(KT):
                        last = mm(PS[:, t // 4, (t % 4) * 80:(t % 4) * 80 + 80], XT[:, kt, t * P:(t + 1) * P],
                                  A1[:, kt, bass.ds(b, 1), :].rearrange("p a n -> p (a n)"), kt == 0, kt == 1)
                last.then_inc(e_sc, 1)
                pe.wait_ge(e_pxn, b + 1)
                for t in range(NT):
                    last = pe.transpose(PS[0:NC, 2 + t // 4, (t % 4) * P:(t % 4 + 1) * P], PX[:, t, 0:NC], ident[:, :])
                last.then_inc(e_pt, 1)
                pe.wait_ge(e_ptsb, b + 1)
                pe.wait_ge(e_vesb, b * 2 + 2)
                for t in range(NT):
                    last = mm(PS[:, 0, t * 4:t * 4 + E3], PT[0:NC, t * P:(t + 1) * P], VE[:, 1792:1792 + E3])
                last.then_inc(e_rt, 1)

                def hidden(q, w, col):
                    hf = q % 2
                    if q >= 4:
                        pe.wait_ge(e_hsb, b * 28 + q - 3)
                    for kt in range(KT):
                        mm(PS[:, 4 + q % 4, :], w(kt), XT[:, kt, hf * HALF:(hf + 1) * HALF], kt == 0, False)
                    mm(PS[:, 4 + q % 4, :], VE[:, col:col + P], PT[0:NC, hf * HALF:(hf + 1) * HALF], False, True).then_inc(e_hps, 1)

                def expert_out(e):
                    pe.wait_ge(e_hsb, b * 28 + 4 + 8 * e + 8)
                    for t in range(NT):
                        o = e * NT + t
                        if o >= 4:
                            pe.wait_ge(e_ho, b * 24 + o - 3)
                        for r in range(RT):
                            last = mm(PS[:, o % 4, 0:D], HE[:, e % 2, r, t * P:(t + 1) * P], EW2[:, e * RT + r, :], r == 0, r == RT - 1)
                        last.then_inc(e_ops, 1)

                for q in range(4):
                    r = q // 2
                    hidden(q, lambda kt: GW1[:, kt, r * P:(r + 1) * P], 1536 + r * P)
                for e in range(E3):
                    for q in range(8):
                        r = q // 2
                        hidden(4 + 8 * e + q, lambda kt: EW1[:, kt, e, r * P:(r + 1) * P], e * RH + r * P)
                    if e == 0:
                        pe.wait_ge(e_rp, b + 1)
                        for t in range(NT):
                            last = pe.transpose(PS[0:E3, t // 4, (t % 4) * P:(t % 4 + 1) * P], RP[:, t, :], ident[:, :])
                        last.then_inc(e_rpt, 1)
                        pe.wait_ge(e_rptsb, b + 1)
                    else:
                        expert_out(e - 1)
                expert_out(E3 - 1)
                pe.wait_ge(e_ho, b * 24 + 24)
                for t in range(NT):
                    for ft in range(KT):
                        last = pe.transpose(PS[:, ft * 2 + t // 4, (t % 4) * P:(t % 4 + 1) * P], ROU[:, t, ft * P:(ft + 1) * P], ident[:, :])
                    if t % 4 == 3:
                        last.then_inc(e_rot, 1)
                for i in range(4):
                    if i % 2 == 0:
                        pe.wait_ge(e_rx_a, b * 2 + i // 2 + 1)
                        pe.wait_ge(e_rx_d, b * 2 + i // 2 + 1)
                    if i >= 2:
                        pe.wait_ge(e_fd, b * 4 + i - 1)
                    for t in (2 * i, 2 * i + 1):
                        c0 = (t % 2) * D
                        for kt in range(KT):
                            mm(PS[:, 4 + (i % 2) * 2, c0:c0 + D], XT[:, kt, t * P:(t + 1) * P], OW[:, kt, :], kt == 0, False)
                        mm(PS[:, 4 + (i % 2) * 2, c0:c0 + D], PTR[:, t * P:(t + 1) * P], B2O, False, True)
                        for kt in range(KT):
                            mm(PS[:, 5 + (i % 2) * 2, c0:c0 + D], GT[:, kt, t * P:(t + 1) * P], GW2[:, kt, :], kt == 0, False)
                        last = mm(PS[:, 5 + (i % 2) * 2, c0:c0 + D], ONE, GB2, False, True)
                    last.then_inc(e_fin, 1)

            with pe.Fori(0, NB) as b:
                layer1_pe(b)

            pe.wait_ge(w_in[2], 5 * 16)
            with pe.Fori(0, NB) as b:
                layer02_pe(2, b)

            pe.wait_ge(w_in[3], 2 * 16)
            with pe.Fori(0, NB) as b:
                norm_pe(norm(3, b, 0))
                cross_pe(3, b)
                out_pe(3, b, 0, c_at, (crosses(3, b) + 1) * 8, Wco, None)

        @block.vector
        def _(dve):
            def step(ins, name):
                ins.then_inc(dve_prep, 1)
                assert done.append(name) is None and DVE_PREP[len(done) - 1] == name, name

            def wait(name):
                dve.wait_ge(dve_prep, at(DVE_PREP, name))

            done = []
            dve.memset(CRS[:, :, :], 0.0)
            dve.memset(MRZ, 0.0)
            step(dve.memset(MHALF[:, :], -0.5), "zeros")
            dve.wait_ge(pe_prep, at(PE_PREP, "cond_T"))
            step(dve.tensor_copy(condT[:, :, :], PS[:, 0, 0:KT * NB].rearrange("p (k b) -> p k b", k=KT)), "cond_T")
            for t in range(NT):
                dve.wait_ge(mask_in[t // 4], 16)
                if t:
                    dve.wait_ge(pe_prep, at(PE_PREP, f"mask_{t - 1}"))
                    wait(f"mask_{t - 1}")
                step(dve.tensor_scalar(MKB, MKU[:, t, :], -1.0, 1.0, ALU.mult, ALU.add), f"mask_bf_{t}")
                wait(f"mask_bf_{t}")
                dve.tensor_reduce(FEW_T[:, t, 0:1], MKB[:, 0:(NT - LIVE) * P], AX.X, ALU.min)
                dve.tensor_reduce(FEW_T[:, t, 1:2], MKB[:, (NT - LIVE) * P:], AX.X, ALU.min)
                dve.wait_ge(pe_prep, at(PE_PREP, f"mask_{t}"))
                for i in range(2):
                    last = dve.tensor_copy(MM[:, i * 4:(i + 1) * 4, t * P:(t + 1) * P], PSB[:, 4 + (t % 2) * 2 + i, 0:HALF].rearrange("p (k q) -> p k q", q=P), saturate=False)
                step(last, f"mask_{t}")
            wait(f"mask_{NT - 1}")
            dve.tensor_tensor(FEW_D, FEW_T[:, :, 0], FEW_T[:, :, 1], ALU.subtract).then_inc(few_own, 1)
            dve.wait_ge(few_own, 1)
            step(dve.tensor_reduce(FEW_Q, FEW_D, AX.X, ALU.min), "few_rows")
            dve.wait_ge(pe_prep, at(PE_PREP, "few_sum"))
            step(dve.tensor_scalar(FEW, PS[0:1, 7, 0:1], -2.0, 1.0 - P, ALU.mult, ALU.add), "few")
            dve.wait_ge(modw_in, 8 * 16)
            for i, (lo, hi) in enumerate(mod_chunks):
                if i in (0, 5):
                    dve.wait_ge(pe_prep, at(PE_PREP, "mod_a" if i == 0 else "mod_b"))
                last = dve.tensor_tensor(MROW[:, lo:hi], PS[0:NB, 1 + i % 5, 0:hi - lo], MBIAS[:, lo:hi], ALU.add)
                if i in (4, 9):
                    step(last, "mod_a" if i == 4 else "mod_b")
            dve.wait_ge(pe_prep, at(PE_PREP, "mod_T"))
            step(dve.tensor_copy(MODC[:, :, :], PS[:, 0, 0:MODN // P * NB].rearrange("p (c b) -> p c b", b=NB)), "mod_T")
            dve.wait_ge(small_in, 15 * 16)
            wait("mod_T")
            for n, scale, shift in ((0, MOD0 + D, MOD0), (1, MOD0 + 4 * D, MOD0 + 3 * D), (2, MOD0 + 7 * D, MOD0 + 6 * D), (3, None, None),
                                    (4, MOD2 + D, MOD2), (5, None, None), (6, MOD2 + 4 * D, MOD2 + 3 * D), (7, MODQ, MODQ + D)):
                for kt in range(KT):
                    A, B = AB[:, n, kt, 0, :], AB[:, n, kt, 1, :]
                    if n < 3:
                        dve.tensor_scalar(A, MODC[:, scale // P + kt, :], 1.0, LNW[:, n, kt:kt + 1], ALU.add, ALU.mult)
                    elif n == 3:
                        dve.tensor_scalar(A, MODC[:, 0, :], 0.0, LNW[:, 3, kt:kt + 1], ALU.mult, ALU.add)
                    elif n == 5:
                        dve.memset(A, 1.0)
                    else:
                        dve.tensor_scalar(A, MODC[:, scale // P + kt, :], 1.0, None, ALU.add)
                    if n == 3:
                        last = dve.tensor_scalar(B, MODC[:, 0, :], 0.0, LNW[:, 4, kt:kt + 1], ALU.mult, ALU.add)
                    elif n == 5:
                        last = dve.memset(B, 0.0)
                    else:
                        last = dve.tensor_copy(B, MODC[:, shift // P + kt, :])
            step(last, "ab")
            dve.wait_ge(ctx_in, 5 * 16)
            for b in range(NB):
                last = dve.bn_stats(CST[:, b, :], CTK[:, 0, b, :])
            step(last, "ctx_stats")
            wait("ctx_stats")
            for b in range(NB):
                last = dve.bn_aggr(CMV[:, b, :], CST[:, b, :])
            last.then_inc(pool_go, 1)
            dve.wait_ge(pool_go, 1)
            dve.wait_ge(pool_prep, POOL_CTX)
            for v in range(2):
                for b in range(NB):
                    last = dve.tensor_scalar(CTK[:, 1 + v, b, :], CTK[:, 0, b, :], CMV[:, b, 0:1], CRS[:, v, b:b + 1], ALU.subtract, ALU.mult)
            step(last, "ctx_rows")
            dve.wait_ge(pe_prep, at(PE_PREP, "ctx_T"))
            for kt in range(KT):
                dve.tensor_copy(CXT[:, 0, kt, :], PS[:, 1 + kt, 0:CTX])
                dve.tensor_copy(CXT[:, 1, kt, :], PS[:, 1 + KT + kt, 0:CTX])
                for b in range(NB):
                    last = dve.tensor_scalar(CXT[:, 2, kt, b * NC:(b + 1) * NC], PS[:, 1 + 2 * KT + kt, b * NC:(b + 1) * NC], AKV[:, kt, b:b + 1],
                                             MODC[:, (MODK + D) // P + kt, b:b + 1], ALU.mult, ALU.add)
            step(last, "ctx_T")
            dve.wait_ge(pe_prep, at(PE_PREP, "kc"))
            dve.wait_ge(pool_prep, POOL_ZERO)
            for l in range(3):
                for m in range(KT):
                    src = PS[:, 1 + l * KT + m, 0:CTX].rearrange("p (b n) -> p b n", b=NB)
                    if l == 0:
                        last = dve.tensor_copy(KCF[:, l, m, :, 0:NC], src)
                    else:
                        last = dve.tensor_scalar(KCF[:, l, m, :, 0:NC], src, QB[:, 3 + l, m:m + 1], None, ALU.add)
            step(last, "kc")
            wait("kc")
            full, rest = BIG[:, 0:3072], BIG[:, 3072:6144]
            part = [BIG[:, 6144 + a * 1536:6144 + (a + 1) * 1536].bitcast(BF16) for a in range(3)]
            step(dve.tensor_copy(part[0], full), "kc_high")
            wait("kc_high")
            step(dve.tensor_tensor(rest, full, part[0], ALU.subtract), "kc_rest")
            wait("kc_rest")
            step(dve.tensor_copy(part[1], rest), "kc_middle")
            wait("kc_middle")
            step(dve.tensor_tensor(part[2], rest, part[1], ALU.subtract), "kc_parts")
            dve.wait_ge(pe_prep, at(PE_PREP, "l1_kv"))
            for m in range(KT):
                dve.tensor_copy(K1T[:, m, :], PS[:, 1 + m, 0:CTX])
                last = dve.tensor_copy(V1T[:, m, :, :], PS[:, 3 + m, 0:CTX].rearrange("p (b n) -> p b n", b=NB))
            step(last, "l1_kv")
            dve.wait_ge(pe_prep, at(PE_PREP, "wq_T"))
            step(dve.tensor_copy(W1QT.rearrange("p k m -> p (k m)"), PS[:, 5, :]), "wq_T")
            dve.wait_ge(pe_prep, at(PE_PREP, "l1_a"))
            for m in range(KT):
                last = dve.tensor_copy(A1[:, m, :, 0:NC], PS[:, 6 + m, 0:CTX].rearrange("p (b n) -> p b n", b=NB))
            step(last, "l1_a")
            for l in range(3):
                dve.wait_ge(pe_prep, at(PE_PREP, f"vc_{l}"))
                if l:
                    dve.wait_ge(vc_out, l * 16)
                for b in range(NB):
                    src = PS[0:NC, 1 + b // 2, (b % 2) * D:(b % 2 + 1) * D].rearrange("p (h d) -> p h d", h=H)
                    if l == 0:
                        last = dve.tensor_copy(VCS[0:NC, b, :, 0:HD], src)
                    else:
                        last = dve.tensor_tensor(VCS[0:NC, b, :, 0:HD], src, (BV, BV3)[l - 1][0:NC, :].rearrange("p (h d) -> p h d", h=H), ALU.add)
                step(last, f"vc_{l}")
            dve.wait_ge(maskrow_in, 16)
            dve.memset(MRF[:, NC:P], 0.0)
            step(dve.tensor_copy(MRF[:, 0:NC], MRU), "mask_row_f")
            wait("mask_row_f")
            dve.tensor_scalar(MRB, MRF, 1.0, -MASKED, ALU.subtract, ALU.mult)
            step(dve.memset(MRZ[:, NC:P], MASKED), "mask_row")
            dve.wait_ge(v_zero, 1)
            step(dve.memset(V[:, :, :, HD:HD + 1], 1.0), "v_ones")
            assert len(done) == len(DVE_PREP)
            few_dve = dve.value_load(FEW)

            def norm_dve(n, b, ln, x_sem, x_val):
                x = X[:, bass.ts(b, NT), :]
                if x_sem is not None:
                    dve.wait_ge(x_sem, x_val)
                    settle(dve)
                    for t in range(NT):
                        last = dve.bn_stats(ST[:, t, :], x[:, t, :])
                    last.then_inc(ln_st, 1)
                dve.wait_ge(ln_st, n + 1)
                settle(dve)
                for t in range(NT):
                    last = dve.bn_aggr(MV[:, t, :], ST[:, t, :])
                last.then_inc(ln_mv, 1)
                dve.wait_ge(ln_rs, n + 1)
                for t in range(NT):
                    dve.tensor_scalar(XN[:, t, :], x[:, t, :], MV[:, t, 0:1], RS[:, t:t + 1], ALU.subtract, ALU.mult).then_inc(ln_norm, 1)
                for hf in range(NH):
                    dve.wait_ge(ln_tp, n * 2 + hf + 1)
                    dve.tensor_scalar(XT[:, 1, hf * HALF:(hf + 1) * HALF], PS[:, 2 + hf, :], AB[:, ln, 1, 0, bass.ds(b, 1)], AB[:, ln, 1, 1, bass.ds(b, 1)],
                                      ALU.mult, ALU.add).then_inc(ln_xt_d, 1)

            def parts_dve(q0, st, steps):
                if 1 <= st <= steps:
                    k = st - 1
                    if k >= 2:
                        dve.wait_ge(qk_l, q0 + k - 1)
                    dve.wait_ge(qk_h, q0 + k + 1)
                    dve.tensor_tensor(RR[:, k % 2, :], FR[:, k % 2, :], QKP[:, 0, k // 2, (k % 2) * HALF:(k % 2 + 1) * HALF], ALU.subtract).then_inc(qk_r, 1)
                if 2 <= st <= steps + 1:
                    k = st - 2
                    dve.wait_ge(qk_m, q0 + k + 1)
                    dve.tensor_tensor(QKP[:, 2, k // 2, (k % 2) * HALF:(k % 2 + 1) * HALF], RR[:, k % 2, :], QKP[:, 1, k // 2, (k % 2) * HALF:(k % 2 + 1) * HALF],
                                      ALU.subtract).then_inc(qk_l, 1)

            def self_dve(l, b):
                s, q0 = selfs(l, b), qsteps(l, b, 0)
                if l == 0:
                    dve.wait_ge(cs_in, (b + 1) * 32)
                for st in range(10):
                    if l == 0 and st < 8:
                        bank = 4 + 2 * (st % 2)
                        dve.wait_ge(qk_ps, q0 + st + 1)
                        if st:
                            dve.wait_ge(qk_f, q0 + st)
                        dve.tensor_tensor(T12[:, 0, :], PS[:, bank, :], COS, ALU.mult)
                        dve.tensor_tensor(T12[:, 1, :], PS[:, bank + 1, :], SIN, ALU.mult).then_inc(qk_t, 1)
                        dve.wait_ge(qk_t, b * 8 + st + 1)
                        dve.tensor_tensor(FR[:, st % 2, :], T12[:, 0, :], T12[:, 1, :], ALU.add).then_inc(qk_f, 1)
                    parts_dve(q0, st, 8)
                for i in range(4):
                    dve.wait_ge(v_ps, s * 4 + i + 1)
                    src = PS[:, i, :].rearrange("p (t h d) -> p t h d", t=2, h=H)
                    for t in range(2):
                        if l == 0:
                            last = dve.tensor_copy(V[:, 2 * i + t, :, 0:HD], src[:, t])
                        else:
                            last = dve.tensor_tensor(V[:, 2 * i + t, :, 0:HD], src[:, t], BV[:, :].rearrange("p (h d) -> p h d", h=H), ALU.add)
                    last.then_inc(v_sb, 1)

                if l == 0:
                    with dve.If(few_dve == 1):
                        attend_dve(s, True)
                    with dve.Else():
                        attend_dve(s, False)
                else:
                    attend_dve(s, False)

            def attend_dve(s, few):
                def ring_op(op, ring, g):
                    if op[0] == "max":
                        _, j, qt, hf = op
                        w = weight(few)
                        dve.wait_ge(ring_full, ring.count() + w)
                        if few:
                            last = dve.tensor_reduce(NMP[:, j, qt:qt + 2, 0], PS[:, ring.bank(), :].rearrange("p (t n) -> p t n", t=2), AX.X, ALU.max, negate=True)
                        else:
                            last = dve.tensor_reduce(NMP[:, j, qt, hf:hf + 1], PS[:, ring.bank(), :], AX.X, ALU.max, negate=True)
                        last.then_inc(ring_free, w)
                        if op == max_uses(few)[-1]:
                            dve.wait_ge(ring_free, ring.count() + w)
                            dve.tensor_tensor(NMG[:, :], NMP[:, :, :, 0].rearrange("p j t -> p (j t)"), NMP[:, :, :, 0 if few else 1].rearrange("p j t -> p (j t)"), ALU.min).then_inc(nm_done, 1)
                    elif op[0] == "nm":
                        dve.wait_ge(ring_full, ring.count() + 2)
                        dve.tensor_copy(NMT[0:HG * NT, :], PS[0:HG * NT, 0, 0:P]).then_inc(nmt_sb, 1)
                        dve.wait_ge(nmt_sb, s * NG + g + 1)
                        dve.tensor_copy(NMK[0:HG * NT, 0:1], NMT[0:HG * NT, 0:1]).then_inc(ring_free, 2)
                    else:
                        dve.wait_ge(ring_full, ring.count() + 2)
                        for hf in range(NH):
                            src = PS[:, hf, :].rearrange("p (t j m) -> p t j m", t=4, j=HG)
                            dve.reciprocal(REC[:, hf * 4:hf * 4 + 4, :], src[:, :, :, HD]).then_inc(rec_done, 1)
                        dve.wait_ge(rec_done, (s * NG + g) * 2 + 2)
                        for t in range(NT):
                            src = PS[:, t // 4, :].rearrange("p (t j m) -> p t j m", t=4, j=HG)
                            last = dve.tensor_tensor(XN[:, t, bass.ts(g, HG * HD)].rearrange("p (j d) -> p j d", j=HG), src[:, t % 4, :, 0:HD],
                                                     REC[:, t, :].rearrange("p (j a) -> p j a", a=1).broadcast_to([P, HG, HD]), ALU.mult)
                            if t % 4 == 3:
                                last.then_inc(at_done, 1)
                        dve.wait_ge(at_done, (s * NG + g) * 2 + 2)
                        dve.tensor_copy(NMK[:, 0:1], REC[:, 0, 0:1]).then_inc(ring_free, 2)
                    ring.use(op)

                def run(g, with_max, with_tail):
                    ring = Ring(ring_at(s, g), few)
                    for op in ring_order(few, with_max, with_tail):
                        ring_op(op, ring, g - 1 if op[0] == "tail" else g + 1)

                ring = Ring(s * RINGN, few, PRO_BANKS)
                for op in max_uses(few) + [("nm",)]:
                    ring_op(op, ring, 0)
                run(0, True, False)
                with dve.Fori(1, NG - 1) as g:
                    run(g, True, True)
                run(NG - 1, False, True)
                ring_op(("tail",), Ring(ring_at(s, NG - 1) + 2, few), NG - 1)

            def out_dve(l, b, i, biased_i, stats=True):
                o = outs(l, b, i)
                for hf in range(NH):
                    dve.wait_ge(o_tp, o * 2 + hf + 1)
                    dve.tensor_copy(XT[:, 1, hf * HALF:(hf + 1) * HALF], PS[:, 2 + hf, :]).then_inc(o_xt_d, 1)
                if biased_i is not None:
                    dve.wait_ge(biased, biased_i + 1)
                for k in range(4):
                    dve.wait_ge(o_ps, o * 4 + k + 1)
                    x = X[:, bass.ds(b * NT + 2 * k, 2), :].rearrange("p a d -> p (a d)")
                    dve.tensor_tensor(x, PS[:, 4 + k, :], x, ALU.add).then_inc(o_done, 1)
                    if stats and k:
                        pair_stats(o, b, k - 1)
                if stats:
                    pair_stats(o, b, 3).then_inc(ln_st, 1)

            def pair_stats(o, b, k):
                dve.wait_ge(o_done, o * 4 + k + 1)
                settle(dve)
                for t in (2 * k, 2 * k + 1):
                    last = dve.bn_stats(ST[:, t, :], X[:, bass.ds(b * NT + t, 1), :].rearrange("p a d -> p (a d)"))
                return last

            def cross_dve(l, b):
                c, q0 = crosses(l, b), qsteps(l, b, 0 if l == 3 else 1)
                for st in range(6):
                    parts_dve(q0, st, 4)
                for r in range(16):
                    g, qt = r // 8 * 2, r % 8
                    dve.wait_ge(c_full, c * 16 + r + 1)
                    dve.tensor_reduce(NM[:, g * HG:(g + 2) * HG, qt].rearrange("p (a j) -> p a j", a=2), PS[:, r % 2 * 2:r % 2 * 2 + 2, 0:HG * NC].rearrange("p a (j n) -> p a j n", j=HG),
                                      AX.X, ALU.max, negate=True).then_inc(c_free, 1)
                dve.wait_ge(c_nmT, c + 1)
                dve.tensor_copy(NMT[:, :], PS[:, 0, 0:P]).then_inc(c_nmt, 1)
                for g in range(NG):
                    dve.wait_ge(c_pv, c * NG + g + 1)
                    if g:
                        dve.wait_ge(c_tp, c * NG + g)
                    dve.tensor_copy(OT[:, :].rearrange("p (a n) -> p a n", a=2), PS[:, 6:8, :]).then_inc(c_acc, 1)
                    dve.wait_ge(c_tp, c * NG + g + 1)
                    for hf in range(NH):
                        src = PS[:, hf, :].rearrange("p (t j m) -> p t j m", t=4, j=HG)
                        dve.reciprocal(REC[:, hf * 4:hf * 4 + 4, :], src[:, :, :, HD]).then_inc(c_rec, 1)
                    dve.wait_ge(c_rec, (c * NG + g) * 2 + 2)
                    for t in range(NT):
                        src = PS[:, t // 4, :].rearrange("p (t j m) -> p t j m", t=4, j=HG)
                        last = dve.tensor_tensor(XN[:, t, g * HG * HD:(g + 1) * HG * HD].rearrange("p (j d) -> p j d", j=HG), src[:, t % 4, :, 0:HD],
                                                 REC[:, t, :].rearrange("p (j a) -> p j a", a=1).broadcast_to([P, HG, HD]), ALU.mult)
                        if t % 4 == 3:
                            last.then_inc(c_at, 1)

            def mlp_dve(l, b):
                m_ = mlps(l, b)
                dve.wait_ge(m_biased, m_ + 1)
                for k in range(4):
                    dve.wait_ge(m_ops, m_ * 4 + k + 1)
                    x = X[:, bass.ds(b * NT + 2 * k, 2), :].rearrange("p a d -> p (a d)")
                    dve.tensor_tensor(x, PS[:, k, :], x, ALU.add).then_inc(m_done, 1)

            def layer02_dve(l, b, x_sem, x_val):
                norm_dve(norm(l, b, 0), b, 0 if l == 0 else 4, x_sem, x_val)
                self_dve(l, b)
                out_dve(l, b, 0, biases(l, b, 0) if l == 2 else None)
                norm_dve(norm(l, b, 1), b, 1 if l == 0 else 5, None, None)
                cross_dve(l, b)
                out_dve(l, b, 1, biases(l, b, 1) if l == 2 else None)
                norm_dve(norm(l, b, 2), b, 2 if l == 0 else 6, None, None)
                mlp_dve(l, b)

            dve.wait_ge(dve_prep, len(DVE_PREP))
            with dve.Fori(0, NB) as b:
                layer02_dve(0, b, x_in, NB * 16)

            dve.wait_ge(w_in[1], (E3 * 5 + 8) * 16)
            dve.memset(ONE, 1.0).then_inc(e_prd, 1)
            dve.wait_ge(e_pro, 1)
            dve.tensor_tensor(ANC, PS[:, 4, 0:14 * NB].rearrange("p (m b) -> p m b", m=14), ANB.rearrange("p (m a) -> p m a", a=1).broadcast_to([P, 14, NB]), ALU.add).then_inc(e_prd, 1)
            dve.tensor_tensor(RAC, PS[:, 5, 0:16].rearrange("p (b e) -> p b e", e=4)[:, :, 0:E3], RB.rearrange("p (a e) -> p a e", a=1).broadcast_to([P, NB, E3]), ALU.add).then_inc(e_prd, 1)
            dve.tensor_tensor(B2O, PS[0:E3, 6, 0:D], OBB, ALU.add).then_inc(e_prd, 1)
            dve.wait_ge(e_prd, 4)

            def layer1_dve(b):
                n = norm(1, b, 0)
                dve.tensor_copy(V1B, V1T[:, :, bass.ds(b, 1), :].rearrange("p k a n -> p k (a n)")).then_inc(e_v1b, 1)
                norm_dve(n, b, 3, m_done, 4 * NB)
                dve.wait_ge(e_sc, b + 1)
                for i in range(2):
                    ps = PS[:, i, 0:320].rearrange("p (t n) -> p t n", n=80)
                    dve.tensor_tensor(RL[:, i * 4:(i + 1) * 4, :], ps[:, :, NC:NC + E3], RAC[:, bass.ds(b, 1), :].broadcast_to([P, 4, E3]), ALU.add).then_inc(e_rl, 1)
                    dve.tensor_reduce(NX1[:, i * 4:(i + 1) * 4], ps[:, :, 0:NC], AX.X, ALU.max, negate=True).then_inc(e_mx, 1)
                dve.wait_ge(e_mx, b * 2 + 2)
                dve.tensor_scalar(SR1, NX1, SCALE1, None, ALU.mult).then_inc(e_mxs, 1)
                dve.wait_ge(e_px, b * NT + NT)
                dve.reciprocal(NX1, SX1).then_inc(e_sr, 1)
                dve.wait_ge(e_sr, b + 1)
                dve.tensor_tensor(PX[:, :, 0:NC], PX[:, :, 0:NC], NX1.rearrange("p (t a) -> p t a", a=1).broadcast_to([P, NT, NC]), ALU.mult).then_inc(e_pxn, 1)
                dve.wait_ge(e_rt, b + 1)
                dve.wait_ge(e_rl, b * 2 + 2)
                dve.tensor_tensor(RL, PS[:, 0, 0:NT * 4].rearrange("p (t e) -> p t e", e=4)[:, :, 0:E3], RL, ALU.add).then_inc(e_r1, 1)
                dve.wait_ge(e_r1, b + 1)
                dve.tensor_reduce(RM, RL, AX.X, ALU.max, negate=True).then_inc(e_r2, 1)
                dve.wait_ge(e_r2, b + 1)
                bc = RM.rearrange("p (t a) -> p t a", a=1).broadcast_to([P, NT, E3])
                dve.tensor_tensor(RL, RL, bc, ALU.add).then_inc(e_r3, 1)
                dve.wait_ge(e_rex, b + 1)
                dve.tensor_reduce(RM, RP, AX.X, ALU.add).then_inc(e_r4, 1)
                dve.wait_ge(e_r4, b + 1)
                dve.reciprocal(SX1, RM).then_inc(e_r5, 1)
                dve.wait_ge(e_r5, b + 1)
                dve.tensor_tensor(RP, RP, SX1.rearrange("p (t a) -> p t a", a=1).broadcast_to([P, NT, E3]), ALU.mult).then_inc(e_rp, 1)
                dve.wait_ge(e_rpt, b + 1)
                dve.tensor_copy(PTR.rearrange("p (a n) -> p a n", a=2), PS[0:E3, 0:2, :]).then_inc(e_rptsb, 1)
                for e in range(E3):
                    for t in range(NT):
                        o = e * NT + t
                        dve.wait_ge(e_ops, b * 24 + o + 1)
                        if e == 0:
                            dve.tensor_scalar(ROU[:, t, :], PS[:, o % 4, 0:D], RP[:, t, 0:1], None, ALU.mult).then_inc(e_ho, 1)
                        else:
                            dve.wait_ge(e_ho, b * 24 + o - NT + 1)
                            dve.scalar_tensor_tensor(ROU[:, t, :], PS[:, o % 4, 0:D], RP[:, t, e:e + 1], ROU[:, t, :], ALU.mult, ALU.add).then_inc(e_ho, 1)
                for hf in range(NH):
                    dve.wait_ge(e_rot, b * 2 + hf + 1)
                    dve.tensor_copy(XT[:, 1, hf * HALF:(hf + 1) * HALF], PS[:, 2 + hf, :]).then_inc(e_rx_d, 1)
                for i in range(4):
                    dve.wait_ge(e_tg, b * 4 + i + 1)
                    if i >= 2:
                        dve.wait_ge(e_fd, b * 4 + i - 1)
                    dve.scalar_tensor_tensor(YG[:, i % 2, :], TG[:, i % 2, :], 1.0, PS[:, 4 + (i % 2) * 2, :], ALU.add, ALU.mult).then_inc(e_yg, 1)
                    dve.wait_ge(e_yg, b * 4 + i + 1)
                    x = X[:, bass.ds(b * NT + 2 * i, 2), :].rearrange("p a d -> p (a d)")
                    dve.scalar_tensor_tensor(x, YG[:, i % 2, :], 0.5, x, ALU.mult, ALU.add).then_inc(e_fd, 1)

            with dve.Fori(0, NB) as b:
                layer1_dve(b)

            dve.wait_ge(w_in[2], 5 * 16)
            dve.wait_ge(v_zero, 2)
            dve.memset(V[:, :, :, HD:HD + 1], 1.0).then_inc(v_one, 1)
            with dve.Fori(0, NB) as b:
                layer02_dve(2, b, e_fd, 4 * NB)

            with dve.Fori(0, NB) as b:
                norm_dve(norm(3, b, 0), b, 7, m_done, 8 * NB)
                cross_dve(3, b)
                out_dve(3, b, 0, biases(3, b, 0), stats=False)

        @block.scalar
        def _(act):
            def copy(out, in_):
                return act.activation(out, in_, ACT.Copy)

            act.wait_ge(dve_prep, at(DVE_PREP, "cond_T"))
            act.activation(csT[:, :, :], condT[:, :, :], ACT.Silu).then_inc(act_prep, 1)

            def norm_act(n, b, ln):
                for hf in range(NH):
                    act.wait_ge(ln_tp, n * 2 + hf + 1)
                    settle(act)
                    act.activation(XT[:, 0, hf * HALF:(hf + 1) * HALF], PS[:, hf, :], ACT.Identity, bias=AB[:, ln, 0, 1, bass.ds(b, 1)],
                                   scale=AB[:, ln, 0, 0, bass.ds(b, 1)]).then_inc(ln_xt_a, 1)

            def parts_act(q0, steps, bias):
                for st in range(steps + 1):
                    if st < steps:
                        k = st
                        if bias is None:
                            act.wait_ge(qk_f, q0 + k + 1)
                        else:
                            act.wait_ge(qk_ps, q0 + k + 1)
                            if k >= 2:
                                act.wait_ge(qk_r, q0 + k - 1)
                            act.activation(FR[:, k % 2, :], PS[:, 4 + 2 * (k % 2), :], ACT.Identity, bias=bias[k // 2]).then_inc(qk_f, 1)
                            act.wait_ge(qk_f, q0 + k + 1)
                        copy(QKP[:, 0, k // 2, (k % 2) * HALF:(k % 2 + 1) * HALF], FR[:, k % 2, :]).then_inc(qk_h, 1)
                    if st >= 1:
                        k = st - 1
                        act.wait_ge(qk_r, q0 + k + 1)
                        copy(QKP[:, 1, k // 2, (k % 2) * HALF:(k % 2 + 1) * HALF], RR[:, k % 2, :]).then_inc(qk_m, 1)

            def self_act(l, b):
                s = selfs(l, b)
                parts_act(qsteps(l, b, 0), 8, None if l == 0 else [QB[:, a, m:m + 1] for m in range(KT) for a in range(2)])
                act.preload_act_table(ACT.Exp)

                if l == 0:
                    with act.If(few_act == 1):
                        attend_act(s, True)
                    with act.Else():
                        attend_act(s, False)
                else:
                    attend_act(s, False)

            def attend_act(s, few):
                w = weight(few)

                def evacuate(g):
                    act.wait_ge(pv_done, (s * NG + g) * 8 + 8)
                    copy(OT[:, :].rearrange("p (a n) -> p a n", a=2), PS[:, 6:8, :]).then_inc(acc_out, 1)

                def body(g, peeled0=False):
                    for k in range(len(key_tiles(few)) * HG):
                        i, j = k // HG, k % HG
                        act.wait_ge(st_full, (s * NG + g) * 32 + (k + 1) * w)
                        if j == 0 and (i >= 2 or not peeled0):
                            act.wait_ge(pv_done, (s * NG + g) * 8 + (i - 1) * w)
                        act.activation(PR[:, i % 2, j, :].rearrange("p (a n) -> p a n", a=2), PS[:, 2 + 2 * (k % 2):4 + 2 * (k % 2), :], ACT.Exp, scale=SCALE).then_inc(ex_done, w)
                        if k == 1 and not peeled0:
                            evacuate(g - 1)

                body(0, True)
                with act.Fori(1, NG) as g:
                    body(g)
                evacuate(NG - 1)

            def out_act(l, b, i):
                o = outs(l, b, i)
                for hf in range(NH):
                    act.wait_ge(o_tp, o * 2 + hf + 1)
                    copy(XT[:, 0, hf * HALF:(hf + 1) * HALF], PS[:, hf, :]).then_inc(o_xt_a, 1)

            def cross_act(l, b):
                c = crosses(l, b)
                parts_act(qsteps(l, b, 0 if l == 3 else 1), 4, [0.0, 0.0] if l == 0 else [QB[:, 2 if l == 2 else 3, m:m + 1] for m in range(KT)])
                for h in range(H):
                    g = h // 4
                    act.wait_ge(c_st, c * H + h + 1)
                    if g >= 2 and h % 4 == 0:
                        act.wait_ge(c_pv, c * NG + g - 1)
                    act.activation(PR[:, g % 2, h % 4, :].rearrange("p (a n) -> p a n", a=2), PS[:, 2 + 2 * (h % 2):4 + 2 * (h % 2), :], ACT.Exp, scale=SCALE).then_inc(c_ex, 1)

            def mlp_act(l, b):
                m_ = mlps(l, b)
                for i in range(MT_ * NH):
                    m, hf = i // 2, i % 2
                    act.wait_ge(m_ps, m_ * 16 + i + 1)
                    act.activation(HT[:, m, hf * HALF:(hf + 1) * HALF], PS[:, 4 + i % 4, :], ACT.Gelu_apprx_tanh, bias=B1[:, 0 if l == 0 else 1, m:m + 1]).then_inc(m_h, 1)

            def layer02_act(l, b):
                norm_act(norm(l, b, 0), b, 0 if l == 0 else 4)
                self_act(l, b)
                out_act(l, b, 0)
                norm_act(norm(l, b, 1), b, 1 if l == 0 else 5)
                cross_act(l, b)
                out_act(l, b, 1)
                norm_act(norm(l, b, 2), b, 2 if l == 0 else 6)
                mlp_act(l, b)

            act.wait_ge(dve_prep, len(DVE_PREP))
            few_act = act.value_load(FEW)
            with act.Fori(0, NB) as b:
                layer02_act(0, b)

            act.wait_ge(e_prd, 4)

            def layer1_act(b):
                n = norm(1, b, 0)
                norm_act(n, b, 3)
                act.wait_ge(e_ve, b + 1)
                copy(VE[:, 0:1536].rearrange("p (a n) -> p a n", a=3), PS[0:NC, 4:7, :]).then_inc(e_vesb, 1)
                copy(VE[:, 1536:1536 + D + E3], PS[0:NC, 7, 0:D + E3]).then_inc(e_vesb, 1)
                act.wait_ge(e_mxs, b + 1)
                for t in range(NT):
                    act.activation(PX[:, t, 0:NC], PS[:, t // 4, (t % 4) * 80:(t % 4) * 80 + NC], ACT.Exp, bias=SR1[:, t:t + 1], scale=SCALE1,
                                   accum_out=SX1[:, t:t + 1]).then_inc(e_px, 1)
                act.wait_ge(e_pt, b + 1)
                copy(PT[0:NC, :].rearrange("p (a n) -> p a n", a=2), PS[0:NC, 2:4, :]).then_inc(e_ptsb, 1)
                act.wait_ge(e_r3, b + 1)
                act.activation(RP, RL, ACT.Exp).then_inc(e_rex, 1)
                for q in range(28):
                    r, hf = (q // 2, q % 2) if q < 4 else ((q - 4) % 8 // 2, q % 2)
                    e = (q - 4) // 8
                    dst = GT[:, r, hf * HALF:(hf + 1) * HALF] if q < 4 else HE[:, e % 2, r, hf * HALF:(hf + 1) * HALF]
                    m = 12 + r if q < 4 else e * RT + r
                    act.wait_ge(e_hps, b * 28 + q + 1)
                    if q == 4 + 16:
                        act.wait_ge(e_ops, b * 24 + NT)
                    settle(act)
                    act.activation(dst, PS[:, 4 + q % 4, :], ACT.Silu, bias=ANC[:, m, bass.ds(b, 1)]).then_inc(e_hsb, 1)
                for hf in range(NH):
                    act.wait_ge(e_rot, b * 2 + hf + 1)
                    copy(XT[:, 0, hf * HALF:(hf + 1) * HALF], PS[:, hf, :]).then_inc(e_rx_a, 1)
                for i in range(4):
                    act.wait_ge(e_fin, b * 4 + i + 1)
                    if i >= 2:
                        act.wait_ge(e_fd, b * 4 + i - 1)
                    act.activation(TG[:, i % 2, :], PS[:, 5 + (i % 2) * 2, :], ACT.Tanh, scale=0.5).then_inc(e_tg, 1)

            with act.Fori(0, NB) as b:
                layer1_act(b)
            act.wait_ge(v_one, 1)
            with act.Fori(0, NB) as b:
                layer02_act(2, b)
            with act.Fori(0, NB) as b:
                norm_act(norm(3, b, 0), b, 7)
                cross_act(3, b)
                out_act(3, b, 0)

        @block.gpsimd
        def _(pool):
            pool.wait_ge(const_in, 16)
            pool.tensor_copy(identb[:, :], ident[:, :])
            pool.tensor_scalar(bigI[:, :], ident[:, :], MASKED, 0.0, ALU.mult, ALU.add).then_inc(pool_prep, 1)
            pool.wait_ge(dve_prep, at(DVE_PREP, "mod_T"))
            pool.tensor_scalar(AKV[:, :, :], MODC[:, MODK // P:MODK // P + KT, :], 1.0, 0.0, ALU.add, ALU.add).then_inc(pool_prep, 1)
            pool.wait_ge(w_in[0], 4 * 16)
            for kt in range(KT):
                src = Wqkv[:, kt, 0:2 * D].rearrange("p (h a d) -> p h a d", a=2, d=HD // 2)
                dst = Wrot[:, kt, :].rearrange("p (h a d) -> p h a d", a=2, d=HD // 2)
                pool.tensor_scalar(dst[:, :, 0, :], src[:, :, 1, :], -1.0, 0.0, ALU.mult, ALU.add)
                last = pool.tensor_copy(dst[:, :, 1, :], src[:, :, 0, :])
            last.then_inc(pool_prep, 1)
            pool.wait_ge(pool_go, 1)
            for v, eps in enumerate((1e-6, 1e-5)):
                pool.tensor_scalar(CRS[:, v, :], CMV[:, :, 1], eps, 0.0, ALU.add, ALU.add).then_inc(pool_prep, 1)
            pool.wait_ge(pool_prep, 5)
            for v in range(2):
                pool.tensor_tensor(CRS[:, v, :], CRS[:, v, :], MHALF[0:NC, 0:NB], ALU.pow).then_inc(pool_prep, 1)
            pool.wait_ge(dve_prep, at(DVE_PREP, "mod_b"))
            pool.memset(BIG[:, 0:3072], 0.0)
            pool.memset(VCS, 0.0).then_inc(pool_prep, 1)
            pool.wait_ge(pool_prep, 8)
            pool.memset(VCS[0:NC, :, :, HD:HD + 1], 1.0).then_inc(pool_prep, 1)
            pool.wait_ge(pe_prep, at(PE_PREP, "ctx_T"))
            pool.memset(V[:, :, :, :], 0.0).then_inc(v_zero, 1)

            def norm_pool(n, ln):
                pool.wait_ge(ln_mv, n + 1)
                settle(pool)
                pool.tensor_scalar(NHLF[:, :], MV[:, :, 1], LN_EPS[ln], 0.0, ALU.add, ALU.add).then_inc(ln_ep, 1)
                pool.wait_ge(ln_ep, n + 1)
                settle(pool)
                pool.tensor_tensor(RS[:, :], NHLF[:, :], MHALF[:, :], ALU.pow).then_inc(ln_rs, 1)

            def add_bias(b, n, bias, done):
                pool.wait_ge(ln_norm, n * 8 + 8)
                settle(pool)
                x = X[:, bass.ts(b, NT), :]
                pool.tensor_tensor(x, x, bias[:, :].rearrange("p (a d) -> p a d", a=1).broadcast_to([P, NT, D]), ALU.add).then_inc(done, 1)

            def gate_weights(gi, w):
                pool.wait_ge(gate_in, (gi + 1) * 16)
                settle(pool)
                pool.tensor_tensor(WG[:, :, :], w, GATE[:, :].rearrange("p (a d) -> p a d", a=1).broadcast_to([P, KT, D]), ALU.mult).then_inc(wg_done, 1)

            def max_parts(src, rows, waits, base, first, p1, p2, p3, p4):
                pool.wait_ge(first, base + 1)
                settle(pool)
                pool.tensor_copy(NMB[0:rows, 0, :], src[0:rows, :]).then_inc(p1, 1)
                pool.wait_ge(p1, base + 1)
                settle(pool)
                pool.tensor_tensor(NMR[0:rows, :], src[0:rows, :], NMB[0:rows, 0, :], ALU.subtract).then_inc(p2, 1)
                pool.wait_ge(p2, base + 1)
                settle(pool)
                pool.tensor_copy(NMB[0:rows, 1, :], NMR[0:rows, :]).then_inc(p3, 1)
                pool.wait_ge(p3, base + 1)
                settle(pool)
                pool.tensor_tensor(NMB[0:rows, 2, :], NMR[0:rows, :], NMB[0:rows, 1, :], ALU.subtract).then_inc(p4, 1)

            def self_pool(l, b):
                s, n = selfs(l, b), norm(l, b, 0)
                gate_weights(gates(l, b, 0), Wo)
                if l == 2:
                    pool.wait_ge(bias_in, (biases(l, b, 0) + 1) * 16)
                    settle(pool)
                    pool.tensor_tensor(BIASB[:, :], BIASB[:, :], GATE[:, :], ALU.mult).then_inc(bg_done, 1)
                    pool.wait_ge(bg_done, b + 1)
                    add_bias(b, n, BIASB, biased)

                def group(g, peeled0=False):
                    if peeled0:
                        pool.wait_ge(v_sb, s * 4 + 4)
                    else:
                        pool.wait_ge(pv_done, (s * NG + g) * 8)
                    settle(pool)
                    pool.tensor_copy(VG[:, :, :, :].rearrange("p t j d -> p t (j d)"), V[:, :, bass.ds(g * HG, HG), :].rearrange("p t j d -> p t (j d)")).then_inc(vg_in, 1)

                max_parts(NMT, HG * NT, None, s * NG, nmt_sb, nm_p1, nm_p2, nm_p3, nm_p4)
                group(0, True)
                max_parts(NMT, HG * NT, None, s * NG + 1, nmt_sb, nm_p1, nm_p2, nm_p3, nm_p4)
                with pool.Fori(1, NG - 1) as g:
                    group(g)
                    max_parts(NMT, HG * NT, None, s * NG + g + 1, nmt_sb, nm_p1, nm_p2, nm_p3, nm_p4)
                group(NG - 1)

            def cross_pool(l, b):
                c, n = crosses(l, b), norm(l, b, 0 if l == 3 else 1)
                if l == 0:
                    gate_weights(gates(l, b, 1), Wco)
                else:
                    bi = biases(l, b, 0 if l == 3 else 1)
                    pool.wait_ge(bias_in, (bi + 1) * 16)
                    add_bias(b, n, BIASB, biased)
                max_parts(NMT, P, None, c, c_nmt, c_p1, c_p2, c_p3, c_p4)

            def mlp_pool(l, b):
                m_, n = mlps(l, b), norm(l, b, 2)
                pool.wait_ge(mg_in, (m_ + 1) * 32)
                settle(pool)
                pool.tensor_tensor(BIASM[:, :], BIASM[:, :], GATEM[:, :], ALU.mult).then_inc(m_bg, 1)
                pool.wait_ge(mw_in, (m_ + 1) * 32)
                settle(pool)
                pool.tensor_tensor(W2, W2, GATEM[:, :].rearrange("p (a d) -> p a d", a=1).broadcast_to([P, MT_, D]), ALU.mult).then_inc(m_w2g, 1)
                pool.wait_ge(m_bg, m_ + 1)
                add_bias(b, n, BIASM, m_biased)

            def layer02_pool(l, b):
                norm_pool(norm(l, b, 0), 0 if l == 0 else 4)
                self_pool(l, b)
                norm_pool(norm(l, b, 1), 1 if l == 0 else 5)
                cross_pool(l, b)
                norm_pool(norm(l, b, 2), 2 if l == 0 else 6)
                mlp_pool(l, b)

            pool.wait_ge(dve_prep, len(DVE_PREP))
            with pool.Fori(0, NB) as b:
                layer02_pool(0, b)
            with pool.Fori(0, NB) as b:
                norm_pool(norm(1, b, 0), 3)
            pool.wait_ge(e_fd, 4 * NB)
            pool.memset(V[:, :, :, :], 0.0).then_inc(v_zero, 1)
            pool.wait_ge(w_in[2], 5 * 16)
            with pool.Fori(0, NB) as b:
                layer02_pool(2, b)
            with pool.Fori(0, NB) as b:
                norm_pool(norm(3, b, 0), 7)
                cross_pool(3, b)




def kernel(**inputs):
    import ml_dtypes
    import concourse.bacc as _bacc
    from concourse.bass_utils import run_bass_kernel_spmd as _run

    nc = _bacc.Bacc("TRN2", target_bir_lowering=False, num_devices=1)
    arrays = {}
    for name, a in inputs.items():
        a = np.ascontiguousarray(a)
        if name == "mask_BxS2_bf1":
            name = "cross_mask"
        if name == "mask_SxS_bk0":
            name = "self_mask"
        arrays[name] = a
    arrays["ident"] = np.eye(P, dtype=np.float32)
    inv = 1.0 / 10000.0 ** (np.arange(0, HD, 2, dtype=np.float32) / HD)
    freqs = np.outer(np.arange(ROPE_N, dtype=np.float32), inv)
    emb = np.concatenate([freqs, freqs], axis=-1).T
    arrays["cos"] = np.ascontiguousarray(np.tile(np.cos(emb), (P // HD, 1)), np.float32)
    arrays["sin"] = np.ascontiguousarray(np.tile(np.sin(emb), (P // HD, 1)), np.float32)
    ones = np.ones((4, H * SEQ), ml_dtypes.bfloat16)
    arrays["q_rows"] = ones
    krows = ones.copy()
    krows[0] = 0
    arrays["k_rows"] = krows
    io = {n: nc.dram_tensor(f"in_{n}", a.shape, mybir.dt.from_np(a.dtype), kind="ExternalInput").ap() for n, a in arrays.items()}
    io["y"] = nc.dram_tensor("out_y", (NB, SEQ, D), F32, kind="ExternalOutput").ap()
    pixart_kernel(nc, io)
    r = _run(nc, [{f"in_{n}": a for n, a in arrays.items()}], core_ids=[0])
    return r.results[0]["out_y"]
```
